# Optimizing a Trainium2 kernel written in Bass

```python
import numpy as np
import jax
import jax.numpy as jnp

def _softmax(x, axis=-1):
    return jax.nn.softmax(x, axis=axis)
def _gelu(x):
    return jax.nn.gelu(x, approximate=True)
def _silu(x):
    return jax.nn.silu(x)
def _sigmoid(x):
    return jax.nn.sigmoid(x)
def _layernorm(x, axis=-1, eps=1e-5):
    m = jnp.mean(x, axis=axis, keepdims=True)
    v = jnp.var(x, axis=axis, keepdims=True)
    return (x - m) / jnp.sqrt(v + eps)
def _scatter_add(tgt, idx, src, axis=0):
    return tgt.at[idx].add(src)
def _segment_sum(src, seg, n):
    return jax.ops.segment_sum(src, seg, n)

kernel_name = 'mk_adj_preln_d4_adj_256_4e1d5b'

def setup_inputs(seed: int = 0):
    np.random.seed(seed)
    _w = jnp.asarray
    def _rec_inputs():
        import jax
        import jax.numpy as jnp
        _gk = jax.random.key(seed)
        x = -0.0002928 + 1 * jax.random.normal(jax.random.fold_in(_gk, 1), (128, 128, 256), jnp.float32)
        _w = (1.0 + jnp.arange(128, dtype=jnp.float32)) ** -0.5
        _w = _w / _w.mean()
        _pij = jnp.clip(0.125 * _w[:, None] * _w[None, :], 0.0, 1.0)
        _a = jax.random.uniform(jax.random.fold_in(_gk, 2), (128, 128)) < _pij
        adj = _a.astype(jnp.int32)
        return x, adj
    x, adj = _rec_inputs()
    def _L0_gnn_setup():
        import jax, jax.numpy as jnp
        import numpy as np
        ALPHA = 0.2
        NEG_INF = -9000000000000000.0

        def _gat(inp, adj_mask, W, a):
            h = jnp.matmul(inp, W)
            F_ = h.shape[-1]
            f1 = jnp.matmul(h, a[:F_, 0])
            f2 = jnp.matmul(h, a[F_:, 0])
            e = jax.nn.leaky_relu(f1[:, :, None] + f2[:, None, :], ALPHA)
            if adj_mask is not None:
                e = jnp.where(adj_mask[None, :, :] > 0, e, NEG_INF)
            att = jax.nn.softmax(e, axis=2)
            h_prime = jnp.einsum('bij,bjf->bif', att, h)
            return jax.nn.elu(h_prime)
        key = jax.random.key(seed)
        ks = jax.random.split(key, 10)
        B, N, Fin, H, O = (16, 1024, 256, 512, 256)

        def xavier(k, shape):
            fan_in, fan_out = (shape[0], shape[-1])
            bound = 1.414 * np.sqrt(6.0 / (fan_in + fan_out))
            return jax.random.uniform(k, shape, jnp.float32, -bound, bound)
        return {'x': jax.random.normal(ks[0], (B, N, Fin), jnp.float32), 'adj': jax.random.randint(ks[1], (N, N), 0, 2, jnp.int32), 'mlp1_w': xavier(ks[2], (Fin, H)), 'mlp1_b': jnp.zeros((H,), jnp.float32), 'mlp2_w': xavier(ks[3], (H, O)), 'mlp2_b': jnp.zeros((O,), jnp.float32), 'W_fc': xavier(ks[4], (H, H)), 'a_fc': xavier(ks[5], (2 * H, 1)), 'W_hand': xavier(ks[6], (O, O)), 'a_hand': xavier(ks[7], (2 * O, 1))}
    _L0_gnn_all = _L0_gnn_setup()
    _L0_gnn_in = {k: v for k, v in _L0_gnn_all.items() if k in ('mlp1_w', 'mlp1_b', 'mlp2_w', 'mlp2_b', 'W_fc', 'a_fc', 'W_hand', 'a_hand', )}
    del _L0_gnn_all

    def _L1_gnn_setup():
        import jax, jax.numpy as jnp
        import numpy as np
        ALPHA = 0.2
        MASK_VAL = -9000000000000000.0
        key = jax.random.key(seed)
        k1, k2, k3, k4 = jax.random.split(key, 4)
        B, N, F = (8, 1024, 256)
        H, OUT = (4, 256)
        hs = OUT // H
        x = jax.random.normal(k1, (B, N, F), dtype=jnp.float32)
        adj = jax.random.randint(k2, (N, N), 0, 2, dtype=jnp.int32)
        wb = float(np.sqrt(6.0 / (F + hs)))
        ab = float(np.sqrt(6.0 / (H + 2 * hs)))
        W = jax.random.uniform(k3, (H, F, hs), dtype=jnp.float32, minval=-wb, maxval=wb)
        a = jax.random.uniform(k4, (H, 2 * hs), dtype=jnp.float32, minval=-ab, maxval=ab)
        return {'x': x, 'adj': adj, 'W': W, 'a': a}
    _L1_gnn_all = _L1_gnn_setup()
    _L1_gnn_in = {k: v for k, v in _L1_gnn_all.items() if k in ('W', 'a', )}
    del _L1_gnn_all

    def _L2_gnn_setup():
        import jax, jax.numpy as jnp
        import numpy as np
        B, N, D_IN, D_OUT, H = (64, 512, 256, 256, 4)
        HD = D_OUT // H
        key = jax.random.key(seed)
        ks = jax.random.split(key, 10)
        x = jax.random.normal(ks[0], (B, N, D_IN), dtype=jnp.float32)
        adj = jax.random.randint(ks[1], (N, N), 0, 2, dtype=jnp.int32)
        adj = adj.at[jnp.arange(N), jnp.arange(N)].set(1)
        s_in = 1.0 / np.sqrt(D_IN)
        s_out = 1.0 / np.sqrt(D_OUT)
        wq = jax.random.uniform(ks[2], (D_OUT, D_IN), jnp.float32, -s_in, s_in)
        bq = jax.random.uniform(ks[3], (D_OUT,), jnp.float32, -s_in, s_in)
        wk = jax.random.uniform(ks[4], (D_OUT, D_IN), jnp.float32, -s_in, s_in)
        bk = jax.random.uniform(ks[5], (D_OUT,), jnp.float32, -s_in, s_in)
        wv = jax.random.uniform(ks[6], (D_OUT, D_IN), jnp.float32, -s_in, s_in)
        bv = jax.random.uniform(ks[7], (D_OUT,), jnp.float32, -s_in, s_in)
        wo = jax.random.uniform(ks[8], (D_OUT, D_OUT), jnp.float32, -s_out, s_out)
        bo = jax.random.uniform(ks[9], (D_OUT,), jnp.float32, -s_out, s_out)
        return {'x': x, 'adj': adj, 'wq': wq, 'bq': bq, 'wk': wk, 'bk': bk, 'wv': wv, 'bv': bv, 'wo': wo, 'bo': bo}
    _L2_gnn_all = _L2_gnn_setup()
    _L2_gnn_in = {k: v for k, v in _L2_gnn_all.items() if k in ('wq', 'bq', 'wk', 'bk', 'wv', 'bv', 'wo', 'bo', )}
    del _L2_gnn_all

    def _L3_gnn_setup():
        import jax, jax.numpy as jnp
        import numpy as np
        ALPHA = 0.2
        NEG_INF = -1000000000000.0
        key = jax.random.key(seed)
        k1, k2, k3, k4, k5 = jax.random.split(key, 5)
        B, N, C_in, C_out = (8, 2048, 256, 256)
        inp = jax.random.normal(k1, (B, N, C_in), dtype=jnp.float32)
        adj = jax.random.randint(k2, (N, N), 0, 2, dtype=jnp.int32)
        limit = 1.414 * np.sqrt(6.0 / (C_in + C_out))
        W1 = jax.random.uniform(k3, (C_in, C_out), jnp.float32, -limit, limit)
        W2 = jax.random.uniform(k4, (C_in, C_out), jnp.float32, -limit, limit)
        W3 = jax.random.uniform(k5, (C_in, C_out), jnp.float32, -limit, limit)
        return {'inp': inp, 'adj': adj, 'W1': W1, 'W2': W2, 'W3': W3}
    _L3_gnn_all = _L3_gnn_setup()
    _L3_gnn_in = {k: v for k, v in _L3_gnn_all.items() if k in ('W1', 'W2', 'W3', )}
    del _L3_gnn_all

    return {
        "x": x,
        "adj": adj,
        "L0_gnn_mlp1_w": _L0_gnn_in["mlp1_w"],
        "L0_gnn_mlp1_b": _L0_gnn_in["mlp1_b"],
        "L0_gnn_mlp2_w": _L0_gnn_in["mlp2_w"],
        "L0_gnn_mlp2_b": _L0_gnn_in["mlp2_b"],
        "L0_gnn_W_fc": _L0_gnn_in["W_fc"],
        "L0_gnn_a_fc": _L0_gnn_in["a_fc"],
        "L0_gnn_W_hand": _L0_gnn_in["W_hand"],
        "L0_gnn_a_hand": _L0_gnn_in["a_hand"],
        "L1_gnn_W": _L1_gnn_in["W"],
        "L1_gnn_a": _L1_gnn_in["a"],
        "L2_gnn_wq": _L2_gnn_in["wq"],
        "L2_gnn_bq": _L2_gnn_in["bq"],
        "L2_gnn_wk": _L2_gnn_in["wk"],
        "L2_gnn_bk": _L2_gnn_in["bk"],
        "L2_gnn_wv": _L2_gnn_in["wv"],
        "L2_gnn_bv": _L2_gnn_in["bv"],
        "L2_gnn_wo": _L2_gnn_in["wo"],
        "L2_gnn_bo": _L2_gnn_in["bo"],
        "L3_gnn_W1": _L3_gnn_in["W1"],
        "L3_gnn_W2": _L3_gnn_in["W2"],
        "L3_gnn_W3": _L3_gnn_in["W3"],
    }

def reference(x, adj, L0_gnn_mlp1_w, L0_gnn_mlp1_b, L0_gnn_mlp2_w, L0_gnn_mlp2_b, L0_gnn_W_fc, L0_gnn_a_fc, L0_gnn_W_hand, L0_gnn_a_hand, L1_gnn_W, L1_gnn_a, L2_gnn_wq, L2_gnn_bq, L2_gnn_wk, L2_gnn_bk, L2_gnn_wv, L2_gnn_bv, L2_gnn_wo, L2_gnn_bo, L3_gnn_W1, L3_gnn_W2, L3_gnn_W3):
    import jax
    import jax.numpy as jnp
    def _L0_gnn_ref(x, adj, mlp1_w, mlp1_b, mlp2_w, mlp2_b, W_fc, a_fc, W_hand, a_hand):
        import jax, jax.numpy as jnp
        import numpy as np
        ALPHA = 0.2
        NEG_INF = -9000000000000000.0

        def _gat(inp, adj_mask, W, a):
            h = jnp.matmul(inp, W)
            F_ = h.shape[-1]
            f1 = jnp.matmul(h, a[:F_, 0])
            f2 = jnp.matmul(h, a[F_:, 0])
            e = jax.nn.leaky_relu(f1[:, :, None] + f2[:, None, :], ALPHA)
            if adj_mask is not None:
                e = jnp.where(adj_mask[None, :, :] > 0, e, NEG_INF)
            att = jax.nn.softmax(e, axis=2)
            h_prime = jnp.einsum('bij,bjf->bif', att, h)
            return jax.nn.elu(h_prime)
        out = jax.nn.relu(jnp.matmul(x, mlp1_w) + mlp1_b)
        residual = out
        out = _gat(jax.nn.relu(out), None, W_fc, a_fc)
        out = jax.nn.elu(out) + residual
        out = jax.nn.relu(jnp.matmul(out, mlp2_w) + mlp2_b)
        residual = out
        out = _gat(jax.nn.relu(out), adj, W_hand, a_hand)
        out = jax.nn.elu(out) + residual
        return jax.nn.relu(out)

    def _L1_gnn_ref(x, adj, W, a):
        import jax, jax.numpy as jnp
        import numpy as np
        ALPHA = 0.2
        MASK_VAL = -9000000000000000.0
        B, N, _ = x.shape
        H, _, hs = W.shape
        Wh = jnp.einsum('bnf,hfd->bhnd', x, W)
        a1, a2 = (a[:, :hs], a[:, hs:])
        ei = jnp.einsum('bhnd,hd->bhn', Wh, a1)
        ej = jnp.einsum('bhnd,hd->bhn', Wh, a2)
        e = ei[:, :, :, None] + ej[:, :, None, :]
        e = jnp.where(e > 0, e, ALPHA * e)
        e = jnp.where(adj[None, None] > 0, e, MASK_VAL)
        att = jax.nn.softmax(e, axis=-1)
        h = jnp.einsum('bhij,bhjd->bhid', att, Wh)
        h = h.transpose(0, 2, 1, 3).reshape(B, N, H * hs)
        return jax.nn.elu(h)

    def _L2_gnn_ref(x, adj, wq, bq, wk, bk, wv, bv, wo, bo):
        import jax, jax.numpy as jnp
        import numpy as np
        B, N, D_IN, D_OUT, H = (64, 512, 256, 256, 4)
        HD = D_OUT // H
        b, n, _ = x.shape
        q = (x @ wq.T + bq).reshape(b, n, H, HD).transpose(0, 2, 1, 3)
        k = (x @ wk.T + bk).reshape(b, n, H, HD).transpose(0, 2, 1, 3)
        v = (x @ wv.T + bv).reshape(b, n, H, HD).transpose(0, 2, 1, 3)
        scores = jnp.einsum('bhnd,bhmd->bhnm', q, k) / jnp.sqrt(jnp.float32(HD))
        scores = jnp.where(adj[None, None] == 0, -jnp.inf, scores)
        attn = jnp.nan_to_num(jax.nn.softmax(scores, axis=-1), nan=0.0)
        out = jnp.einsum('bhnm,bhmd->bhnd', attn, v)
        out = out.transpose(0, 2, 1, 3).reshape(b, n, D_OUT)
        return out @ wo.T + bo

    def _L3_gnn_ref(inp, adj, W1, W2, W3):
        import jax, jax.numpy as jnp
        import numpy as np
        ALPHA = 0.2
        NEG_INF = -1000000000000.0
        h1 = jnp.einsum('bnc,cd->bnd', inp, W1)
        h2 = jnp.einsum('bnc,cd->bnd', inp, W2)
        h3 = jnp.einsum('bnc,cd->bnd', inp, W3)
        e = jnp.einsum('bnd,bmd->bnm', h1, h2)
        e = jax.nn.leaky_relu(e, ALPHA)
        e = jnp.where(adj[None, :, :] > 0, e, NEG_INF)
        attention = jax.nn.softmax(e, axis=-1)
        h_prime = jnp.einsum('bnm,bmd->bnd', attention, h3)
        return jax.nn.relu(h_prime)

    h = jnp.maximum(_layernorm(x, axis=-1), 0.0)
    x = x + _L0_gnn_ref(h, adj, L0_gnn_mlp1_w, L0_gnn_mlp1_b, L0_gnn_mlp2_w, L0_gnn_mlp2_b, L0_gnn_W_fc, L0_gnn_a_fc, L0_gnn_W_hand, L0_gnn_a_hand)
    h = jnp.maximum(_layernorm(x, axis=-1), 0.0)
    x = x + _L1_gnn_ref(h, adj, L1_gnn_W, L1_gnn_a)
    h = jnp.maximum(_layernorm(x, axis=-1), 0.0)
    x = x + _L2_gnn_ref(h, adj, L2_gnn_wq, L2_gnn_bq, L2_gnn_wk, L2_gnn_bk, L2_gnn_wv, L2_gnn_bv, L2_gnn_wo, L2_gnn_bo)
    h = jnp.maximum(_layernorm(x, axis=-1), 0.0)
    x = x + _L3_gnn_ref(h, adj, L3_gnn_W1, L3_gnn_W2, L3_gnn_W3)
    return x


_drawn_inputs = setup_inputs


def setup_inputs(seed=0):
    import zlib

    import numpy as np

    out = dict(_drawn_inputs(seed))
    spreads = {'L0_gnn_mlp1_b': (0.0, 0.1), 'L0_gnn_mlp2_b': (0.0, 0.1)}
    factors = {'L2_gnn_wq': 8.0,
     'L2_gnn_bq': 27.408,
     'L2_gnn_wk': 8.0,
     'L2_gnn_bk': 64.0,
     'L2_gnn_bv': 4.29}
    for name, (base, spread) in spreads.items():
        noise = np.random.default_rng([zlib.crc32(name.encode()), seed]).standard_normal(out[name].shape)
        drawn = base * np.exp(spread * noise) if base else spread * noise
        out[name] = jnp.asarray(drawn.astype(out[name].dtype))
    for name, factor in factors.items():
        out[name] = (out[name] * factor).astype(out[name].dtype)
    return out
```

```python
from contextlib import ExitStack

import concourse.bass as bass
from concourse import mybir


def gnn_stack_kernel(nc, ins, out):
    f32, f32r, bf16, i32 = mybir.dt.float32, mybir.dt.float32r, mybir.dt.bfloat16, mybir.dt.int32
    ALU, ACT, AX = mybir.AluOpType, mybir.ActivationFunctionType, mybir.AxisListType.X

    B, N, F = ins["x"].shape
    HID = ins["w_mlp1"].shape[1]
    HEADS = 4
    HD = F // HEADS
    G = 4
    T = G * N
    NT = B // G
    P = 128
    FC, HC = F // P, HID // P
    GP = G // 2
    EPS, SLOPE, MASKED = 1e-5, 0.2, -9.0e15
    QK_SCALE = float(HD) ** -0.5
    X_GROUPS = ins["x"].rearrange("(t g) n f -> t n g f", g=G)
    OUT_GROUPS = out.rearrange("(t g) n f -> t n g f", g=G)

    ctx = ExitStack()
    with ctx:
        def sb(name, shape, dt=f32):
            return ctx.enter_context(nc.sbuf_tensor(name, shape, dt))

        def sem(name):
            return ctx.enter_context(nc.semaphore(name))

        def split(name, chunks, cols):
            return sb(name + "_hi", [P, chunks, cols], f32r), sb(name + "_lo", [P, chunks, cols], f32r)

        mlp1_w, fc_w = split("mlp1_w", FC, HID), split("fc_w", HC, HID)
        mlp2_w, hand_w = split("mlp2_w", HC, F), split("hand_w", FC, F)
        l1_w, q_w, k_w, v_w, o_w = (split(n, FC, F) for n in ("l1_w", "q_w", "k_w", "v_w", "o_w"))
        bil_w, h3_w = split("bil_w", FC, F), split("h3_w", FC, F)
        fa1_w, fa2_w, fah_w = split("fa1_w", HC, P), split("fa2_w", FC, P), split("fah_w", FC, P)

        ident = sb("ident", [P, P])
        ident_bf = sb("ident_bf", [P, P], bf16)
        mask_gt = sb("mask_gt", [P, 4, N], bf16)
        mask_ne = sb("mask_ne", [P, 4, N], bf16)
        has_edge = sb("has_edge", [P, 1])
        row0, row1 = sb("row0", [P, 1]), sb("row1", [P, 1])
        mlp1_b, mlp2_b = sb("mlp1_b", [P, HC]), sb("mlp2_b", [P, FC])
        q_b, k_b = sb("q_b", [P, FC]), sb("k_b", [P, FC])
        half, k_bh = sb("half", [P, 2]), sb("k_bh", [P, FC, 2])
        v_b, o_b = sb("v_b", [P, F]), sb("o_b", [P, F])
        minus1, carrier = sb("minus1", [P, 1]), sb("carrier", [P, 1])
        eps_t, pow_t = sb("eps_t", [P, G]), sb("pow_t", [P, G])

        ax = sb("ax", [P, G, F])
        ax_res = sb("ax_res", [P, G, F])
        axn = sb("axn", [P, G, F])
        ah2 = axn
        a_in = sb("a_in_hi", [P, FC, T], f32r), sb("a_in_lo", [P, FC, T], f32r)
        a_mid = sb("a_mid_hi", [P, HC, T], f32r), sb("a_mid_lo", [P, HC, T], f32r)
        o1 = sb("o1", [P, HC, T])
        o2 = o1
        ah = sb("ah", [P, G, HID])
        ay = ah[:, 0:FC, :]
        ap, aq = sb("ap", [P, T]), sb("aq", [P, T])
        at_, az, apt = sb("at", [P, T]), sb("az", [P, T]), sb("apt", [P, T])
        aE, aR, aF = sb("aE", [P, 2, T]), sb("aR", [P, 2, T]), sb("aF", [P, 2, T])
        a_st, a_mv = sb("a_st", [P, G, 6]), sb("a_mv", [P, G, 2])
        a_ve, a_rs = sb("a_ve", [P, G]), sb("a_rs", [P, G])
        a_max, a_sum, a_inv = sb("a_max", [P, G]), sb("a_sum", [P, G]), sb("a_inv", [P, G])
        x1 = sb("x1", [P, G, F])
        bx = sb("bx", [P, G, F])
        bxn = sb("bxn", [P, G, F])
        b_in = sb("b_in_hi", [P, FC, T], f32r), sb("b_in_lo", [P, FC, T], f32r)
        b1, b2, b3 = sb("b1", [P, 2, T]), sb("b2", [P, 2, T]), sb("b3", [P, G, F])
        bt, bz, bpt = sb("bt", [P, 2, T]), sb("bz", [P, 2, T]), sb("bpt", [P, G, T])
        bE, bR = sb("bE", [P, T]), sb("bR", [P, T])
        b_st, b_mv = sb("b_st", [P, G, 6]), sb("b_mv", [P, G, 2])
        b_ve, b_rs = sb("b_ve", [P, G]), sb("b_rs", [P, G])
        b_max, b_sum, b_inv = sb("b_max", [P, 2, 4]), sb("b_sum", [P, 2, 4]), sb("b_inv", [P, 2, 4])

        banks = [ctx.enter_context(nc.psum_tensor(f"bank{i}", [P, T], f32)) for i in range(8)]

        s_const, s_used = sem("s_const"), sem("s_used")
        s_stage = [sem("s_stage0"), sem("s_stage1")]
        s_id, s_setup_pe, s_folded = sem("s_id"), sem("s_setup_pe"), sem("s_folded")
        stage = [o1[:, :, :].rearrange("p a b -> p (a b)"), ah[:, :, :].rearrange("p a b -> p (a b)")]
        adj_i = az[:, 0:N].bitcast(i32)
        w_plan = [("w_mlp1", mlp1_w), ("w_fc", fc_w), ("w_mlp2", mlp2_w), ("w_hand", hand_w), ("w_l1", l1_w),
                  ("w_q", q_w), ("w_k", k_w), ("w_v", v_w), ("w_o", o_w), ("w_h3", h3_w)]
        f_plan = [("w_fcT", "a_fc", fa1_w, HC, HC, 2), ("w_handT", "a_hand", fa2_w, FC, FC, 2),
                  ("w_l1T", "a_l1", fah_w, FC, FC, 2 * HEADS), ("w_1T", "w_2T", bil_w, FC, FC, F)]
        with nc.Block() as block:
            @block.sync
            def _(sp):
                consts = [(adj_i, ins["adj"]),
                          (mlp1_b[:, :], ins["b_mlp1"].rearrange("(c p) -> p c", p=P)),
                          (mlp2_b[:, :], ins["b_mlp2"].rearrange("(c p) -> p c", p=P)),
                          (q_b[:, :], ins["b_q"].rearrange("(c p) -> p c", p=P)),
                          (k_b[:, :], ins["b_k"].rearrange("(c p) -> p c", p=P)),
                          (v_b[:, :], ins["b_v"].rearrange("(a f) -> a f", a=1).to_broadcast([P, F])),
                          (o_b[:, :], ins["b_o"].rearrange("(a f) -> a f", a=1).to_broadcast([P, F]))]
                with nc.allow_non_contiguous_dma("small vectors, once"):
                    for dst, src in consts:
                        sp.dma_start(dst, src).then_inc(s_const, 16)
                    for i, (name, w) in enumerate(w_plan):
                        if i >= 2:
                            sp.wait_ge(s_used, i - 1)
                        c, n = w[0].shape[1], w[0].shape[2]
                        sp.dma_start(stage[i % 2][:, 0:c * n].rearrange("p (c n) -> p c n", c=c),
                                     ins[name].rearrange("(c p) n -> p c n", p=P)).then_inc(s_stage[i % 2], 16)
                    for j, (name, right, w, kc, dc, n) in enumerate(f_plan):
                        if j == 0:
                            sp.wait_ge(s_used, len(w_plan))
                        else:
                            sp.wait_ge(s_folded, j)
                        cols = ins[name].shape[1]
                        sp.dma_start(stage[0][:, 0:dc * cols].rearrange("p (c n) -> p c n", c=dc),
                                     ins[name].rearrange("(c p) n -> p c n", p=P)).then_inc(s_stage[0], 16)
                        sp.dma_start(stage[1][:, 0:dc * n].rearrange("p (c n) -> p c n", c=dc),
                                     ins[right].rearrange("(c p) n -> p c n", p=P)).then_inc(s_stage[1], 16)

            @block.gpsimd
            def _(pool):
                nc.gpsimd.memset(ident[:, :], 0.0).then_inc(s_id, 1)
                pool.wait_ge(s_id, 1)
                nc.gpsimd.affine_select(out=ident[:, :], in_=ident[:, :], compare_op=ALU.not_equal, fill=1.0,
                                        base=0, pattern=[[-1, P]], channel_multiplier=1).then_inc(s_id, 1)
                nc.gpsimd.memset(minus1[:, :], -1.0)
                nc.gpsimd.memset(eps_t[:, :], EPS)
                nc.gpsimd.memset(pow_t[:, :], -0.5)

            @block.tensor
            def _(pe):
                for j, (name, right, w, kc, dc, n) in enumerate(f_plan):
                    for part in s_stage:
                        pe.wait_ge(part, 16 * (len(w_plan) // 2 + j + 1))
                    if j:
                        pe.wait_ge(s_folded, j)
                    for k in range(kc):
                        for d in range(dc):
                            lhs = stage[0][:, 0:dc * kc * P].rearrange("p (c n) -> p c n", c=dc)[:, d, k * P:(k + 1) * P]
                            rhs = stage[1][:, 0:dc * n].rearrange("p (c n) -> p c n", c=dc)[:, d, :]
                            last = nc.tensor.matmul(banks[k][:, 0:n], lhs, rhs, start=d == 0, stop=d == dc - 1)
                    last.then_inc(s_setup_pe, 1)

            @block.vector
            def _(dve):
                links = sem("s_setup_links")
                done = [0]

                def link(i):
                    done[0] += 1
                    i.then_inc(links, 1)
                    dve.wait_ge(links, done[0])

                for w in (fa1_w, fa2_w, fah_w):
                    if w is fa1_w:
                        link(nc.vector.memset(at_[:, :], 0.0))
                    for part in w:
                        c = part.shape[1]
                        link(nc.vector.tensor_copy(part[:, :, :], at_[:, 0:c * P].rearrange("p (c n) -> p c n", c=c)))
                for i, (name, w) in enumerate(w_plan):
                    c, n = w[0].shape[1], w[0].shape[2]
                    src = stage[i % 2][:, 0:c * n].rearrange("p (c n) -> p c n", c=c)
                    dve.wait_ge(s_stage[i % 2], 16 * (i // 2 + 1))
                    link(nc.vector.tensor_copy(w[0][:, :, :], src))
                    nc.vector.tensor_tensor(w[1][:, :, :], src, w[0][:, :, :], ALU.subtract).then_inc(s_used, 1)
                for j, (name, right, w, kc, dc, n) in enumerate(f_plan):
                    dve.wait_ge(s_setup_pe, j + 1)
                    for k in range(kc):
                        if n == 2:
                            src = banks[k][:, 0:2]
                            hi, lo = (part[:, k, 0:2] for part in w)
                        elif n == F:
                            src = banks[k][:, 0:F]
                            hi, lo = (part[:, k, :] for part in w)
                        else:
                            src = banks[k][:, 0:n].rearrange("p (h x) -> p h x", x=2)
                            hi, lo = (part[:, k, :].rearrange("p (h x) -> p h x", x=P // HEADS)[:, :, 0:2] for part in w)
                        link(nc.vector.tensor_copy(hi, src))
                        last = nc.vector.tensor_tensor(lo, src, hi, ALU.subtract)
                    last.then_inc(s_folded, 1)
                dve.wait_ge(s_id, 2)
                nc.vector.tensor_copy(ident_bf[:, :], ident[:, :])
                nc.vector.tensor_reduce(row0[:, :], ident[:, 0:P:32], AX, ALU.add)
                nc.vector.tensor_reduce(row1[:, :], ident[:, 1:P:32], AX, ALU.add)
                link(nc.vector.tensor_reduce(half[:, :], ident[:, :].rearrange("p (i d) -> p i d", i=2), AX, ALU.add))
                dve.wait_ge(s_const, 16 * 7)
                link(nc.vector.tensor_scalar(q_b[:, :], q_b[:, :], QK_SCALE, None, ALU.mult))
                for m in range(FC):
                    nc.vector.tensor_scalar(k_bh[:, m, :], half[:, :], k_b[:, m:m + 1], None, ALU.mult)
                for mask, op in ((mask_gt, ALU.is_gt), (mask_ne, ALU.not_equal)):
                    link(nc.vector.tensor_scalar(at_[:, 0:N], adj_i, 0.0, None, op))
                    for r in range(4):
                        link(nc.vector.tensor_scalar(mask[:, r, :], at_[:, 0:N], 1.0, -MASKED, ALU.subtract, ALU.mult))
                link(nc.vector.tensor_reduce(has_edge[:, :], at_[:, 0:N], AX, ALU.max))

        class Job:
            def __init__(self, name, n):
                self.n, self.full, self.taken = n, sem(name + "_full"), sem(name + "_taken")

        def at(g, n, k):
            return g * n + (k + 1)

        A_ORDER = ["xt"] * 2 + ["m1"] * 4 + ["f1"] + ["h1"] * 4 + ["s1"] + ["p1"] + ["v1"] * 4 + ["m2"] * 2 + \
                  ["f2"] + ["h2"] * 2 + ["s2"] + ["p2"] + ["v2"] * 2 + ["y0"] * 2
        L1S = ["s", "s", "p", "s", "p", "s", "p", "p"]
        B_ORDER = ["1x"] * 2 + ["1f"] + ["1h"] * 2 + ["1" + c for c in L1S] + ["1v"] * 2 + ["1y"] * 2 + \
                  ["2x"] * 2 + ["2q"] * 2 + ["2k"] * 2 + ["2h"] * 2 + ["2" + c for c in L1S] + ["2v"] * 2 + ["2y"] * 2 + \
                  ["3x"] * 2 + ["3g"] * 2 + ["3h"] * 2 + ["3s"] + ["3p"] + ["3y"] * 2

        def numbered(order, prefix):
            jobs, seen, where, at = {}, {}, {}, []
            for i, name in enumerate(order):
                k = seen.get(name, 0)
                seen[name] = k + 1
                where[name, k] = i
                at.append((name, k))
            for name in seen:
                jobs[name] = Job(prefix + name, seen[name])
            return jobs, where, at

        JA, WA, SA = numbered(A_ORDER, "a_")
        JB, WB, SB_ = numbered(B_ORDER, "b_")

        def bank_a(name, k):
            return banks[WA[name, k] % 4]

        def bank_b(name, k):
            return banks[4 + WB[name, k] % 4]

        def bank_free(jobs, where, order, name, k, g):
            i = where[name, k]
            if i >= 4:
                before, j = order[i - 4]
                return jobs[before].taken, at(g, jobs[before].n, j)
            before, _ = order[max(j for j in range(len(order)) if j % 4 == i)]
            return jobs[before].taken, g * jobs[before].n

        def a_bank_free(name, k, g):
            return bank_free(JA, WA, SA, name, k, g)

        def b_bank_free(name, k, g):
            return bank_free(JB, WB, SB_, name, k, g)

        names = ("ax_loaded ax_res_loaded a_var a_rstd axn_ready a_hi_ready m1_ready m1_hi m1_hi_d m2_ready "
                 "a_p_ready a_t_ready a_z_max a_shifted a_exp a_inv_ready a_norm a_e1 a_e2 a_u a_f v1_hi "
                 "b_var b_rstd bxn_ready b_hi_ready b1_p b_t_ready b_z_max b_shifted b_exp b_inv_ready b_norm "
                 "b_e b_full bx_bias 2v_hi 3x_full out_stored").split()
        S = {n: sem("s_" + n) for n in names}

        def three(pe, psum, lhs, rhs, start, stop):
            nc.tensor.matmul(psum, lhs[0], rhs[0], start=start, stop=False)
            nc.tensor.matmul(psum, lhs[0], rhs[1], start=False, stop=False)
            return nc.tensor.matmul(psum, lhs[1], rhs[0], start=False, stop=stop)

        def parts(pair, *index):
            return pair[0][index], pair[1][index]

        def four(ap):
            return ap.rearrange("p (g j) -> p g j", g=4)

        ALL = slice(None)
        a_link, b_link, a_ve_link, b_ve_link = sem("a_stats_done"), sem("b_stats_done"), sem("a_var_eps"), sem("b_var_eps")
        a_sum_link, b_sum_link, max_link, b_edge_link = sem("a_sum_done"), sem("b_sum_done"), sem("b_max_done"), sem("b_inv_done")

        def steps(eng, body):
            body(0, None, True, False)
            body(1, 0, True, True)
            with eng.Fori(2, NT) as t:
                body(t, t - 1, True, True)
            body(None, NT - 1, False, True)

        with nc.Block() as block:
            @block.sync
            def _(sp):
                sp.dma_start(ax[:, :, :], X_GROUPS[0]).then_inc(S["ax_loaded"], 16)

                def body(ga, gb, with_a, with_b, another=True):
                    if with_a:
                        if with_b:
                            sp.wait_ge(JA["y0"].taken, at(ga - 1, 2, 1))
                        sp.dma_start(ax_res[:, :, :], X_GROUPS[ga]).then_inc(S["ax_res_loaded"], 16)
                        if another:
                            sp.wait_ge(S["axn_ready"], at(ga, 1, 0))
                            sp.dma_start(ax[:, :, :], X_GROUPS[ga + 1]).then_inc(S["ax_loaded"], 16)
                    if with_b:
                        sp.wait_ge(JB["3y"].taken, at(gb, 2, 1))
                        sp.dma_start(OUT_GROUPS[gb], bxn[:, :, :]).then_inc(S["out_stored"], 16)
                body(0, None, True, False)
                body(1, 0, True, True)
                with sp.Fori(2, NT - 1) as t:
                    body(t, t - 1, True, True)
                body(NT - 1, NT - 2, True, True, another=False)
                body(None, NT - 1, False, True)
                sp.wait_ge(S["out_stored"], 16 * NT)

            @block.tensor
            def _(pe):
                def body(ga, gb, with_a, with_b):
                    def transposes(bank, srcs):
                        for i, s in enumerate(srcs):
                            last = nc.tensor.transpose(bank[:, i * P:(i + 1) * P], s, ident[:, :])
                        return last

                    def project(bank, w, x, chunks, m):
                        for c in range(chunks):
                            last = three(pe, bank[:, :], parts(w, ALL, c, slice(m * P, (m + 1) * P)), parts(x, ALL, c, ALL),
                                         c == 0, c == chunks - 1)
                        return last

                    def project_nodes(bank, off, n, w, x, chunks, g):
                        for c in range(chunks):
                            last = three(pe, bank[:, off:off + n], parts(x, ALL, c, slice(g * N, (g + 1) * N)),
                                         parts(w, ALL, c, ALL), c == 0, c == chunks - 1)
                        return last

                    def xt(c):
                        bank = bank_a("xt", c)
                        pe.wait_ge(*a_bank_free("xt", c, ga))
                        if c == 0:
                            pe.wait_ge(S["axn_ready"], at(ga, 1, 0))
                        transposes(bank, [axn[:, g, c * P:(c + 1) * P] for g in range(G)]).then_inc(JA["xt"].full, 1)

                    def m1(m):
                        bank = bank_a("m1", m)
                        pe.wait_ge(*a_bank_free("m1", m, ga))
                        pe.wait_ge(JA["xt"].taken, at(ga, 2, 1))
                        project(bank, mlp1_w, a_in, FC, m).then_inc(JA["m1"].full, 1)

                    def f1():
                        bank = bank_a("f1", 0)
                        pe.wait_ge(*a_bank_free("f1", 0, ga))
                        pe.wait_ge(S["m1_ready"], at(ga, HC, HC - 1))
                        project(bank, fa1_w, a_mid, HC, 0).then_inc(JA["f1"].full, 1)

                    def h1(g):
                        bank = bank_a("h1", g)
                        pe.wait_ge(*a_bank_free("h1", g, ga))
                        project_nodes(bank, 0, HID, fc_w, a_mid, HC, g).then_inc(JA["h1"].full, 1)

                    def s1():
                        bank = bank_a("s1", 0)
                        pe.wait_ge(*a_bank_free("s1", 0, ga))
                        pe.wait_ge(S["a_p_ready"], at(ga, 2, 0))
                        pe.wait_ge(JA["f1"].taken, at(ga, 1, 0))
                        for g in range(G):
                            r = slice(g * N, (g + 1) * N)
                            last = nc.tensor.matmul(bank[:, r], ap[0:2, r], aq[0:2, r], start=True, stop=True)
                        last.then_inc(JA["s1"].full, 1)

                    def p1(which=0):
                        name = ("p1", "p2")[which]
                        bank = bank_a(name, 0)
                        pe.wait_ge(*a_bank_free(name, 0, ga))
                        pe.wait_ge(S["a_norm"], at(ga, 2, which))
                        transposes(bank, [az[:, g * N:(g + 1) * N] for g in range(G)]).then_inc(JA[name].full, 1)

                    def v1(c):
                        bank = bank_a("v1", c)
                        pe.wait_ge(*a_bank_free("v1", c, ga))
                        pe.wait_ge(JA["p1"].taken, at(ga, 1, 0))
                        pe.wait_ge(JA["h1"].taken, at(ga, G, G - 1))
                        for g in range(G):
                            r = slice(g * N, (g + 1) * N)
                            last = nc.tensor.matmul(bank[:, r], ah[:, g, c * P:(c + 1) * P], apt[:, r], start=True, stop=True)
                        last.then_inc(JA["v1"].full, 1)

                    def m2(m):
                        bank = bank_a("m2", m)
                        pe.wait_ge(*a_bank_free("m2", m, ga))
                        pe.wait_ge(S["v1_hi"], at(ga, HC, HC - 1))
                        project(bank, mlp2_w, a_mid, HC, m).then_inc(JA["m2"].full, 1)

                    def f2():
                        bank = bank_a("f2", 0)
                        pe.wait_ge(*a_bank_free("f2", 0, ga))
                        pe.wait_ge(S["m2_ready"], at(ga, FC, FC - 1))
                        project(bank, fa2_w, a_in, FC, 0).then_inc(JA["f2"].full, 1)

                    def h2(b):
                        bank = bank_a("h2", b)
                        pe.wait_ge(*a_bank_free("h2", b, ga))
                        for i in range(2):
                            last = project_nodes(bank, i * F, F, hand_w, a_in, FC, 2 * b + i)
                        last.then_inc(JA["h2"].full, 1)

                    def s2():
                        bank = bank_a("s2", 0)
                        pe.wait_ge(*a_bank_free("s2", 0, ga))
                        pe.wait_ge(S["a_p_ready"], at(ga, 2, 1))
                        pe.wait_ge(JA["f2"].taken, at(ga, 1, 0))
                        nc.tensor.matmul(bank[:, :], ident_bf[:, :], mask_gt[:, :, :].rearrange("p a b -> p (a b)"), start=True, stop=False)
                        for g in range(G):
                            r = slice(g * N, (g + 1) * N)
                            last = nc.tensor.matmul(bank[:, r], ap[0:2, r], aq[0:2, r], start=False, stop=g == G - 1)
                        last.then_inc(JA["s2"].full, 1)

                    def v2(c):
                        bank = bank_a("v2", c)
                        pe.wait_ge(*a_bank_free("v2", c, ga))
                        pe.wait_ge(JA["p2"].taken, at(ga, 1, 0))
                        pe.wait_ge(JA["h2"].taken, at(ga, 2, 1))
                        for g in range(G):
                            r = slice(g * N, (g + 1) * N)
                            last = nc.tensor.matmul(bank[:, r], ah2[:, g, c * P:(c + 1) * P], apt[:, r], start=True, stop=True)
                        last.then_inc(JA["v2"].full, 1)

                    def y0(b):
                        bank = bank_a("y0", b)
                        pe.wait_ge(*a_bank_free("y0", b, ga))
                        pe.wait_ge(S["a_f"], at(ga, HC + FC, HC + FC - 1))
                        transposes(bank, [ay[:, c, (2 * b + i) * N:(2 * b + i + 1) * N] for i in range(2) for c in range(FC)]) \
                            .then_inc(JA["y0"].full, 1)

                    def x(l, c):
                        bank = bank_b(f"{l}x", c)
                        pe.wait_ge(*b_bank_free(f"{l}x", c, gb))
                        if c == 0:
                            pe.wait_ge(S["bxn_ready"], at(gb, 3, l - 1))
                        transposes(bank, [bxn[:, g, c * P:(c + 1) * P] for g in range(G)]).then_inc(JB[f"{l}x"].full, 1)

                    def proj(l, name, w, m):
                        bank = bank_b(f"{l}{name}", m)
                        pe.wait_ge(*b_bank_free(f"{l}{name}", m, gb))
                        pe.wait_ge(JB[f"{l}x"].taken, at(gb, 2, 1))
                        project(bank, w, b_in, FC, m).then_inc(JB[f"{l}{name}"].full, 1)

                    def nodes(l, w, b):
                        bank = bank_b(f"{l}h", b)
                        pe.wait_ge(*b_bank_free(f"{l}h", b, gb))
                        pe.wait_ge(JB[f"{l}x"].taken, at(gb, 2, 1))
                        for i in range(2):
                            last = project_nodes(bank, i * F, F, w, b_in, FC, 2 * b + i)
                        last.then_inc(JB[f"{l}h"].full, 1)

                    def s_l1(g):
                        bank = bank_b("1s", g)
                        pe.wait_ge(*b_bank_free("1s", g, gb))
                        if g == 0:
                            pe.wait_ge(S["b1_p"], at(gb, 1, 0))
                            pe.wait_ge(JB["1f"].taken, at(gb, 1, 0))
                        nc.tensor.matmul(bank[:, :], ident_bf[:, :], mask_gt[:, :, :].rearrange("p a b -> p (a b)"), start=True, stop=False)
                        r = slice(g * N, (g + 1) * N)
                        nc.tensor.matmul(bank[:, :], b1[:, 0, r], bpt[:, g, :], start=False, stop=True).then_inc(JB["1s"].full, 1)

                    def s_l2(g):
                        bank = bank_b("2s", g)
                        pe.wait_ge(*b_bank_free("2s", g, gb))
                        if g == 0:
                            pe.wait_ge(JB["2q"].taken, at(gb, 2, 1))
                            pe.wait_ge(JB["2k"].taken, at(gb, 2, 1))
                        nc.tensor.matmul(bank[:, :], ident_bf[:, :], mask_ne[:, :, :].rearrange("p a b -> p (a b)"), start=True, stop=False)
                        r = slice(g * N, (g + 1) * N)
                        for c in range(FC):
                            last = nc.tensor.matmul(bank[:, 2 * c * N:2 * (c + 1) * N], b1[:, c, r], bpt[:, g, 2 * c * N:2 * (c + 1) * N],
                                                    start=False, stop=c == FC - 1)
                        last.then_inc(JB["2s"].full, 1)

                    def p(l, g):
                        bank = bank_b(f"{l}p", g)
                        pe.wait_ge(*b_bank_free(f"{l}p", g, gb))
                        base = {1: 0, 2: G, 3: 2 * G}[l]
                        pe.wait_ge(S["b_norm"], at(gb, 2 * G + 1, base + g))
                        slot = (base + g) % 2
                        transposes(bank, [bz[:, slot, h * N:(h + 1) * N] for h in range(4)]).then_inc(JB[f"{l}p"].full, 1)

                    def v(l, c):
                        bank = bank_b(f"{l}v", c)
                        pe.wait_ge(*b_bank_free(f"{l}v", c, gb))
                        pe.wait_ge(JB[f"{l}h"].taken, at(gb, 2, 1))
                        pe.wait_ge(JB[f"{l}p"].taken, at(gb, G, G - 1))
                        for g in range(G):
                            for i in range(2):
                                h = 2 * c + i
                                last = nc.tensor.matmul(bank[i * HD:(i + 1) * HD, g * N:(g + 1) * N], b3[:, g, h * HD:(h + 1) * HD],
                                                        bpt[:, g, h * N:(h + 1) * N], start=True, stop=True)
                        last.then_inc(JB[f"{l}v"].full, 1)

                    def y_l1(b):
                        bank = bank_b("1y", b)
                        pe.wait_ge(*b_bank_free("1y", b, gb))
                        pe.wait_ge(S["b_full"], at(gb, FC, FC - 1))
                        transposes(bank, [b2[:, c, (2 * b + i) * N:(2 * b + i + 1) * N] for i in range(2) for c in range(FC)]) \
                            .then_inc(JB["1y"].full, 1)

                    def y_l2(b):
                        bank = bank_b("2y", b)
                        pe.wait_ge(*b_bank_free("2y", b, gb))
                        pe.wait_ge(JB["2v"].taken, at(gb, 2, 1))
                        for i in range(2):
                            last = project_nodes(bank, i * F, F, o_w, b_in, FC, 2 * b + i)
                        last.then_inc(JB["2y"].full, 1)

                    def s_l3():
                        bank = bank_b("3s", 0)
                        pe.wait_ge(*b_bank_free("3s", 0, gb))
                        pe.wait_ge(JB["3g"].taken, at(gb, 2, 1))
                        pe.wait_ge(S["3x_full"], at(gb, 2, 1))
                        nc.tensor.matmul(bank[:, :], ident_bf[:, :], mask_gt[:, :, :].rearrange("p a b -> p (a b)"), start=True, stop=False)
                        for g in range(G):
                            r = slice(g * N, (g + 1) * N)
                            for c in range(FC):
                                last = nc.tensor.matmul(bank[:, r], b1[:, c, r], b2[:, c, r], start=False, stop=(g, c) == (G - 1, FC - 1))
                        last.then_inc(JB["3s"].full, 1)

                    def y_l3(b):
                        bank = bank_b("3y", b)
                        pe.wait_ge(*b_bank_free("3y", b, gb))
                        pe.wait_ge(JB["3h"].taken, at(gb, 2, 1))
                        pe.wait_ge(JB["3p"].taken, at(gb, 1, 0))
                        for i in range(2):
                            g = 2 * b + i
                            last = nc.tensor.matmul(bank[:, i * F:(i + 1) * F], bpt[:, 0, g * N:(g + 1) * N], b3[:, g, :], start=True, stop=True)
                        last.then_inc(JB["3y"].full, 1)

                    if with_b:
                        x(1, 0); x(1, 1)
                    if with_a:
                        xt(0); xt(1)
                    if with_b:
                        proj(1, 'f', fah_w, 0); nodes(1, l1_w, 0); nodes(1, l1_w, 1)
                    if with_a:
                        m1(0)
                    if with_b:
                        s_l1(0); s_l1(1)
                    if with_a:
                        m1(1); m1(2); m1(3)
                    if with_b:
                        p(1, 0); s_l1(2); p(1, 1); s_l1(3)
                    if with_a:
                        f1(); h1(0)
                    if with_b:
                        p(1, 2)
                    if with_a:
                        h1(1)
                    if with_b:
                        p(1, 3)
                    if with_a:
                        h1(2)
                    if with_b:
                        v(1, 0); v(1, 1)
                    if with_a:
                        h1(3)
                    if with_b:
                        y_l1(0); y_l1(1)
                    if with_a:
                        s1()
                    if with_b:
                        x(2, 0); x(2, 1); proj(2, 'q', q_w, 0); proj(2, 'q', q_w, 1); proj(2, 'k', k_w, 0)
                        proj(2, 'k', k_w, 1); nodes(2, v_w, 0); nodes(2, v_w, 1); s_l2(0); s_l2(1)
                    if with_a:
                        p1(0); v1(0); v1(1); v1(2)
                    if with_b:
                        p(2, 0); s_l2(2); p(2, 1); s_l2(3)
                    if with_a:
                        v1(3)
                    if with_b:
                        p(2, 2); p(2, 3); v(2, 0); v(2, 1); y_l2(0); y_l2(1)
                    if with_a:
                        m2(0); m2(1)
                    if with_b:
                        x(3, 0); x(3, 1)
                    if with_a:
                        f2(); h2(0)
                    if with_b:
                        proj(3, 'g', bil_w, 0)
                    if with_a:
                        h2(1)
                    if with_b:
                        proj(3, 'g', bil_w, 1)
                    if with_a:
                        s2()
                    if with_b:
                        nodes(3, h3_w, 0); nodes(3, h3_w, 1); s_l3()
                    if with_a:
                        p1(1); v2(0); v2(1)
                    if with_b:
                        p(3, 0); y_l3(0); y_l3(1)
                    if with_a:
                        y0(0); y0(1)
                steps(pe, body)

            @block.scalar
            def _(act):
                def body(ga, gb, with_a, with_b):
                    def xt(c):
                        bank = bank_a("xt", c)
                        act.wait_ge(JA["xt"].full, at(ga, JA["xt"].n, c))
                        nc.scalar.activation(a_in[0][:, c, :], bank[:, :], ACT.Relu).then_inc(S["a_hi_ready"], 1)

                    def m1(m):
                        bank = bank_a("m1", m)
                        act.wait_ge(JA["m1"].full, at(ga, JA["m1"].n, m))
                        nc.scalar.activation(o1[:, m, :], bank[:, :], ACT.Relu, bias=mlp1_b[:, m:m + 1]).then_inc(JA["m1"].taken, 1)

                    def rows_p(which):
                        bank = bank_a(("f1", "f2")[which], 0)
                        act.wait_ge(JA[("f1", "f2")[which]].full, at(ga, JA[("f1", "f2")[which]].n, 0))
                        nc.scalar.activation(ap[0:2, :], bank[0:2, :], ACT.Identity, bias=row1[0:2, :], scale=row0[0:2, :]) \
                            .then_inc(S["a_p_ready"], 1)

                    def h1(g):
                        bank = bank_a("h1", g)
                        act.wait_ge(JA["h1"].full, at(ga, JA["h1"].n, g))
                        nc.scalar.activation(ah[:, g, :], bank[:, :], ACT.Copy).then_inc(JA["h1"].taken, 1)

                    def scaled(which):
                        bank = bank_a(("s1", "s2")[which], 0)
                        act.wait_ge(JA[("s1", "s2")[which]].full, at(ga, JA[("s1", "s2")[which]].n, 0))
                        nc.scalar.activation(at_[:, :], bank[:, :], ACT.Copy, scale=SLOPE).then_inc(S["a_t_ready"], 1)

                    def exp(which):
                        act.wait_ge(S["a_shifted"], at(ga, 2, which))
                        nc.scalar.activation(az[:, :], az[:, :], ACT.Exp).then_inc(S["a_exp"], 1)

                    def pt(which):
                        name = ("p1", "p2")[which]
                        bank = bank_a(name, 0)
                        act.wait_ge(JA[name].full, at(ga, JA[name].n, 0))
                        nc.scalar.activation(apt[:, :], bank[:, :], ACT.Copy).then_inc(JA[name].taken, 1)

                    def e1(which, c):
                        bank = bank_a(("v1", "v2")[which], c)
                        act.wait_ge(JA[("v1", "v2")[which]].full, at(ga, JA[("v1", "v2")[which]].n, c))
                        k = which * HC + c
                        if k >= 2:
                            act.wait_ge(S["a_f"], at(ga, HC + FC, k - 2))
                        nc.scalar.activation(aE[:, k % 2, :], bank[:, :], ACT.Exp).then_inc(S["a_e1"], 1)

                    def e2(which, c):
                        k = which * HC + c
                        act.wait_ge(S["a_u"], at(ga, HC + FC, k))
                        nc.scalar.activation(aE[:, k % 2, :], aE[:, k % 2, :], ACT.Exp, bias=minus1[:, :]).then_inc(S["a_e2"], 1)

                    def v1_hi(c):
                        act.wait_ge(S["a_f"], at(ga, HC + FC, c))
                        nc.scalar.activation(a_mid[0][:, c, :], aF[:, c % 2, :], ACT.Copy).then_inc(S["m1_hi"], 1)

                    def m2(m):
                        bank = bank_a("m2", m)
                        act.wait_ge(JA["m2"].full, at(ga, JA["m2"].n, m))
                        nc.scalar.activation(o2[:, m, :], bank[:, :], ACT.Relu, bias=mlp2_b[:, m:m + 1]).then_inc(JA["m2"].taken, 1)

                    def h2(b):
                        bank = bank_a("h2", b)
                        act.wait_ge(JA["h2"].full, at(ga, JA["h2"].n, b))
                        nc.scalar.activation(ah2[:, 2 * b:2 * b + 2, :].rearrange("p a b -> p (a b)"), bank[:, :], ACT.Copy) \
                            .then_inc(JA["h2"].taken, 1)

                    def x(l, c):
                        bank = bank_b(f"{l}x", c)
                        act.wait_ge(JB[f"{l}x"].full, at(gb, JB[f"{l}x"].n, c))
                        nc.scalar.activation(b_in[0][:, c, :], bank[:, :], ACT.Relu).then_inc(S["b_hi_ready"], 1)

                    def x_full(c):
                        bank = bank_b("3x", c)
                        act.wait_ge(JB["3x"].full, at(gb, JB["3x"].n, c))
                        nc.scalar.activation(b2[:, c, :], bank[:, :], ACT.Relu).then_inc(S["3x_full"], 1)

                    def rows_l1():
                        bank = bank_b("1f", 0)
                        act.wait_ge(JB["1f"].full, at(gb, JB["1f"].n, 0))
                        nc.scalar.activation(b1[:, 0, :], bank[:, :], ACT.Identity, bias=row1[:, :], scale=row0[:, :]).then_inc(S["b1_p"], 1)

                    def copy_nodes(l, b):
                        bank = bank_b(f"{l}h", b)
                        act.wait_ge(JB[f"{l}h"].full, at(gb, JB[f"{l}h"].n, b))
                        nc.scalar.activation(b3[:, 2 * b:2 * b + 2, :].rearrange("p a b -> p (a b)"), bank[:, :], ACT.Copy) \
                            .then_inc(JB[f"{l}h"].taken, 1)

                    def b_scaled(l, g):
                        k = g if l == 1 else G
                        bank = bank_b(f"{l}s", g)
                        act.wait_ge(JB[f"{l}s"].full, at(gb, JB[f"{l}s"].n, g))
                        if l == 1 and g >= 2:
                            act.wait_ge(JB["1s"].taken, at(gb, G, g - 2))
                        nc.scalar.activation(bt[:, k % 2, :], bank[:, :], ACT.Copy, scale=SLOPE).then_inc(S["b_t_ready"], 1)

                    def b_exp(l, g):
                        k = {1: 0, 2: G, 3: 2 * G}[l] + g
                        if l == 2:
                            act.wait_ge(JB["2s"].taken, at(gb, G, g))
                        else:
                            act.wait_ge(S["b_shifted"], at(gb, G + 1, g if l == 1 else G))
                        nc.scalar.activation(bz[:, k % 2, :], bz[:, k % 2, :], ACT.Exp).then_inc(S["b_exp"], 1)

                    def b_pt(l, g):
                        bank = bank_b(f"{l}p", g)
                        act.wait_ge(JB[f"{l}p"].full, at(gb, JB[f"{l}p"].n, g))
                        nc.scalar.activation(bpt[:, g, :], bank[:, :], ACT.Copy).then_inc(JB[f"{l}p"].taken, 1)

                    def b_e(c):
                        bank = bank_b("1v", c)
                        act.wait_ge(JB["1v"].full, at(gb, JB["1v"].n, c))
                        if c:
                            act.wait_ge(S["b_full"], at(gb, FC, c - 1))
                        nc.scalar.activation(bE[:, :], bank[:, :], ACT.Exp).then_inc(S["b_e"], 1)

                    def q(m):
                        bank = bank_b("2q", m)
                        act.wait_ge(JB["2q"].full, at(gb, JB["2q"].n, m))
                        nc.scalar.activation(b1[:, m, :], bank[:, :], ACT.Identity, bias=q_b[:, m:m + 1], scale=QK_SCALE).then_inc(JB["2q"].taken, 1)

                    def k(m):
                        bank = bank_b("2k", m)
                        act.wait_ge(JB["2k"].full, at(gb, JB["2k"].n, m))
                        for i in range(2):
                            h = 2 * m + i
                            last = nc.scalar.activation(bpt[:, :, h * N:(h + 1) * N], four(bank[:, :]), ACT.Identity, bias=k_bh[:, m, i:i + 1],
                                                        scale=half[:, i:i + 1])
                        last.then_inc(JB["2k"].taken, 1)

                    def heads_hi(c):
                        bank = bank_b("2v", c)
                        act.wait_ge(JB["2v"].full, at(gb, JB["2v"].n, c))
                        nc.scalar.activation(b_in[0][:, c, :], bank[:, :], ACT.Copy).then_inc(S["2v_hi"], 1)

                    def g3(m):
                        bank = bank_b("3g", m)
                        act.wait_ge(JB["3g"].full, at(gb, JB["3g"].n, m))
                        nc.scalar.activation(b1[:, m, :], bank[:, :], ACT.Copy).then_inc(JB["3g"].taken, 1)

                    if with_b:
                        x(1, 0); x(1, 1)
                    if with_a:
                        xt(0); xt(1)
                    if with_b:
                        rows_l1(); copy_nodes(1, 0); copy_nodes(1, 1)
                    if with_a:
                        m1(0)
                    if with_b:
                        b_scaled(1, 0); b_scaled(1, 1)
                    if with_a:
                        m1(1)
                    if with_b:
                        b_exp(1, 0)
                    if with_a:
                        m1(2)
                    if with_b:
                        b_exp(1, 1)
                    if with_a:
                        m1(3)
                    if with_b:
                        b_pt(1, 0); b_scaled(1, 2); b_pt(1, 1); b_exp(1, 2); b_scaled(1, 3)
                    if with_a:
                        rows_p(0); h1(0)
                    if with_b:
                        b_exp(1, 3); b_pt(1, 2)
                    if with_a:
                        h1(1)
                    if with_b:
                        b_pt(1, 3)
                    if with_a:
                        h1(2)
                    if with_b:
                        b_e(0); b_e(1)
                    if with_a:
                        h1(3); scaled(0); exp(0)
                    if with_b:
                        x(2, 0); x(2, 1); q(0); q(1); k(0); k(1); b_exp(2, 0)
                    if with_a:
                        pt(0)
                    if with_b:
                        b_exp(2, 1)
                    if with_a:
                        e1(0, 0); e2(0, 0)
                    if with_b:
                        b_pt(2, 0)
                    if with_a:
                        v1_hi(0)
                    if with_b:
                        b_pt(2, 1)
                    if with_a:
                        e1(0, 1)
                    if with_b:
                        b_exp(2, 2)
                    if with_a:
                        e2(0, 1)
                    if with_b:
                        b_exp(2, 3)
                    if with_a:
                        v1_hi(1); e1(0, 2)
                    if with_b:
                        b_pt(2, 2)
                    if with_a:
                        e2(0, 2)
                    if with_b:
                        b_pt(2, 3)
                    if with_a:
                        v1_hi(2); e1(0, 3)
                    if with_b:
                        heads_hi(0)
                    if with_a:
                        e2(0, 3)
                    if with_b:
                        heads_hi(1)
                    if with_a:
                        v1_hi(3); m2(0); m2(1)
                    if with_b:
                        x(3, 0); x_full(0); x(3, 1); x_full(1)
                    if with_a:
                        rows_p(1); h2(0)
                    if with_b:
                        g3(0)
                    if with_a:
                        h2(1)
                    if with_b:
                        g3(1)
                    if with_a:
                        scaled(1)
                    if with_b:
                        copy_nodes(3, 0); copy_nodes(3, 1)
                    if with_a:
                        exp(1)
                    if with_b:
                        b_scaled(3, 0)
                    if with_a:
                        pt(1)
                    if with_b:
                        b_exp(3, 0)
                    if with_a:
                        e1(1, 0); e1(1, 1); e2(1, 0)
                    if with_b:
                        b_pt(3, 0)
                    if with_a:
                        e2(1, 1)
                steps(act, body)

            @block.vector
            def _(dve):
                def body(ga, gb, with_a, with_b):
                    def stats(x, st, mv, link):
                        for g in range(G):
                            last = nc.vector.bn_stats(st[:, g, :], x[:, g, :])
                        last.then_inc(link[0], 1)
                        dve.wait_ge(link[0], at(*link[1:]))
                        nc.vector.memset(carrier[:, :], 0.0)
                        for g in range(G):
                            last = nc.vector.bn_aggr(mv[:, g, :], st[:, g, :])
                        return last

                    def normalise(x, xn, mv, rs):
                        for g in range(G):
                            last = nc.vector.tensor_scalar(xn[:, g, :], x[:, g, :], mv[:, g, 0:1], rs[:, g:g + 1], ALU.subtract, ALU.mult)
                        return last

                    def a_stats():
                        dve.wait_ge(S["ax_loaded"], at(ga, 16, 15))
                        stats(ax, a_st, a_mv, (a_link, ga, 1, 0)).then_inc(S["a_var"], 1)

                    def a_normalise():
                        dve.wait_ge(S["a_rstd"], at(ga, 1, 0))
                        normalise(ax, axn, a_mv, a_rs).then_inc(S["axn_ready"], 1)

                    def xt(c):
                        bank = bank_a("xt", c)
                        dve.wait_ge(JA["xt"].full, at(ga, JA["xt"].n, c))
                        dve.wait_ge(S["a_hi_ready"], at(ga, 2, c))
                        nc.vector.scalar_tensor_tensor(out=a_in[1][:, c, :], in0=bank[:, :], scalar=0.0, in1=a_in[0][:, c, :],
                                                       op0=ALU.max, op1=ALU.subtract).then_inc(JA["xt"].taken, 1)

                    def m1(m):
                        dve.wait_ge(JA["m1"].taken, at(ga, HC, m))
                        nc.vector.tensor_copy(a_mid[0][:, m, :], o1[:, m, :]).then_inc(S["m1_hi_d"], 1)
                        dve.wait_ge(S["m1_hi_d"], at(ga, HC + FC, m))
                        nc.vector.tensor_tensor(a_mid[1][:, m, :], o1[:, m, :], a_mid[0][:, m, :], ALU.subtract).then_inc(S["m1_ready"], 1)

                    def rows_q(which):
                        name = ("f1", "f2")[which]
                        bank = bank_a(name, 0)
                        dve.wait_ge(JA[name].full, at(ga, JA[name].n, 0))
                        dve.wait_ge(S["a_p_ready"], at(ga, 2, which))
                        nc.vector.tensor_scalar(aq[0:2, :], bank[0:2, :], row1[0:2, :], row0[0:2, :], ALU.mult, ALU.add) \
                            .then_inc(JA[name].taken, 1)

                    def lrelu(which):
                        name = ("s1", "s2")[which]
                        dve.wait_ge(S["a_t_ready"], at(ga, 2, which))
                        nc.vector.tensor_tensor(az[:, :], bank_a(name, 0)[:, :], at_[:, :], ALU.max).then_inc(JA[name].taken, 1)
                        dve.wait_ge(JA[name].taken, at(ga, 1, 0))
                        nc.vector.tensor_reduce(a_max[:, :], four(az[:, :]), AX, ALU.max).then_inc(S["a_z_max"], 1)

                    def total(which):
                        dve.wait_ge(S["a_exp"], at(ga, 2, which))
                        nc.vector.tensor_reduce(a_sum[:, :], four(az[:, :]), AX, ALU.add).then_inc(a_sum_link, 1)
                        dve.wait_ge(a_sum_link, at(ga, 2, which))
                        nc.vector.reciprocal(a_inv[:, :], a_sum[:, :]).then_inc(S["a_inv_ready"], 1)

                    def u(which, c):
                        k = which * HC + c
                        name = ("v1", "v2")[which]
                        dve.wait_ge(S["a_e1"], at(ga, HC + FC, k))
                        nc.vector.tensor_scalar(aE[:, k % 2, :], aE[:, k % 2, :], 1.0, None, ALU.min).then_inc(S["a_u"], 1)
                        res = (o1, o2)[which]
                        nc.vector.scalar_tensor_tensor(out=aR[:, k % 2, :], in0=bank_a(name, c)[:, :], scalar=0.0, in1=res[:, c, :],
                                                       op0=ALU.max, op1=ALU.add).then_inc(JA[name].taken, 1)

                    def out1(c):
                        dve.wait_ge(S["a_e2"], at(ga, HC + FC, c))
                        dve.wait_ge(JA["v1"].taken, at(ga, HC, c))
                        nc.vector.scalar_tensor_tensor(out=aF[:, c % 2, :], in0=aE[:, c % 2, :], scalar=-1.0, in1=aR[:, c % 2, :],
                                                       op0=ALU.add, op1=ALU.add).then_inc(S["a_f"], 1)

                    def out1_lo(c):
                        dve.wait_ge(S["m1_hi"], at(ga, HC, c))
                        nc.vector.tensor_tensor(a_mid[1][:, c, :], aF[:, c % 2, :], a_mid[0][:, c, :], ALU.subtract).then_inc(S["v1_hi"], 1)

                    def m2(m):
                        dve.wait_ge(JA["m2"].taken, at(ga, FC, m))
                        nc.vector.tensor_copy(a_in[0][:, m, :], o2[:, m, :]).then_inc(S["m1_hi_d"], 1)
                        dve.wait_ge(S["m1_hi_d"], at(ga, HC + FC, HC + m))
                        nc.vector.tensor_tensor(a_in[1][:, m, :], o2[:, m, :], a_in[0][:, m, :], ALU.subtract).then_inc(S["m2_ready"], 1)

                    def out2(c):
                        k = HC + c
                        dve.wait_ge(S["a_e2"], at(ga, HC + FC, k))
                        dve.wait_ge(JA["v2"].taken, at(ga, FC, c))
                        nc.vector.scalar_tensor_tensor(out=ay[:, c, :], in0=aE[:, k % 2, :], scalar=-1.0, in1=aR[:, k % 2, :],
                                                       op0=ALU.add, op1=ALU.add).then_inc(S["a_f"], 1)

                    def y0(b):
                        bank = bank_a("y0", b)
                        dve.wait_ge(JA["y0"].full, at(ga, JA["y0"].n, b))
                        if b == 0:
                            dve.wait_ge(S["ax_res_loaded"], at(ga, 16, 15))
                        nc.vector.scalar_tensor_tensor(out=x1[:, 2 * b:2 * b + 2, :].rearrange("p a b -> p (a b)"), in0=bank[:, :], scalar=0.0,
                                                       in1=ax_res[:, 2 * b:2 * b + 2, :].rearrange("p a b -> p (a b)"),
                                                       op0=ALU.max, op1=ALU.add).then_inc(JA["y0"].taken, 1)

                    def b_stats(l):
                        x = x1 if l == 1 else bx
                        if l == 1:
                            dve.wait_ge(JA["y0"].taken, at(gb, 2, 1))
                        else:
                            name = f"{l - 1}y"
                            dve.wait_ge(JB[name].taken, at(gb, 2, 1))
                        stats(x, b_st, b_mv, (b_link, gb, 3, l - 1)).then_inc(S["b_var"], 1)

                    def b_normalise(l):
                        dve.wait_ge(S["b_rstd"], at(gb, 3, l - 1))
                        if l == 1 and not isinstance(gb, int) or l == 1 and gb > 0:
                            dve.wait_ge(S["out_stored"], gb * 16)
                        normalise(x1 if l == 1 else bx, bxn, b_mv, b_rs).then_inc(S["bxn_ready"], 1)

                    def x(l, c):
                        bank = bank_b(f"{l}x", c)
                        dve.wait_ge(JB[f"{l}x"].full, at(gb, JB[f"{l}x"].n, c))
                        dve.wait_ge(S["b_hi_ready"], at(gb, 6, 2 * (l - 1) + c))
                        if l == 3:
                            dve.wait_ge(S["3x_full"], at(gb, 2, c))
                        nc.vector.scalar_tensor_tensor(out=b_in[1][:, c, :], in0=bank[:, :], scalar=0.0, in1=b_in[0][:, c, :],
                                                       op0=ALU.max, op1=ALU.subtract).then_inc(JB[f"{l}x"].taken, 1)

                    def rows_l1():
                        bank = bank_b("1f", 0)
                        dve.wait_ge(JB["1f"].full, at(gb, JB["1f"].n, 0))
                        dve.wait_ge(S["b1_p"], at(gb, 1, 0))
                        for h in range(HEADS):
                            last = nc.vector.tensor_scalar(bpt[:, :, h * N:(h + 1) * N], four(bank[:, :]), ident[:, 32 * h + 1:32 * h + 2],
                                                           ident[:, 32 * h:32 * h + 1], ALU.mult, ALU.add)
                        last.then_inc(JB["1f"].taken, 1)

                    def b_lrelu(l, g):
                        k = {1: 0, 3: 2 * G}[l] + g
                        kt = g if l == 1 else G
                        dve.wait_ge(S["b_t_ready"], at(gb, G + 1, kt))
                        z_free(l, g)
                        nc.vector.tensor_tensor(bz[:, k % 2, :], bank_b(f"{l}s", g)[:, :], bt[:, kt % 2, :], ALU.max).then_inc(JB[f"{l}s"].taken, 1)
                        dve.wait_ge(JB[f"{l}s"].taken, at(gb, JB[f"{l}s"].n, g))
                        nc.vector.tensor_reduce(b_max[:, k % 2, :], four(bz[:, k % 2, :]), AX, ALU.max).then_inc(S["b_z_max"], 1)

                    def z_free(l, g):
                        if g >= 2:
                            dve.wait_ge(JB[f"{l}p"].full, at(gb, G, g - 2))

                    def b_max2(g):
                        k = G + g
                        bank = bank_b("2s", g)
                        dve.wait_ge(JB["2s"].full, at(gb, JB["2s"].n, g))
                        z_free(2, g)
                        nc.vector.tensor_reduce(b_max[:, k % 2, :], four(bank[:, :]), AX, ALU.max).then_inc(max_link, 1)
                        dve.wait_ge(max_link, at(gb, G, g))
                        nc.vector.tensor_tensor(four(bz[:, k % 2, :]), four(bank[:, :]), b_max[:, k % 2, :].unsqueeze(2).to_broadcast([P, 4, N]),
                                                ALU.subtract).then_inc(JB["2s"].taken, 1)

                    def b_total(l, g):
                        k = {1: 0, 2: G, 3: 2 * G}[l] + g
                        dve.wait_ge(S["b_exp"], at(gb, 2 * G + 1, k))
                        nc.vector.tensor_reduce(b_sum[:, k % 2, :], four(bz[:, k % 2, :]), AX, ALU.add).then_inc(b_sum_link, 1)
                        dve.wait_ge(b_sum_link, at(gb, 2 * G + 1, k))
                        i = nc.vector.reciprocal(b_inv[:, k % 2, :], b_sum[:, k % 2, :])
                        if l == 2:
                            i.then_inc(b_edge_link, 1)
                            dve.wait_ge(b_edge_link, at(gb, G, g))
                            i = nc.vector.tensor_scalar(b_inv[:, k % 2, :], b_inv[:, k % 2, :], has_edge[:, :], None, ALU.mult)
                        i.then_inc(S["b_inv_ready"], 1)

                    def elu(c):
                        bank = bank_b("1v", c)
                        dve.wait_ge(JB["1v"].full, at(gb, JB["1v"].n, c))
                        dve.wait_ge(S["b_e"], at(gb, FC, c))
                        nc.vector.tensor_scalar(bR[:, :], bank[:, :], 0.0, -1.0, ALU.max, ALU.add).then_inc(JB["1v"].taken, 1)
                        dve.wait_ge(JB["1v"].taken, at(gb, FC, c))
                        nc.vector.scalar_tensor_tensor(out=b2[:, c, :], in0=bE[:, :], scalar=1.0, in1=bR[:, :],
                                                       op0=ALU.min, op1=ALU.add).then_inc(S["b_full"], 1)

                    def y_l1(b):
                        bank = bank_b("1y", b)
                        dve.wait_ge(JB["1y"].full, at(gb, JB["1y"].n, b))
                        r = slice(2 * b, 2 * b + 2)
                        nc.vector.tensor_tensor(bx[:, r, :].rearrange("p a b -> p (a b)"), bank[:, :], x1[:, r, :].rearrange("p a b -> p (a b)"),
                                                ALU.add).then_inc(JB["1y"].taken, 1)

                    def v_bias(b):
                        bank = bank_b("2h", b)
                        dve.wait_ge(JB["2h"].full, at(gb, JB["2h"].n, b))
                        nc.vector.tensor_tensor(b3[:, 2 * b:2 * b + 2, :], bank[:, :].rearrange("p (a b) -> p a b", a=2),
                                                v_b[:, :].unsqueeze(1).to_broadcast([P, 2, F]), ALU.add).then_inc(JB["2h"].taken, 1)

                    def heads_lo(c):
                        bank = bank_b("2v", c)
                        dve.wait_ge(S["2v_hi"], at(gb, 2, c))
                        nc.vector.tensor_tensor(b_in[1][:, c, :], bank[:, :], b_in[0][:, c, :], ALU.subtract).then_inc(JB["2v"].taken, 1)

                    def y_l2(b):
                        bank = bank_b("2y", b)
                        dve.wait_ge(JB["2y"].full, at(gb, JB["2y"].n, b))
                        r = slice(2 * b, 2 * b + 2)
                        if b == 0:
                            dve.wait_ge(S["bx_bias"], at(gb, 1, 0))
                        v = bx[:, r, :].rearrange("p a b -> p (a b)")
                        nc.vector.tensor_tensor(v, bank[:, :], v, ALU.add).then_inc(JB["2y"].taken, 1)

                    def y_l3(b):
                        bank = bank_b("3y", b)
                        dve.wait_ge(JB["3y"].full, at(gb, JB["3y"].n, b))
                        r = slice(2 * b, 2 * b + 2)
                        nc.vector.scalar_tensor_tensor(out=bxn[:, r, :].rearrange("p a b -> p (a b)"), in0=bank[:, :], scalar=0.0,
                                                       in1=bx[:, r, :].rearrange("p a b -> p (a b)"), op0=ALU.max, op1=ALU.add) \
                            .then_inc(JB["3y"].taken, 1)

                    if with_b:
                        b_stats(1)
                    if with_a:
                        a_stats()
                    if with_b:
                        b_normalise(1)
                    if with_a:
                        a_normalise()
                    if with_b:
                        x(1, 0); x(1, 1)
                    if with_a:
                        xt(0); xt(1)
                    if with_b:
                        rows_l1()
                    if with_a:
                        m1(0)
                    if with_b:
                        b_lrelu(1, 0); b_lrelu(1, 1)
                    if with_a:
                        m1(1)
                    if with_b:
                        b_total(1, 0); b_total(1, 1)
                    if with_a:
                        m1(2); m1(3)
                    if with_b:
                        b_lrelu(1, 2); b_total(1, 2); b_lrelu(1, 3)
                    if with_a:
                        rows_q(0)
                    if with_b:
                        b_total(1, 3); elu(0); elu(1); y_l1(0); y_l1(1); b_stats(2)
                    if with_a:
                        lrelu(0)
                    if with_b:
                        b_normalise(2)
                    if with_a:
                        total(0)
                    if with_b:
                        x(2, 0); x(2, 1); v_bias(0); v_bias(1); b_max2(0); b_max2(1); b_total(2, 0)
                        b_total(2, 1)
                    if with_a:
                        u(0, 0); out1(0)
                    if with_b:
                        b_max2(2)
                    if with_a:
                        u(0, 1)
                    if with_b:
                        b_total(2, 2); b_max2(3)
                    if with_a:
                        out1(1)
                    if with_b:
                        b_total(2, 3)
                    if with_a:
                        out1_lo(0); u(0, 2); out1(2); out1_lo(1); u(0, 3)
                    if with_b:
                        heads_lo(0)
                    if with_a:
                        out1(3)
                    if with_b:
                        heads_lo(1)
                    if with_a:
                        out1_lo(2); out1_lo(3)
                    if with_b:
                        y_l2(0); y_l2(1); b_stats(3); b_normalise(3)
                    if with_a:
                        m2(0); m2(1)
                    if with_b:
                        x(3, 0); x(3, 1)
                    if with_a:
                        rows_q(1); lrelu(1); total(1)
                    if with_b:
                        b_lrelu(3, 0); b_total(3, 0)
                    if with_a:
                        u(1, 0); u(1, 1); out2(0); out2(1)
                    if with_b:
                        y_l3(0); y_l3(1)
                    if with_a:
                        y0(0); y0(1)
                steps(dve, body)

            @block.gpsimd
            def _(pool):
                def body(ga, gb, with_a, with_b):
                    def rstd(mv, ve, rs, link):
                        nc.gpsimd.tensor_tensor(ve[:, :], mv[:, :, 1], eps_t[:, :], ALU.add).then_inc(link[0], 1)
                        pool.wait_ge(link[0], at(*link[1:]))
                        return nc.gpsimd.tensor_tensor(rs[:, :], ve[:, :], pow_t[:, :], ALU.pow)

                    def a_rstd():
                        pool.wait_ge(S["a_var"], at(ga, 1, 0))
                        rstd(a_mv, a_ve, a_rs, (a_ve_link, ga, 1, 0)).then_inc(S["a_rstd"], 1)

                    def b_rstd(l):
                        pool.wait_ge(S["b_var"], at(gb, 3, l - 1))
                        rstd(b_mv, b_ve, b_rs, (b_ve_link, gb, 3, l - 1)).then_inc(S["b_rstd"], 1)

                    def shift(which):
                        pool.wait_ge(S["a_z_max"], at(ga, 2, which))
                        nc.gpsimd.tensor_tensor(four(az[:, :]), four(az[:, :]), a_max[:, :].unsqueeze(2).to_broadcast([P, 4, N]), ALU.subtract) \
                            .then_inc(S["a_shifted"], 1)

                    def norm(which):
                        pool.wait_ge(S["a_inv_ready"], at(ga, 2, which))
                        nc.gpsimd.tensor_tensor(four(az[:, :]), four(az[:, :]), a_inv[:, :].unsqueeze(2).to_broadcast([P, 4, N]), ALU.mult) \
                            .then_inc(S["a_norm"], 1)

                    def b_shift(l, g):
                        k = {1: 0, 3: 2 * G}[l] + g
                        kt = g if l == 1 else G
                        pool.wait_ge(S["b_z_max"], at(gb, G + 1, kt))
                        z = four(bz[:, k % 2, :])
                        nc.gpsimd.tensor_tensor(z, z, b_max[:, k % 2, :].unsqueeze(2).to_broadcast([P, 4, N]), ALU.subtract) \
                            .then_inc(S["b_shifted"], 1)

                    def b_norm(l, g):
                        k = {1: 0, 2: G, 3: 2 * G}[l] + g
                        pool.wait_ge(S["b_inv_ready"], at(gb, 2 * G + 1, k))
                        z = four(bz[:, k % 2, :])
                        nc.gpsimd.tensor_tensor(z, z, b_inv[:, k % 2, :].unsqueeze(2).to_broadcast([P, 4, N]), ALU.mult) \
                            .then_inc(S["b_norm"], 1)

                    def out_bias():
                        pool.wait_ge(S["bxn_ready"], at(gb, 3, 1))
                        nc.gpsimd.tensor_tensor(bx[:, :, :], bx[:, :, :], o_b[:, :].unsqueeze(1).to_broadcast([P, G, F]), ALU.add) \
                            .then_inc(S["bx_bias"], 1)

                    if with_b:
                        b_rstd(1)
                    if with_a:
                        a_rstd()
                    if with_b:
                        b_shift(1, 0); b_shift(1, 1); b_norm(1, 0); b_norm(1, 1); b_shift(1, 2); b_norm(1, 2)
                        b_shift(1, 3); b_norm(1, 3); b_rstd(2)
                    if with_a:
                        shift(0)
                    if with_b:
                        out_bias()
                    if with_a:
                        norm(0)
                    if with_b:
                        b_norm(2, 0); b_norm(2, 1); b_norm(2, 2); b_norm(2, 3); b_rstd(3)
                    if with_a:
                        shift(1); norm(1)
                    if with_b:
                        b_shift(3, 0); b_norm(3, 0)
                steps(pool, body)


_OUT_SHAPE = (128, 128, 256)


def kernel(**inputs):
    import numpy as np
    import concourse.bacc as bacc
    from concourse.bass_utils import run_bass_kernel_spmd as run

    heads, feats, hd = inputs["L1_gnn_W"].shape
    a = np.asarray(inputs["L1_gnn_a"])
    a_blocks = np.zeros((heads, hd, heads, 2), a.dtype)
    for h in range(heads):
        a_blocks[h, :, h, 0] = a[h, :hd]
        a_blocks[h, :, h, 1] = a[h, hd:]

    def pair(v):
        v = np.asarray(v)
        return v.reshape(2, -1).T

    def t(name):
        return np.asarray(inputs[name]).T

    l1 = np.asarray(inputs["L1_gnn_W"])
    arrays = {
        "x": inputs["x"], "adj": inputs["adj"],
        "w_mlp1": inputs["L0_gnn_mlp1_w"], "b_mlp1": inputs["L0_gnn_mlp1_b"],
        "w_mlp2": inputs["L0_gnn_mlp2_w"], "b_mlp2": inputs["L0_gnn_mlp2_b"],
        "w_fc": inputs["L0_gnn_W_fc"], "w_fcT": t("L0_gnn_W_fc"), "a_fc": pair(inputs["L0_gnn_a_fc"]),
        "w_hand": inputs["L0_gnn_W_hand"], "w_handT": t("L0_gnn_W_hand"), "a_hand": pair(inputs["L0_gnn_a_hand"]),
        "w_l1": l1.transpose(1, 0, 2).reshape(feats, heads * hd), "w_l1T": l1.transpose(0, 2, 1).reshape(heads * hd, feats),
        "a_l1": a_blocks.reshape(heads * hd, 2 * heads),
        "w_q": t("L2_gnn_wq"), "b_q": inputs["L2_gnn_bq"], "w_k": t("L2_gnn_wk"), "b_k": inputs["L2_gnn_bk"],
        "w_v": t("L2_gnn_wv"), "b_v": inputs["L2_gnn_bv"], "w_o": t("L2_gnn_wo"), "b_o": inputs["L2_gnn_bo"],
        "w_1T": t("L3_gnn_W1"), "w_2T": t("L3_gnn_W2"), "w_h3": inputs["L3_gnn_W3"],
    }
    arrays = {k: np.ascontiguousarray(v) for k, v in arrays.items()}
    nc = bacc.Bacc("TRN2", target_bir_lowering=False, num_devices=1)
    ins = {k: nc.dram_tensor("in_" + k, v.shape, mybir.dt.from_np(v.dtype), kind="ExternalInput").ap() for k, v in arrays.items()}
    out = nc.dram_tensor("out_0", _OUT_SHAPE, mybir.dt.float32, kind="ExternalOutput").ap()
    gnn_stack_kernel(nc, ins, out)
    r = run(nc, [{"in_" + k: v for k, v in arrays.items()}], core_ids=[0])
    return r.results[0]["out_0"]
```

```python
from contextlib import ExitStack

import concourse.bass as bass
from concourse import mybir


def gnn_stack_kernel(nc, ins, out):
    f32, f32r, bf16, i32 = mybir.dt.float32, mybir.dt.float32r, mybir.dt.bfloat16, mybir.dt.int32
    ALU, ACT, AX = mybir.AluOpType, mybir.ActivationFunctionType, mybir.AxisListType.X

    B, N, F = ins["x"].shape
    HID = ins["w_mlp1"].shape[1]
    HEADS = 4
    HD = F // HEADS
    G = 4
    T = G * N
    NT = B // G
    P = 128
    FC, HC = F // P, HID // P
    GP = G // 2
    EPS, SLOPE, MASKED = 1e-5, 0.2, -9.0e15
    QK_SCALE = float(HD) ** -0.5
    X_GROUPS = ins["x"].rearrange("(t g) n f -> t n g f", g=G)
    OUT_GROUPS = out.rearrange("(t g) n f -> t n g f", g=G)

    ctx = ExitStack()
    with ctx:
        def sb(name, shape, dt=f32):
            return ctx.enter_context(nc.sbuf_tensor(name, shape, dt))

        def sem(name):
            return ctx.enter_context(nc.semaphore(name))

        def split(name, chunks, cols):
            return sb(name + "_hi", [P, chunks, cols], f32r), sb(name + "_lo", [P, chunks, cols], f32r)

        mlp1_w, fc_w = split("mlp1_w", FC, HID), split("fc_w", HC, HID)
        mlp2_w, hand_w = split("mlp2_w", HC, F), split("hand_w", FC, F)
        l1_w, q_w, k_w, v_w, o_w = (split(n, FC, F) for n in ("l1_w", "q_w", "k_w", "v_w", "o_w"))
        bil_w, h3_w = split("bil_w", FC, F), split("h3_w", FC, F)
        fa1_w, fa2_w, fah_w = split("fa1_w", HC, P), split("fa2_w", FC, P), split("fah_w", FC, P)

        ident = sb("ident", [P, P])
        ident_bf = sb("ident_bf", [P, P], bf16)
        mask_gt = sb("mask_gt", [P, N], bf16)
        mask_ne = sb("mask_ne", [P, N], bf16)
        has_edge = sb("has_edge", [P, 1])
        row0, row1 = sb("row0", [P, 1]), sb("row1", [P, 1])
        mlp1_b, mlp2_b = sb("mlp1_b", [P, HC]), sb("mlp2_b", [P, FC])
        q_b, k_b = sb("q_b", [P, FC]), sb("k_b", [P, FC])
        half, k_bh = sb("half", [P, 2]), sb("k_bh", [P, FC, 2])
        v_b, o_b = sb("v_b", [P, F]), sb("o_b", [P, F])
        minus1, carrier = sb("minus1", [P, 1]), sb("carrier", [P, 1])
        eps_t, pow_t = sb("eps_t", [P, G]), sb("pow_t", [P, G])

        ax = sb("ax", [P, G, F])
        a_in = sb("a_in_hi", [P, FC, T], f32r), sb("a_in_lo", [P, FC, T], f32r)
        a_mid = sb("a_mid_hi", [P, HC, T], f32r), sb("a_mid_lo", [P, HC, T], f32r)
        o1 = sb("o1", [P, HC, T])
        o2 = o1
        ah = sb("ah", [P, G, HID])
        ay = ah[:, 0:FC, :]
        az, apt = sb("az", [P, T]), sb("apt", [P, T])
        aE, aR, aF = sb("aE", [P, 2, T]), sb("aR", [P, 2, T]), sb("aF", [P, 2, T])
        at_ = aE[:, 0, :]
        ap, aq = aR[:, 0, :], aR[:, 1, :]
        axn = ah2 = aF[:, :, :].rearrange("p a (b f) -> p (a b) f", f=F)
        a_st, a_mv = sb("a_st", [P, G, 6]), sb("a_mv", [P, G, 2])
        a_ve, a_rs = sb("a_ve", [P, G]), sb("a_rs", [P, G])
        a_max, a_sum, a_inv = sb("a_max", [P, G]), sb("a_sum", [P, G]), sb("a_inv", [P, G])
        x1 = sb("x1", [P, G, F])
        bx = sb("bx", [P, G, F])
        b_in = sb("b_in_hi", [P, FC, T], f32r), sb("b_in_lo", [P, FC, T], f32r)
        b1, b3 = sb("b1", [P, 2, T]), sb("b3", [P, G, F])
        bxn, b2 = b3, b1
        bt, bz, bpt = sb("bt", [P, 2, T]), sb("bz", [P, 2, T]), sb("bpt", [P, G, T])
        bE, bR = bt[:, 0, :], bt[:, 1, :]
        b_st, b_mv = sb("b_st", [P, G, 6]), sb("b_mv", [P, G, 2])
        b_ve, b_rs = sb("b_ve", [P, G]), sb("b_rs", [P, G])
        b_max, b_sum, b_inv = sb("b_max", [P, 2, 4]), sb("b_sum", [P, 2, 4]), sb("b_inv", [P, 2, 4])
        cx = sb("cx", [P, G, F])
        c_in = sb("c_in_hi", [P, FC, T], f32r), sb("c_in_lo", [P, FC, T], f32r)
        c1, c2, c3 = sb("c1", [P, 2, T]), sb("c2", [P, 2, T]), sb("c3", [P, G, F])
        cxn = c3
        ct, cz, cpt = c2[:, 0, :], c2[:, 1, :], c1[:, 0, :]
        c_st, c_mv = sb("c_st", [P, G, 6]), sb("c_mv", [P, G, 2])
        c_ve, c_rs = sb("c_ve", [P, G]), sb("c_rs", [P, G])
        c_max, c_sum, c_inv = sb("c_max", [P, G]), sb("c_sum", [P, G]), sb("c_inv", [P, G])

        banks = [ctx.enter_context(nc.psum_tensor(f"bank{i}", [P, T], f32)) for i in range(8)]

        s_const, s_used = sem("s_const"), sem("s_used")
        s_stage = [sem("s_stage0"), sem("s_stage1")]
        s_id, s_setup_pe, s_folded = sem("s_id"), sem("s_setup_pe"), sem("s_folded")
        stage = [o1[:, :, :].rearrange("p a b -> p (a b)"), ah[:, :, :].rearrange("p a b -> p (a b)")]
        adj_i = az[:, 0:N].bitcast(i32)
        w_plan = [("w_mlp1", mlp1_w), ("w_fc", fc_w), ("w_mlp2", mlp2_w), ("w_hand", hand_w), ("w_l1", l1_w),
                  ("w_q", q_w), ("w_k", k_w), ("w_v", v_w), ("w_o", o_w), ("w_h3", h3_w)]
        f_plan = [("w_fcT", "a_fc", fa1_w, HC, HC, 2), ("w_handT", "a_hand", fa2_w, FC, FC, 2),
                  ("w_l1T", "a_l1", fah_w, FC, FC, 2 * HEADS), ("w_1T", "w_2T", bil_w, FC, FC, F)]
        with nc.Block() as block:
            @block.sync
            def _(sp):
                consts = [(adj_i, ins["adj"]),
                          (mlp1_b[:, :], ins["b_mlp1"].rearrange("(c p) -> p c", p=P)),
                          (mlp2_b[:, :], ins["b_mlp2"].rearrange("(c p) -> p c", p=P)),
                          (q_b[:, :], ins["b_q"].rearrange("(c p) -> p c", p=P)),
                          (k_b[:, :], ins["b_k"].rearrange("(c p) -> p c", p=P)),
                          (v_b[:, :], ins["b_v"].rearrange("(a f) -> a f", a=1).to_broadcast([P, F])),
                          (o_b[:, :], ins["b_o"].rearrange("(a f) -> a f", a=1).to_broadcast([P, F]))]
                with nc.allow_non_contiguous_dma("small vectors, once"):
                    for dst, src in consts:
                        sp.dma_start(dst, src).then_inc(s_const, 16)
                    for i, (name, w) in enumerate(w_plan):
                        if i >= 2:
                            sp.wait_ge(s_used, i - 1)
                        c, n = w[0].shape[1], w[0].shape[2]
                        sp.dma_start(stage[i % 2][:, 0:c * n].rearrange("p (c n) -> p c n", c=c),
                                     ins[name].rearrange("(c p) n -> p c n", p=P)).then_inc(s_stage[i % 2], 16)
                    for j, (name, right, w, kc, dc, n) in enumerate(f_plan):
                        if j == 0:
                            sp.wait_ge(s_used, len(w_plan))
                        else:
                            sp.wait_ge(s_folded, j)
                        cols = ins[name].shape[1]
                        sp.dma_start(stage[0][:, 0:dc * cols].rearrange("p (c n) -> p c n", c=dc),
                                     ins[name].rearrange("(c p) n -> p c n", p=P)).then_inc(s_stage[0], 16)
                        sp.dma_start(stage[1][:, 0:dc * n].rearrange("p (c n) -> p c n", c=dc),
                                     ins[right].rearrange("(c p) n -> p c n", p=P)).then_inc(s_stage[1], 16)

            @block.gpsimd
            def _(pool):
                nc.gpsimd.memset(ident[:, :], 0.0).then_inc(s_id, 1)
                pool.wait_ge(s_id, 1)
                nc.gpsimd.affine_select(out=ident[:, :], in_=ident[:, :], compare_op=ALU.not_equal, fill=1.0,
                                        base=0, pattern=[[-1, P]], channel_multiplier=1).then_inc(s_id, 1)
                nc.gpsimd.memset(minus1[:, :], -1.0)
                nc.gpsimd.memset(eps_t[:, :], EPS)
                nc.gpsimd.memset(pow_t[:, :], -0.5)

            @block.tensor
            def _(pe):
                for j, (name, right, w, kc, dc, n) in enumerate(f_plan):
                    for part in s_stage:
                        pe.wait_ge(part, 16 * (len(w_plan) // 2 + j + 1))
                    if j:
                        pe.wait_ge(s_folded, j)
                    for k in range(kc):
                        for d in range(dc):
                            lhs = stage[0][:, 0:dc * kc * P].rearrange("p (c n) -> p c n", c=dc)[:, d, k * P:(k + 1) * P]
                            rhs = stage[1][:, 0:dc * n].rearrange("p (c n) -> p c n", c=dc)[:, d, :]
                            last = nc.tensor.matmul(banks[k][:, 0:n], lhs, rhs, start=d == 0, stop=d == dc - 1)
                    last.then_inc(s_setup_pe, 1)

            @block.vector
            def _(dve):
                links = sem("s_setup_links")
                done = [0]

                def link(i):
                    done[0] += 1
                    i.then_inc(links, 1)
                    dve.wait_ge(links, done[0])

                for w in (fa1_w, fa2_w, fah_w):
                    if w is fa1_w:
                        link(nc.vector.memset(at_, 0.0))
                    for part in w:
                        c = part.shape[1]
                        link(nc.vector.tensor_copy(part[:, :, :], at_[:, 0:c * P].rearrange("p (c n) -> p c n", c=c)))
                for i, (name, w) in enumerate(w_plan):
                    c, n = w[0].shape[1], w[0].shape[2]
                    src = stage[i % 2][:, 0:c * n].rearrange("p (c n) -> p c n", c=c)
                    dve.wait_ge(s_stage[i % 2], 16 * (i // 2 + 1))
                    link(nc.vector.tensor_copy(w[0][:, :, :], src))
                    nc.vector.tensor_tensor(w[1][:, :, :], src, w[0][:, :, :], ALU.subtract).then_inc(s_used, 1)
                for j, (name, right, w, kc, dc, n) in enumerate(f_plan):
                    dve.wait_ge(s_setup_pe, j + 1)
                    for k in range(kc):
                        if n == 2:
                            src = banks[k][:, 0:2]
                            hi, lo = (part[:, k, 0:2] for part in w)
                        elif n == F:
                            src = banks[k][:, 0:F]
                            hi, lo = (part[:, k, :] for part in w)
                        else:
                            src = banks[k][:, 0:n].rearrange("p (h x) -> p h x", x=2)
                            hi, lo = (part[:, k, :].rearrange("p (h x) -> p h x", x=P // HEADS)[:, :, 0:2] for part in w)
                        link(nc.vector.tensor_copy(hi, src))
                        last = nc.vector.tensor_tensor(lo, src, hi, ALU.subtract)
                    last.then_inc(s_folded, 1)
                dve.wait_ge(s_id, 2)
                nc.vector.tensor_copy(ident_bf[:, :], ident[:, :])
                nc.vector.tensor_reduce(row0[:, :], ident[:, 0:P:32], AX, ALU.add)
                nc.vector.tensor_reduce(row1[:, :], ident[:, 1:P:32], AX, ALU.add)
                link(nc.vector.tensor_reduce(half[:, :], ident[:, :].rearrange("p (i d) -> p i d", i=2), AX, ALU.add))
                dve.wait_ge(s_const, 16 * 7)
                link(nc.vector.tensor_scalar(q_b[:, :], q_b[:, :], QK_SCALE, None, ALU.mult))
                for m in range(FC):
                    nc.vector.tensor_scalar(k_bh[:, m, :], half[:, :], k_b[:, m:m + 1], None, ALU.mult)
                for mask, op in ((mask_gt, ALU.is_gt), (mask_ne, ALU.not_equal)):
                    link(nc.vector.tensor_scalar(at_[:, 0:N], adj_i, 0.0, None, op))
                    link(nc.vector.tensor_scalar(mask[:, :], at_[:, 0:N], 1.0, -MASKED, ALU.subtract, ALU.mult))
                link(nc.vector.tensor_reduce(has_edge[:, :], at_[:, 0:N], AX, ALU.max))

        class Job:
            def __init__(self, name, n):
                self.n, self.full, self.taken = n, sem(name + "_full"), sem(name + "_taken")

        def at(g, n, k):
            return g * n + (k + 1)

        A_ORDER = ["xt"] * 2 + ["m1"] * 4 + ["f1"] + ["h1"] * 4 + ["s1"] + ["p1"] + ["v1"] * 4 + ["m2"] * 2 + \
                  ["f2"] + ["h2"] * 2 + ["s2"] + ["p2"] + ["v2"] * 2 + ["y0"] * 2
        L1S = ["s", "s", "p", "s", "p", "s", "p", "p"]
        B_ORDER = ["1x"] * 2 + ["1f"] + ["1h"] * 2 + ["1" + c for c in L1S] + ["1v"] * 2 + ["1y"] * 2 + \
                  ["2x"] * 2 + ["2q"] * 2 + ["2k"] * 2 + ["2h"] * 2 + ["2" + c for c in L1S] + ["2v"] * 2 + ["2y"] * 2
        C_ORDER = ["3x"] * 2 + ["3g"] * 2 + ["3h"] * 2 + ["3s"] + ["3p"] + ["3y"] * 2

        def numbered(order, prefix):
            jobs, seen, where, at = {}, {}, {}, []
            for i, name in enumerate(order):
                k = seen.get(name, 0)
                seen[name] = k + 1
                where[name, k] = i
                at.append((name, k))
            for name in seen:
                jobs[name] = Job(prefix + name, seen[name])
            return jobs, where, at

        JA, WA, SA = numbered(A_ORDER, "a_")
        JB, WB, SB_ = numbered(B_ORDER, "b_")
        JC, WC, SC_ = numbered(C_ORDER, "c_")
        A_BANKS, B_BANKS, C_BANKS = banks[0:3], banks[3:6], banks[6:8]

        def bank_a(name, k):
            return A_BANKS[WA[name, k] % len(A_BANKS)]

        def bank_b(name, k):
            return B_BANKS[WB[name, k] % len(B_BANKS)]

        def bank_c(name, k):
            return C_BANKS[WC[name, k] % len(C_BANKS)]

        def bank_free(jobs, where, order, n, name, k, g):
            i = where[name, k]
            if i >= n:
                before, j = order[i - n]
                return jobs[before].taken, at(g, jobs[before].n, j)
            before, _ = order[max(j for j in range(len(order)) if j % n == i)]
            return jobs[before].taken, g * jobs[before].n

        def a_bank_free(name, k, g):
            return bank_free(JA, WA, SA, len(A_BANKS), name, k, g)

        def b_bank_free(name, k, g):
            return bank_free(JB, WB, SB_, len(B_BANKS), name, k, g)

        def c_bank_free(name, k, g):
            return bank_free(JC, WC, SC_, len(C_BANKS), name, k, g)

        names = ("ax_loaded x1_loaded a_var a_rstd axn_ready a_hi_ready m1_ready m1_hi m1_hi_d m2_ready "
                 "a_p_ready a_t_ready a_z_max a_shifted a_exp a_inv_ready a_norm a_e1 a_e2 a_u a_f v1_hi "
                 "b_var b_rstd bxn_ready b_hi_ready b1_p b_t_ready b_z_max b_shifted b_exp b_inv_ready b_norm "
                 "b_e b_full bx_bias 2v_hi "
                 "c_var c_rstd cxn_ready c_hi_ready 3x_full c_t_ready c_z_max c_shifted c_exp c_inv_ready c_norm out_stored").split()
        S = {n: sem("s_" + n) for n in names}

        def three(pe, psum, lhs, rhs, start, stop):
            nc.tensor.matmul(psum, lhs[0], rhs[0], start=start, stop=False)
            nc.tensor.matmul(psum, lhs[0], rhs[1], start=False, stop=False)
            return nc.tensor.matmul(psum, lhs[1], rhs[0], start=False, stop=stop)

        def parts(pair, *index):
            return pair[0][index], pair[1][index]

        def four(ap):
            return ap.rearrange("p (g j) -> p g j", g=4)

        ALL = slice(None)
        a_link, b_link, a_ve_link, b_ve_link = sem("a_stats_done"), sem("b_stats_done"), sem("a_var_eps"), sem("b_var_eps")
        c_link, c_ve_link, c_sum_link = sem("c_stats_done"), sem("c_var_eps"), sem("c_sum_done")
        a_sum_link, b_sum_link, max_link, b_edge_link = sem("a_sum_done"), sem("b_sum_done"), sem("b_max_done"), sem("b_inv_done")

        def steps(eng, body):
            body(0, None, None, True, False, False)
            body(1, 0, None, True, True, False)
            body(2, 1, 0, True, True, True)
            with eng.Fori(3, NT) as t:
                body(t, t - 1, t - 2, True, True, True)
            body(None, NT - 1, NT - 2, False, True, True)
            body(None, None, NT - 1, False, False, True)

        with nc.Block() as block:
            @block.sync
            def _(sp):
                sp.dma_start(ax[:, :, :], X_GROUPS[0]).then_inc(S["ax_loaded"], 16)

                def body(ga, gb, gc, with_a, with_b, with_c, another=True):
                    if with_a and another:
                        sp.wait_ge(S["axn_ready"], at(ga, 1, 0))
                        sp.dma_start(ax[:, :, :], X_GROUPS[ga + 1]).then_inc(S["ax_loaded"], 16)
                    if with_a:
                        if with_b:
                            sp.wait_ge(JB["1y"].taken, at(gb, 2, 1))
                        sp.dma_start(x1[:, :, :], X_GROUPS[ga]).then_inc(S["x1_loaded"], 16)
                    if with_c:
                        sp.wait_ge(JC["3y"].taken, at(gc, 2, 1))
                        sp.dma_start(OUT_GROUPS[gc], cx[:, :, :]).then_inc(S["out_stored"], 16)

                body(0, None, None, True, False, False)
                body(1, 0, None, True, True, False)
                body(2, 1, 0, True, True, True)
                with sp.Fori(3, NT - 1) as t:
                    body(t, t - 1, t - 2, True, True, True)
                body(NT - 1, NT - 2, NT - 3, True, True, True, another=False)
                body(None, NT - 1, NT - 2, False, True, True)
                body(None, None, NT - 1, False, False, True)
                sp.wait_ge(S["out_stored"], 16 * NT)

            @block.tensor
            def _(pe):
                def body(ga, gb, gc, with_a, with_b, with_c):
                    def transposes(bank, srcs):
                        for i, s in enumerate(srcs):
                            last = nc.tensor.transpose(bank[:, i * P:(i + 1) * P], s, ident[:, :])
                        return last

                    def project(bank, w, x, chunks, m):
                        for c in range(chunks):
                            last = three(pe, bank[:, :], parts(w, ALL, c, slice(m * P, (m + 1) * P)), parts(x, ALL, c, ALL),
                                         c == 0, c == chunks - 1)
                        return last

                    def project_nodes(bank, off, n, w, x, chunks, g):
                        for c in range(chunks):
                            last = three(pe, bank[:, off:off + n], parts(x, ALL, c, slice(g * N, (g + 1) * N)),
                                         parts(w, ALL, c, ALL), c == 0, c == chunks - 1)
                        return last

                    def xt(c):
                        bank = bank_a("xt", c)
                        pe.wait_ge(*a_bank_free("xt", c, ga))
                        if c == 0:
                            pe.wait_ge(S["axn_ready"], at(ga, 1, 0))
                        transposes(bank, [axn[:, g, c * P:(c + 1) * P] for g in range(G)]).then_inc(JA["xt"].full, 1)

                    def m1(m):
                        bank = bank_a("m1", m)
                        pe.wait_ge(*a_bank_free("m1", m, ga))
                        pe.wait_ge(JA["xt"].taken, at(ga, 2, 1))
                        project(bank, mlp1_w, a_in, FC, m).then_inc(JA["m1"].full, 1)

                    def f1():
                        bank = bank_a("f1", 0)
                        pe.wait_ge(*a_bank_free("f1", 0, ga))
                        pe.wait_ge(S["m1_ready"], at(ga, HC, HC - 1))
                        project(bank, fa1_w, a_mid, HC, 0).then_inc(JA["f1"].full, 1)

                    def h1(g):
                        bank = bank_a("h1", g)
                        pe.wait_ge(*a_bank_free("h1", g, ga))
                        project_nodes(bank, 0, HID, fc_w, a_mid, HC, g).then_inc(JA["h1"].full, 1)

                    def s1():
                        bank = bank_a("s1", 0)
                        pe.wait_ge(*a_bank_free("s1", 0, ga))
                        pe.wait_ge(S["a_p_ready"], at(ga, 2, 0))
                        pe.wait_ge(JA["f1"].taken, at(ga, 1, 0))
                        for g in range(G):
                            r = slice(g * N, (g + 1) * N)
                            last = nc.tensor.matmul(bank[:, r], ap[0:2, r], aq[0:2, r], start=True, stop=True)
                        last.then_inc(JA["s1"].full, 1)

                    def p1(which=0):
                        name = ("p1", "p2")[which]
                        bank = bank_a(name, 0)
                        pe.wait_ge(*a_bank_free(name, 0, ga))
                        pe.wait_ge(S["a_norm"], at(ga, 2, which))
                        transposes(bank, [az[:, g * N:(g + 1) * N] for g in range(G)]).then_inc(JA[name].full, 1)

                    def v1(c):
                        bank = bank_a("v1", c)
                        pe.wait_ge(*a_bank_free("v1", c, ga))
                        pe.wait_ge(JA["p1"].taken, at(ga, 1, 0))
                        pe.wait_ge(JA["h1"].taken, at(ga, G, G - 1))
                        for g in range(G):
                            r = slice(g * N, (g + 1) * N)
                            last = nc.tensor.matmul(bank[:, r], ah[:, g, c * P:(c + 1) * P], apt[:, r], start=True, stop=True)
                        last.then_inc(JA["v1"].full, 1)

                    def m2(m):
                        bank = bank_a("m2", m)
                        pe.wait_ge(*a_bank_free("m2", m, ga))
                        pe.wait_ge(S["v1_hi"], at(ga, HC, HC - 1))
                        project(bank, mlp2_w, a_mid, HC, m).then_inc(JA["m2"].full, 1)

                    def f2():
                        bank = bank_a("f2", 0)
                        pe.wait_ge(*a_bank_free("f2", 0, ga))
                        pe.wait_ge(S["m2_ready"], at(ga, FC, FC - 1))
                        project(bank, fa2_w, a_in, FC, 0).then_inc(JA["f2"].full, 1)

                    def h2(b):
                        bank = bank_a("h2", b)
                        pe.wait_ge(*a_bank_free("h2", b, ga))
                        for i in range(2):
                            last = project_nodes(bank, i * F, F, hand_w, a_in, FC, 2 * b + i)
                        last.then_inc(JA["h2"].full, 1)

                    def s2():
                        bank = bank_a("s2", 0)
                        pe.wait_ge(*a_bank_free("s2", 0, ga))
                        pe.wait_ge(S["a_p_ready"], at(ga, 2, 1))
                        pe.wait_ge(JA["f2"].taken, at(ga, 1, 0))
                        nc.tensor.matmul(four(bank[:, :]), ident_bf[:, :], mask_gt[:, :].unsqueeze(1).to_broadcast([P, 4, N]), start=True, stop=False)
                        for g in range(G):
                            r = slice(g * N, (g + 1) * N)
                            last = nc.tensor.matmul(bank[:, r], ap[0:2, r], aq[0:2, r], start=False, stop=g == G - 1)
                        last.then_inc(JA["s2"].full, 1)

                    def v2(c):
                        bank = bank_a("v2", c)
                        pe.wait_ge(*a_bank_free("v2", c, ga))
                        pe.wait_ge(JA["p2"].taken, at(ga, 1, 0))
                        pe.wait_ge(JA["h2"].taken, at(ga, 2, 1))
                        for g in range(G):
                            r = slice(g * N, (g + 1) * N)
                            last = nc.tensor.matmul(bank[:, r], ah2[:, g, c * P:(c + 1) * P], apt[:, r], start=True, stop=True)
                        last.then_inc(JA["v2"].full, 1)

                    def y0(b):
                        bank = bank_a("y0", b)
                        pe.wait_ge(*a_bank_free("y0", b, ga))
                        pe.wait_ge(S["a_f"], at(ga, HC + FC, HC + FC - 1))
                        transposes(bank, [ay[:, c, (2 * b + i) * N:(2 * b + i + 1) * N] for i in range(2) for c in range(FC)]) \
                            .then_inc(JA["y0"].full, 1)

                    def x(l, c):
                        bank = bank_b(f"{l}x", c)
                        pe.wait_ge(*b_bank_free(f"{l}x", c, gb))
                        if c == 0:
                            pe.wait_ge(S["bxn_ready"], at(gb, 2, l - 1))
                        transposes(bank, [bxn[:, g, c * P:(c + 1) * P] for g in range(G)]).then_inc(JB[f"{l}x"].full, 1)

                    def proj(l, name, w, m):
                        bank = bank_b(f"{l}{name}", m)
                        pe.wait_ge(*b_bank_free(f"{l}{name}", m, gb))
                        pe.wait_ge(JB[f"{l}x"].taken, at(gb, 2, 1))
                        project(bank, w, b_in, FC, m).then_inc(JB[f"{l}{name}"].full, 1)

                    def nodes(l, w, b):
                        bank = bank_b(f"{l}h", b)
                        pe.wait_ge(*b_bank_free(f"{l}h", b, gb))
                        pe.wait_ge(JB[f"{l}x"].taken, at(gb, 2, 1))
                        for i in range(2):
                            last = project_nodes(bank, i * F, F, w, b_in, FC, 2 * b + i)
                        last.then_inc(JB[f"{l}h"].full, 1)

                    def s_l1(g):
                        bank = bank_b("1s", g)
                        pe.wait_ge(*b_bank_free("1s", g, gb))
                        if g == 0:
                            pe.wait_ge(S["b1_p"], at(gb, 1, 0))
                            pe.wait_ge(JB["1f"].taken, at(gb, 1, 0))
                        nc.tensor.matmul(four(bank[:, :]), ident_bf[:, :], mask_gt[:, :].unsqueeze(1).to_broadcast([P, 4, N]), start=True, stop=False)
                        r = slice(g * N, (g + 1) * N)
                        nc.tensor.matmul(bank[:, :], b1[:, 0, r], bpt[:, g, :], start=False, stop=True).then_inc(JB["1s"].full, 1)

                    def s_l2(g):
                        bank = bank_b("2s", g)
                        pe.wait_ge(*b_bank_free("2s", g, gb))
                        if g == 0:
                            pe.wait_ge(JB["2q"].taken, at(gb, 2, 1))
                            pe.wait_ge(JB["2k"].taken, at(gb, 2, 1))
                        nc.tensor.matmul(four(bank[:, :]), ident_bf[:, :], mask_ne[:, :].unsqueeze(1).to_broadcast([P, 4, N]), start=True, stop=False)
                        r = slice(g * N, (g + 1) * N)
                        for c in range(FC):
                            last = nc.tensor.matmul(bank[:, 2 * c * N:2 * (c + 1) * N], b1[:, c, r], bpt[:, g, 2 * c * N:2 * (c + 1) * N],
                                                    start=False, stop=c == FC - 1)
                        last.then_inc(JB["2s"].full, 1)

                    def p(l, g):
                        bank = bank_b(f"{l}p", g)
                        pe.wait_ge(*b_bank_free(f"{l}p", g, gb))
                        base = (l - 1) * G
                        pe.wait_ge(S["b_norm"], at(gb, 2 * G, base + g))
                        slot = (base + g) % 2
                        transposes(bank, [bz[:, slot, h * N:(h + 1) * N] for h in range(4)]).then_inc(JB[f"{l}p"].full, 1)

                    def v(l, c):
                        bank = bank_b(f"{l}v", c)
                        pe.wait_ge(*b_bank_free(f"{l}v", c, gb))
                        pe.wait_ge(JB[f"{l}h"].taken, at(gb, 2, 1))
                        pe.wait_ge(JB[f"{l}p"].taken, at(gb, G, G - 1))
                        for g in range(G):
                            for i in range(2):
                                h = 2 * c + i
                                last = nc.tensor.matmul(bank[i * HD:(i + 1) * HD, g * N:(g + 1) * N], b3[:, g, h * HD:(h + 1) * HD],
                                                        bpt[:, g, h * N:(h + 1) * N], start=True, stop=True)
                        last.then_inc(JB[f"{l}v"].full, 1)

                    def y_l1(b):
                        bank = bank_b("1y", b)
                        pe.wait_ge(*b_bank_free("1y", b, gb))
                        pe.wait_ge(S["b_full"], at(gb, FC, FC - 1))
                        transposes(bank, [b2[:, c, (2 * b + i) * N:(2 * b + i + 1) * N] for i in range(2) for c in range(FC)]) \
                            .then_inc(JB["1y"].full, 1)

                    def y_l2(b):
                        bank = bank_b("2y", b)
                        pe.wait_ge(*b_bank_free("2y", b, gb))
                        pe.wait_ge(JB["2v"].taken, at(gb, 2, 1))
                        for i in range(2):
                            last = project_nodes(bank, i * F, F, o_w, b_in, FC, 2 * b + i)
                        last.then_inc(JB["2y"].full, 1)

                    def x_c(c):
                        bank = bank_c("3x", c)
                        pe.wait_ge(*c_bank_free("3x", c, gc))
                        if c == 0:
                            pe.wait_ge(S["cxn_ready"], at(gc, 1, 0))
                        transposes(bank, [cxn[:, g, c * P:(c + 1) * P] for g in range(G)]).then_inc(JC["3x"].full, 1)

                    def g_c(m):
                        bank = bank_c("3g", m)
                        pe.wait_ge(*c_bank_free("3g", m, gc))
                        pe.wait_ge(JC["3x"].taken, at(gc, 2, 1))
                        project(bank, bil_w, c_in, FC, m).then_inc(JC["3g"].full, 1)

                    def h_c(b):
                        bank = bank_c("3h", b)
                        pe.wait_ge(*c_bank_free("3h", b, gc))
                        for i in range(2):
                            last = project_nodes(bank, i * F, F, h3_w, c_in, FC, 2 * b + i)
                        last.then_inc(JC["3h"].full, 1)

                    def s_c():
                        bank = bank_c("3s", 0)
                        pe.wait_ge(*c_bank_free("3s", 0, gc))
                        pe.wait_ge(JC["3g"].taken, at(gc, 2, 1))
                        pe.wait_ge(S["3x_full"], at(gc, 2, 1))
                        nc.tensor.matmul(four(bank[:, :]), ident_bf[:, :], mask_gt[:, :].unsqueeze(1).to_broadcast([P, 4, N]), start=True, stop=False)
                        for g in range(G):
                            r = slice(g * N, (g + 1) * N)
                            for c in range(FC):
                                last = nc.tensor.matmul(bank[:, r], c1[:, c, r], c2[:, c, r], start=False, stop=(g, c) == (G - 1, FC - 1))
                        last.then_inc(JC["3s"].full, 1)

                    def p_c():
                        bank = bank_c("3p", 0)
                        pe.wait_ge(*c_bank_free("3p", 0, gc))
                        pe.wait_ge(S["c_norm"], at(gc, 1, 0))
                        transposes(bank, [cz[:, g * N:(g + 1) * N] for g in range(G)]).then_inc(JC["3p"].full, 1)

                    def y_c(b):
                        bank = bank_c("3y", b)
                        pe.wait_ge(*c_bank_free("3y", b, gc))
                        pe.wait_ge(JC["3h"].taken, at(gc, 2, 1))
                        pe.wait_ge(JC["3p"].taken, at(gc, 1, 0))
                        for i in range(2):
                            g = 2 * b + i
                            last = nc.tensor.matmul(bank[:, i * F:(i + 1) * F], cpt[:, g * N:(g + 1) * N], c3[:, g, :], start=True, stop=True)
                        last.then_inc(JC["3y"].full, 1)

                    if with_a:
                        xt(0); xt(1)
                    if with_b:
                        x(1, 0); x(1, 1)
                    if with_a:
                        m1(0); m1(1); m1(2)
                    if with_b:
                        proj(1, 'f', fah_w, 0); nodes(1, l1_w, 0); nodes(1, l1_w, 1)
                    if with_a:
                        m1(3)
                    if with_b:
                        s_l1(0); s_l1(1)
                    if with_c:
                        x_c(0)
                    if with_a:
                        f1(); h1(0)
                    if with_b:
                        p(1, 0); s_l1(2); p(1, 1); s_l1(3)
                    if with_a:
                        h1(1); h1(2)
                    if with_b:
                        p(1, 2)
                    if with_a:
                        h1(3); s1()
                    if with_b:
                        p(1, 3)
                    if with_c:
                        x_c(1)
                    if with_b:
                        v(1, 0); v(1, 1)
                    if with_c:
                        g_c(0); g_c(1)
                    if with_a:
                        p1(0)
                    if with_b:
                        y_l1(0); y_l1(1)
                    if with_a:
                        v1(0); v1(1); v1(2)
                    if with_c:
                        h_c(0)
                    if with_a:
                        v1(3)
                    if with_c:
                        h_c(1)
                    if with_b:
                        x(2, 0); x(2, 1)
                    if with_c:
                        s_c()
                    if with_b:
                        proj(2, 'q', q_w, 0); proj(2, 'q', q_w, 1); proj(2, 'k', k_w, 0); proj(2, 'k', k_w, 1)
                        nodes(2, v_w, 0); nodes(2, v_w, 1); s_l2(0); s_l2(1)
                    if with_a:
                        m2(0); m2(1)
                    if with_b:
                        p(2, 0); s_l2(2); p(2, 1); s_l2(3)
                    if with_a:
                        f2(); h2(0); h2(1); s2()
                    if with_b:
                        p(2, 2)
                    if with_c:
                        p_c()
                    if with_b:
                        p(2, 3)
                    if with_c:
                        y_c(0)
                    if with_b:
                        v(2, 0); v(2, 1)
                    if with_c:
                        y_c(1)
                    if with_a:
                        p1(1); v2(0); v2(1)
                    if with_b:
                        y_l2(0); y_l2(1)
                    if with_a:
                        y0(0); y0(1)
                steps(pe, body)

            @block.scalar
            def _(act):
                def body(ga, gb, gc, with_a, with_b, with_c):
                    def xt(c):
                        bank = bank_a("xt", c)
                        act.wait_ge(JA["xt"].full, at(ga, JA["xt"].n, c))
                        nc.scalar.activation(a_in[0][:, c, :], bank[:, :], ACT.Relu).then_inc(S["a_hi_ready"], 1)

                    def m1(m):
                        bank = bank_a("m1", m)
                        act.wait_ge(JA["m1"].full, at(ga, JA["m1"].n, m))
                        nc.scalar.activation(o1[:, m, :], bank[:, :], ACT.Relu, bias=mlp1_b[:, m:m + 1]).then_inc(JA["m1"].taken, 1)

                    def rows_p(which):
                        bank = bank_a(("f1", "f2")[which], 0)
                        act.wait_ge(JA[("f1", "f2")[which]].full, at(ga, JA[("f1", "f2")[which]].n, 0))
                        nc.scalar.activation(ap[0:2, :], bank[0:2, :], ACT.Identity, bias=row1[0:2, :], scale=row0[0:2, :]) \
                            .then_inc(S["a_p_ready"], 1)

                    def h1(g):
                        bank = bank_a("h1", g)
                        act.wait_ge(JA["h1"].full, at(ga, JA["h1"].n, g))
                        nc.scalar.activation(ah[:, g, :], bank[:, :], ACT.Copy).then_inc(JA["h1"].taken, 1)

                    def scaled(which):
                        bank = bank_a(("s1", "s2")[which], 0)
                        act.wait_ge(JA[("s1", "s2")[which]].full, at(ga, JA[("s1", "s2")[which]].n, 0))
                        nc.scalar.activation(at_, bank[:, :], ACT.Copy, scale=SLOPE).then_inc(S["a_t_ready"], 1)

                    def exp(which):
                        act.wait_ge(S["a_shifted"], at(ga, 2, which))
                        nc.scalar.activation(az[:, :], az[:, :], ACT.Exp).then_inc(S["a_exp"], 1)

                    def pt(which):
                        name = ("p1", "p2")[which]
                        bank = bank_a(name, 0)
                        act.wait_ge(JA[name].full, at(ga, JA[name].n, 0))
                        nc.scalar.activation(apt[:, :], bank[:, :], ACT.Copy).then_inc(JA[name].taken, 1)

                    def e1(which, c):
                        bank = bank_a(("v1", "v2")[which], c)
                        act.wait_ge(JA[("v1", "v2")[which]].full, at(ga, JA[("v1", "v2")[which]].n, c))
                        k = which * HC + c
                        if k >= 2:
                            act.wait_ge(S["a_f"], at(ga, HC + FC, k - 2))
                        nc.scalar.activation(aE[:, k % 2, :], bank[:, :], ACT.Exp).then_inc(S["a_e1"], 1)

                    def e2(which, c):
                        k = which * HC + c
                        act.wait_ge(S["a_u"], at(ga, HC + FC, k))
                        nc.scalar.activation(aE[:, k % 2, :], aE[:, k % 2, :], ACT.Exp, bias=minus1[:, :]).then_inc(S["a_e2"], 1)

                    def v1_hi(c):
                        act.wait_ge(S["a_f"], at(ga, HC + FC, c))
                        nc.scalar.activation(a_mid[0][:, c, :], aF[:, c % 2, :], ACT.Copy).then_inc(S["m1_hi"], 1)

                    def m2(m):
                        bank = bank_a("m2", m)
                        act.wait_ge(JA["m2"].full, at(ga, JA["m2"].n, m))
                        nc.scalar.activation(o2[:, m, :], bank[:, :], ACT.Relu, bias=mlp2_b[:, m:m + 1]).then_inc(JA["m2"].taken, 1)

                    def h2(b):
                        bank = bank_a("h2", b)
                        act.wait_ge(JA["h2"].full, at(ga, JA["h2"].n, b))
                        nc.scalar.activation(ah2[:, 2 * b:2 * b + 2, :].rearrange("p a b -> p (a b)"), bank[:, :], ACT.Copy) \
                            .then_inc(JA["h2"].taken, 1)

                    def x(l, c):
                        bank = bank_b(f"{l}x", c)
                        act.wait_ge(JB[f"{l}x"].full, at(gb, JB[f"{l}x"].n, c))
                        nc.scalar.activation(b_in[0][:, c, :], bank[:, :], ACT.Relu).then_inc(S["b_hi_ready"], 1)

                    def rows_l1():
                        bank = bank_b("1f", 0)
                        act.wait_ge(JB["1f"].full, at(gb, JB["1f"].n, 0))
                        nc.scalar.activation(b1[:, 0, :], bank[:, :], ACT.Identity, bias=row1[:, :], scale=row0[:, :]).then_inc(S["b1_p"], 1)

                    def copy_nodes(b):
                        bank = bank_b("1h", b)
                        act.wait_ge(JB["1h"].full, at(gb, 2, b))
                        nc.scalar.activation(b3[:, 2 * b:2 * b + 2, :].rearrange("p a b -> p (a b)"), bank[:, :], ACT.Copy) \
                            .then_inc(JB["1h"].taken, 1)

                    def b_scaled(g):
                        bank = bank_b("1s", g)
                        act.wait_ge(JB["1s"].full, at(gb, JB["1s"].n, g))
                        if g >= 2:
                            act.wait_ge(JB["1s"].taken, at(gb, G, g - 2))
                        nc.scalar.activation(bt[:, g % 2, :], bank[:, :], ACT.Copy, scale=SLOPE).then_inc(S["b_t_ready"], 1)

                    def b_exp(l, g):
                        k = (l - 1) * G + g
                        if l == 2:
                            act.wait_ge(JB["2s"].taken, at(gb, G, g))
                        else:
                            act.wait_ge(S["b_shifted"], at(gb, G, g))
                        nc.scalar.activation(bz[:, k % 2, :], bz[:, k % 2, :], ACT.Exp).then_inc(S["b_exp"], 1)

                    def b_pt(l, g):
                        bank = bank_b(f"{l}p", g)
                        act.wait_ge(JB[f"{l}p"].full, at(gb, JB[f"{l}p"].n, g))
                        nc.scalar.activation(bpt[:, g, :], bank[:, :], ACT.Copy).then_inc(JB[f"{l}p"].taken, 1)

                    def b_e(c):
                        bank = bank_b("1v", c)
                        act.wait_ge(JB["1v"].full, at(gb, JB["1v"].n, c))
                        if c:
                            act.wait_ge(S["b_full"], at(gb, FC, c - 1))
                        nc.scalar.activation(bE[:, :], bank[:, :], ACT.Exp).then_inc(S["b_e"], 1)

                    def q(m):
                        bank = bank_b("2q", m)
                        act.wait_ge(JB["2q"].full, at(gb, JB["2q"].n, m))
                        nc.scalar.activation(b1[:, m, :], bank[:, :], ACT.Identity, bias=q_b[:, m:m + 1], scale=QK_SCALE).then_inc(JB["2q"].taken, 1)

                    def k(m):
                        bank = bank_b("2k", m)
                        act.wait_ge(JB["2k"].full, at(gb, JB["2k"].n, m))
                        for i in range(2):
                            h = 2 * m + i
                            last = nc.scalar.activation(bpt[:, :, h * N:(h + 1) * N], four(bank[:, :]), ACT.Identity, bias=k_bh[:, m, i:i + 1],
                                                        scale=half[:, i:i + 1])
                        last.then_inc(JB["2k"].taken, 1)

                    def heads_hi(c):
                        bank = bank_b("2v", c)
                        act.wait_ge(JB["2v"].full, at(gb, JB["2v"].n, c))
                        nc.scalar.activation(b_in[0][:, c, :], bank[:, :], ACT.Copy).then_inc(S["2v_hi"], 1)

                    def x_c(c):
                        bank = bank_c("3x", c)
                        act.wait_ge(JC["3x"].full, at(gc, 2, c))
                        nc.scalar.activation(c_in[0][:, c, :], bank[:, :], ACT.Relu).then_inc(S["c_hi_ready"], 1)
                        nc.scalar.activation(c2[:, c, :], bank[:, :], ACT.Relu).then_inc(S["3x_full"], 1)

                    def g_c(m):
                        bank = bank_c("3g", m)
                        act.wait_ge(JC["3g"].full, at(gc, 2, m))
                        nc.scalar.activation(c1[:, m, :], bank[:, :], ACT.Copy).then_inc(JC["3g"].taken, 1)

                    def h_c(b):
                        bank = bank_c("3h", b)
                        act.wait_ge(JC["3h"].full, at(gc, 2, b))
                        nc.scalar.activation(c3[:, 2 * b:2 * b + 2, :].rearrange("p a b -> p (a b)"), bank[:, :], ACT.Copy) \
                            .then_inc(JC["3h"].taken, 1)

                    def scaled_c():
                        act.wait_ge(JC["3s"].full, at(gc, 1, 0))
                        nc.scalar.activation(ct, bank_c("3s", 0)[:, :], ACT.Copy, scale=SLOPE).then_inc(S["c_t_ready"], 1)

                    def exp_c():
                        act.wait_ge(S["c_shifted"], at(gc, 1, 0))
                        nc.scalar.activation(cz, cz, ACT.Exp).then_inc(S["c_exp"], 1)

                    def pt_c():
                        act.wait_ge(JC["3p"].full, at(gc, 1, 0))
                        nc.scalar.activation(cpt, bank_c("3p", 0)[:, :], ACT.Copy).then_inc(JC["3p"].taken, 1)

                    if with_a:
                        xt(0); xt(1)
                    if with_b:
                        x(1, 0); x(1, 1)
                    if with_a:
                        m1(0); m1(1); m1(2)
                    if with_b:
                        rows_l1(); copy_nodes(0); copy_nodes(1)
                    if with_a:
                        m1(3)
                    if with_b:
                        b_scaled(0); b_scaled(1)
                    if with_c:
                        x_c(0)
                    if with_b:
                        b_exp(1, 0)
                    if with_a:
                        rows_p(0)
                    if with_b:
                        b_exp(1, 1)
                    if with_a:
                        h1(0)
                    if with_b:
                        b_pt(1, 0); b_scaled(2); b_pt(1, 1); b_exp(1, 2); b_scaled(3)
                    if with_a:
                        h1(1); h1(2)
                    if with_b:
                        b_exp(1, 3); b_pt(1, 2)
                    if with_a:
                        h1(3); scaled(0)
                    if with_b:
                        b_pt(1, 3)
                    if with_c:
                        x_c(1)
                    if with_b:
                        b_e(0)
                    if with_a:
                        exp(0)
                    if with_b:
                        b_e(1)
                    if with_c:
                        g_c(0); g_c(1)
                    if with_a:
                        pt(0); e1(0, 0); e2(0, 0)
                    if with_c:
                        h_c(0)
                    if with_a:
                        v1_hi(0); e1(0, 1)
                    if with_b:
                        x(2, 0); x(2, 1)
                    if with_c:
                        h_c(1)
                    if with_a:
                        e2(0, 1)
                    if with_c:
                        scaled_c()
                    if with_a:
                        v1_hi(1); e1(0, 2)
                    if with_b:
                        q(0); q(1)
                    if with_a:
                        e2(0, 2)
                    if with_b:
                        k(0)
                    if with_a:
                        v1_hi(2); e1(0, 3)
                    if with_b:
                        k(1)
                    if with_a:
                        e2(0, 3)
                    if with_c:
                        exp_c()
                    if with_a:
                        v1_hi(3)
                    if with_b:
                        b_exp(2, 0)
                    if with_a:
                        m2(0)
                    if with_b:
                        b_exp(2, 1)
                    if with_a:
                        m2(1)
                    if with_b:
                        b_pt(2, 0); b_pt(2, 1); b_exp(2, 2)
                    if with_a:
                        rows_p(1); h2(0)
                    if with_b:
                        b_exp(2, 3)
                    if with_a:
                        h2(1); scaled(1)
                    if with_b:
                        b_pt(2, 2)
                    if with_c:
                        pt_c()
                    if with_b:
                        b_pt(2, 3)
                    if with_a:
                        exp(1)
                    if with_b:
                        heads_hi(0); heads_hi(1)
                    if with_a:
                        pt(1); e1(1, 0); e1(1, 1); e2(1, 0); e2(1, 1)
                steps(act, body)

            @block.vector
            def _(dve):
                def body(ga, gb, gc, with_a, with_b, with_c):
                    def stats(x, st, mv, link):
                        for g in range(G):
                            last = nc.vector.bn_stats(st[:, g, :], x[:, g, :])
                        last.then_inc(link[0], 1)
                        dve.wait_ge(link[0], at(*link[1:]))
                        nc.vector.memset(carrier[:, :], 0.0)
                        for g in range(G):
                            last = nc.vector.bn_aggr(mv[:, g, :], st[:, g, :])
                        return last

                    def normalise(x, xn, mv, rs):
                        for g in range(G):
                            last = nc.vector.tensor_scalar(xn[:, g, :], x[:, g, :], mv[:, g, 0:1], rs[:, g:g + 1], ALU.subtract, ALU.mult)
                        return last

                    def a_stats():
                        dve.wait_ge(S["ax_loaded"], at(ga, 16, 15))
                        stats(ax, a_st, a_mv, (a_link, ga, 1, 0)).then_inc(S["a_var"], 1)

                    def a_normalise():
                        dve.wait_ge(S["a_rstd"], at(ga, 1, 0))
                        normalise(ax, axn, a_mv, a_rs).then_inc(S["axn_ready"], 1)

                    def xt(c):
                        bank = bank_a("xt", c)
                        dve.wait_ge(JA["xt"].full, at(ga, JA["xt"].n, c))
                        dve.wait_ge(S["a_hi_ready"], at(ga, 2, c))
                        nc.vector.scalar_tensor_tensor(out=a_in[1][:, c, :], in0=bank[:, :], scalar=0.0, in1=a_in[0][:, c, :],
                                                       op0=ALU.max, op1=ALU.subtract).then_inc(JA["xt"].taken, 1)

                    def m1(m):
                        dve.wait_ge(JA["m1"].taken, at(ga, HC, m))
                        nc.vector.tensor_copy(a_mid[0][:, m, :], o1[:, m, :]).then_inc(S["m1_hi_d"], 1)
                        dve.wait_ge(S["m1_hi_d"], at(ga, HC + FC, m))
                        nc.vector.tensor_tensor(a_mid[1][:, m, :], o1[:, m, :], a_mid[0][:, m, :], ALU.subtract).then_inc(S["m1_ready"], 1)

                    def rows_q(which):
                        name = ("f1", "f2")[which]
                        bank = bank_a(name, 0)
                        dve.wait_ge(JA[name].full, at(ga, JA[name].n, 0))
                        dve.wait_ge(S["a_p_ready"], at(ga, 2, which))
                        nc.vector.tensor_scalar(aq[0:2, :], bank[0:2, :], row1[0:2, :], row0[0:2, :], ALU.mult, ALU.add) \
                            .then_inc(JA[name].taken, 1)

                    def lrelu(which):
                        name = ("s1", "s2")[which]
                        dve.wait_ge(S["a_t_ready"], at(ga, 2, which))
                        nc.vector.tensor_tensor(az[:, :], bank_a(name, 0)[:, :], at_, ALU.max).then_inc(JA[name].taken, 1)
                        dve.wait_ge(JA[name].taken, at(ga, 1, 0))
                        nc.vector.tensor_reduce(a_max[:, :], four(az[:, :]), AX, ALU.max).then_inc(S["a_z_max"], 1)

                    def total(which):
                        dve.wait_ge(S["a_exp"], at(ga, 2, which))
                        nc.vector.tensor_reduce(a_sum[:, :], four(az[:, :]), AX, ALU.add).then_inc(a_sum_link, 1)
                        dve.wait_ge(a_sum_link, at(ga, 2, which))
                        nc.vector.reciprocal(a_inv[:, :], a_sum[:, :]).then_inc(S["a_inv_ready"], 1)

                    def u(which, c):
                        k = which * HC + c
                        name = ("v1", "v2")[which]
                        dve.wait_ge(S["a_e1"], at(ga, HC + FC, k))
                        nc.vector.tensor_scalar(aE[:, k % 2, :], aE[:, k % 2, :], 1.0, None, ALU.min).then_inc(S["a_u"], 1)
                        res = (o1, o2)[which]
                        nc.vector.scalar_tensor_tensor(out=aR[:, k % 2, :], in0=bank_a(name, c)[:, :], scalar=0.0, in1=res[:, c, :],
                                                       op0=ALU.max, op1=ALU.add).then_inc(JA[name].taken, 1)

                    def out1(c):
                        dve.wait_ge(S["a_e2"], at(ga, HC + FC, c))
                        dve.wait_ge(JA["v1"].taken, at(ga, HC, c))
                        nc.vector.scalar_tensor_tensor(out=aF[:, c % 2, :], in0=aE[:, c % 2, :], scalar=-1.0, in1=aR[:, c % 2, :],
                                                       op0=ALU.add, op1=ALU.add).then_inc(S["a_f"], 1)

                    def out1_lo(c):
                        dve.wait_ge(S["m1_hi"], at(ga, HC, c))
                        nc.vector.tensor_tensor(a_mid[1][:, c, :], aF[:, c % 2, :], a_mid[0][:, c, :], ALU.subtract).then_inc(S["v1_hi"], 1)

                    def m2(m):
                        dve.wait_ge(JA["m2"].taken, at(ga, FC, m))
                        nc.vector.tensor_copy(a_in[0][:, m, :], o2[:, m, :]).then_inc(S["m1_hi_d"], 1)
                        dve.wait_ge(S["m1_hi_d"], at(ga, HC + FC, HC + m))
                        nc.vector.tensor_tensor(a_in[1][:, m, :], o2[:, m, :], a_in[0][:, m, :], ALU.subtract).then_inc(S["m2_ready"], 1)

                    def out2(c):
                        k = HC + c
                        dve.wait_ge(S["a_e2"], at(ga, HC + FC, k))
                        dve.wait_ge(JA["v2"].taken, at(ga, FC, c))
                        nc.vector.scalar_tensor_tensor(out=ay[:, c, :], in0=aE[:, k % 2, :], scalar=-1.0, in1=aR[:, k % 2, :],
                                                       op0=ALU.add, op1=ALU.add).then_inc(S["a_f"], 1)

                    def y0(b):
                        bank = bank_a("y0", b)
                        dve.wait_ge(JA["y0"].full, at(ga, JA["y0"].n, b))
                        if b == 0:
                            dve.wait_ge(S["x1_loaded"], at(ga, 16, 15))
                        nc.vector.scalar_tensor_tensor(out=x1[:, 2 * b:2 * b + 2, :].rearrange("p a b -> p (a b)"), in0=bank[:, :], scalar=0.0,
                                                       in1=x1[:, 2 * b:2 * b + 2, :].rearrange("p a b -> p (a b)"),
                                                       op0=ALU.max, op1=ALU.add).then_inc(JA["y0"].taken, 1)

                    def b_stats(l):
                        x = x1 if l == 1 else bx
                        if l == 1:
                            dve.wait_ge(JA["y0"].taken, at(gb, 2, 1))
                        else:
                            name = f"{l - 1}y"
                            dve.wait_ge(JB[name].taken, at(gb, 2, 1))
                        stats(x, b_st, b_mv, (b_link, gb, 2, l - 1)).then_inc(S["b_var"], 1)

                    def b_normalise(l):
                        dve.wait_ge(S["b_rstd"], at(gb, 2, l - 1))
                        normalise(x1 if l == 1 else bx, bxn, b_mv, b_rs).then_inc(S["bxn_ready"], 1)

                    def x(l, c):
                        bank = bank_b(f"{l}x", c)
                        dve.wait_ge(JB[f"{l}x"].full, at(gb, JB[f"{l}x"].n, c))
                        dve.wait_ge(S["b_hi_ready"], at(gb, 4, 2 * (l - 1) + c))
                        nc.vector.scalar_tensor_tensor(out=b_in[1][:, c, :], in0=bank[:, :], scalar=0.0, in1=b_in[0][:, c, :],
                                                       op0=ALU.max, op1=ALU.subtract).then_inc(JB[f"{l}x"].taken, 1)

                    def rows_l1():
                        bank = bank_b("1f", 0)
                        dve.wait_ge(JB["1f"].full, at(gb, JB["1f"].n, 0))
                        dve.wait_ge(S["b1_p"], at(gb, 1, 0))
                        for h in range(HEADS):
                            last = nc.vector.tensor_scalar(bpt[:, :, h * N:(h + 1) * N], four(bank[:, :]), ident[:, 32 * h + 1:32 * h + 2],
                                                           ident[:, 32 * h:32 * h + 1], ALU.mult, ALU.add)
                        last.then_inc(JB["1f"].taken, 1)

                    def b_lrelu(g):
                        dve.wait_ge(S["b_t_ready"], at(gb, G, g))
                        z_free(1, g)
                        nc.vector.tensor_tensor(bz[:, g % 2, :], bank_b("1s", g)[:, :], bt[:, g % 2, :], ALU.max).then_inc(JB["1s"].taken, 1)
                        dve.wait_ge(JB["1s"].taken, at(gb, JB["1s"].n, g))
                        nc.vector.tensor_reduce(b_max[:, g % 2, :], four(bz[:, g % 2, :]), AX, ALU.max).then_inc(S["b_z_max"], 1)

                    def z_free(l, g):
                        if g >= 2:
                            dve.wait_ge(JB[f"{l}p"].full, at(gb, G, g - 2))

                    def b_max2(g):
                        k = G + g
                        bank = bank_b("2s", g)
                        dve.wait_ge(JB["2s"].full, at(gb, JB["2s"].n, g))
                        z_free(2, g)
                        nc.vector.tensor_reduce(b_max[:, k % 2, :], four(bank[:, :]), AX, ALU.max).then_inc(max_link, 1)
                        dve.wait_ge(max_link, at(gb, G, g))
                        nc.vector.tensor_tensor(four(bz[:, k % 2, :]), four(bank[:, :]), b_max[:, k % 2, :].unsqueeze(2).to_broadcast([P, 4, N]),
                                                ALU.subtract).then_inc(JB["2s"].taken, 1)

                    def b_total(l, g):
                        k = (l - 1) * G + g
                        dve.wait_ge(S["b_exp"], at(gb, 2 * G, k))
                        nc.vector.tensor_reduce(b_sum[:, k % 2, :], four(bz[:, k % 2, :]), AX, ALU.add).then_inc(b_sum_link, 1)
                        dve.wait_ge(b_sum_link, at(gb, 2 * G, k))
                        i = nc.vector.reciprocal(b_inv[:, k % 2, :], b_sum[:, k % 2, :])
                        if l == 2:
                            i.then_inc(b_edge_link, 1)
                            dve.wait_ge(b_edge_link, at(gb, G, g))
                            i = nc.vector.tensor_scalar(b_inv[:, k % 2, :], b_inv[:, k % 2, :], has_edge[:, :], None, ALU.mult)
                        i.then_inc(S["b_inv_ready"], 1)

                    def elu(c):
                        bank = bank_b("1v", c)
                        dve.wait_ge(JB["1v"].full, at(gb, JB["1v"].n, c))
                        dve.wait_ge(S["b_e"], at(gb, FC, c))
                        nc.vector.tensor_scalar(bR[:, :], bank[:, :], 0.0, -1.0, ALU.max, ALU.add).then_inc(JB["1v"].taken, 1)
                        dve.wait_ge(JB["1v"].taken, at(gb, FC, c))
                        nc.vector.scalar_tensor_tensor(out=b2[:, c, :], in0=bE[:, :], scalar=1.0, in1=bR[:, :],
                                                       op0=ALU.min, op1=ALU.add).then_inc(S["b_full"], 1)

                    def y_l1(b):
                        bank = bank_b("1y", b)
                        dve.wait_ge(JB["1y"].full, at(gb, JB["1y"].n, b))
                        r = slice(2 * b, 2 * b + 2)
                        nc.vector.tensor_tensor(bx[:, r, :].rearrange("p a b -> p (a b)"), bank[:, :], x1[:, r, :].rearrange("p a b -> p (a b)"),
                                                ALU.add).then_inc(JB["1y"].taken, 1)

                    def v_bias(b):
                        bank = bank_b("2h", b)
                        dve.wait_ge(JB["2h"].full, at(gb, JB["2h"].n, b))
                        nc.vector.tensor_tensor(b3[:, 2 * b:2 * b + 2, :], bank[:, :].rearrange("p (a b) -> p a b", a=2),
                                                v_b[:, :].unsqueeze(1).to_broadcast([P, 2, F]), ALU.add).then_inc(JB["2h"].taken, 1)

                    def heads_lo(c):
                        bank = bank_b("2v", c)
                        dve.wait_ge(S["2v_hi"], at(gb, 2, c))
                        nc.vector.tensor_tensor(b_in[1][:, c, :], bank[:, :], b_in[0][:, c, :], ALU.subtract).then_inc(JB["2v"].taken, 1)

                    def y_l2(b):
                        bank = bank_b("2y", b)
                        dve.wait_ge(JB["2y"].full, at(gb, JB["2y"].n, b))
                        r = slice(2 * b, 2 * b + 2)
                        if b == 0:
                            dve.wait_ge(S["bx_bias"], at(gb, 1, 0))
                            dve.wait_ge(S["out_stored"], 16 * gb)
                        nc.vector.tensor_tensor(cx[:, r, :].rearrange("p a b -> p (a b)"), bank[:, :],
                                                bx[:, r, :].rearrange("p a b -> p (a b)"), ALU.add).then_inc(JB["2y"].taken, 1)

                    def stats_c():
                        dve.wait_ge(JB["2y"].taken, at(gc, 2, 1))
                        stats(cx, c_st, c_mv, (c_link, gc, 1, 0)).then_inc(S["c_var"], 1)

                    def normalise_c():
                        dve.wait_ge(S["c_rstd"], at(gc, 1, 0))
                        normalise(cx, cxn, c_mv, c_rs).then_inc(S["cxn_ready"], 1)

                    def x_c(c):
                        bank = bank_c("3x", c)
                        dve.wait_ge(S["3x_full"], at(gc, 2, c))
                        nc.vector.scalar_tensor_tensor(out=c_in[1][:, c, :], in0=bank[:, :], scalar=0.0, in1=c_in[0][:, c, :],
                                                       op0=ALU.max, op1=ALU.subtract).then_inc(JC["3x"].taken, 1)

                    def lrelu_c():
                        dve.wait_ge(S["c_t_ready"], at(gc, 1, 0))
                        nc.vector.tensor_tensor(cz, bank_c("3s", 0)[:, :], ct, ALU.max).then_inc(JC["3s"].taken, 1)
                        dve.wait_ge(JC["3s"].taken, at(gc, 1, 0))
                        nc.vector.tensor_reduce(c_max[:, :], four(cz), AX, ALU.max).then_inc(S["c_z_max"], 1)

                    def total_c():
                        dve.wait_ge(S["c_exp"], at(gc, 1, 0))
                        nc.vector.tensor_reduce(c_sum[:, :], four(cz), AX, ALU.add).then_inc(c_sum_link, 1)
                        dve.wait_ge(c_sum_link, at(gc, 1, 0))
                        nc.vector.reciprocal(c_inv[:, :], c_sum[:, :]).then_inc(S["c_inv_ready"], 1)

                    def y_c(b):
                        bank = bank_c("3y", b)
                        dve.wait_ge(JC["3y"].full, at(gc, JC["3y"].n, b))
                        r = slice(2 * b, 2 * b + 2)
                        nc.vector.scalar_tensor_tensor(out=cx[:, r, :].rearrange("p a b -> p (a b)"), in0=bank[:, :], scalar=0.0,
                                                       in1=cx[:, r, :].rearrange("p a b -> p (a b)"), op0=ALU.max, op1=ALU.add) \
                            .then_inc(JC["3y"].taken, 1)

                    if with_a:
                        a_stats()
                    if with_b:
                        b_stats(1)
                    if with_a:
                        a_normalise()
                    if with_b:
                        b_normalise(1)
                    if with_a:
                        xt(0); xt(1)
                    if with_b:
                        x(1, 0)
                    if with_c:
                        stats_c()
                    if with_b:
                        x(1, 1)
                    if with_c:
                        normalise_c()
                    if with_a:
                        m1(0); m1(1)
                    if with_b:
                        rows_l1()
                    if with_a:
                        m1(2); m1(3)
                    if with_b:
                        b_lrelu(0); b_lrelu(1)
                    if with_c:
                        x_c(0)
                    if with_b:
                        b_total(1, 0)
                    if with_a:
                        rows_q(0)
                    if with_b:
                        b_total(1, 1); b_lrelu(2); b_total(1, 2); b_lrelu(3); b_total(1, 3)
                    if with_a:
                        lrelu(0)
                    if with_c:
                        x_c(1)
                    if with_b:
                        elu(0)
                    if with_a:
                        total(0)
                    if with_b:
                        elu(1); y_l1(0); y_l1(1); b_stats(2)
                    if with_a:
                        u(0, 0)
                    if with_b:
                        b_normalise(2)
                    if with_a:
                        out1(0); u(0, 1)
                    if with_b:
                        x(2, 0); x(2, 1)
                    if with_a:
                        out1(1); out1_lo(0)
                    if with_c:
                        lrelu_c()
                    if with_a:
                        u(0, 2); out1(2); out1_lo(1); u(0, 3)
                    if with_b:
                        v_bias(0)
                    if with_a:
                        out1(3); out1_lo(2); out1_lo(3)
                    if with_b:
                        v_bias(1); b_max2(0); b_max2(1); b_total(2, 0); b_total(2, 1)
                    if with_a:
                        m2(0); m2(1)
                    if with_b:
                        b_max2(2)
                    if with_c:
                        total_c()
                    if with_b:
                        b_total(2, 2); b_max2(3)
                    if with_a:
                        rows_q(1)
                    if with_b:
                        b_total(2, 3)
                    if with_a:
                        lrelu(1)
                    if with_c:
                        y_c(0)
                    if with_a:
                        total(1)
                    if with_b:
                        heads_lo(0)
                    if with_c:
                        y_c(1)
                    if with_b:
                        heads_lo(1)
                    if with_a:
                        u(1, 0); u(1, 1)
                    if with_b:
                        y_l2(0)
                    if with_a:
                        out2(0); out2(1)
                    if with_b:
                        y_l2(1)
                    if with_a:
                        y0(0); y0(1)
                steps(dve, body)

            @block.gpsimd
            def _(pool):
                def body(ga, gb, gc, with_a, with_b, with_c):
                    def rstd(mv, ve, rs, link):
                        nc.gpsimd.tensor_tensor(ve[:, :], mv[:, :, 1], eps_t[:, :], ALU.add).then_inc(link[0], 1)
                        pool.wait_ge(link[0], at(*link[1:]))
                        return nc.gpsimd.tensor_tensor(rs[:, :], ve[:, :], pow_t[:, :], ALU.pow)

                    def a_rstd():
                        pool.wait_ge(S["a_var"], at(ga, 1, 0))
                        rstd(a_mv, a_ve, a_rs, (a_ve_link, ga, 1, 0)).then_inc(S["a_rstd"], 1)

                    def b_rstd(l):
                        pool.wait_ge(S["b_var"], at(gb, 2, l - 1))
                        rstd(b_mv, b_ve, b_rs, (b_ve_link, gb, 2, l - 1)).then_inc(S["b_rstd"], 1)

                    def shift(which):
                        pool.wait_ge(S["a_z_max"], at(ga, 2, which))
                        nc.gpsimd.tensor_tensor(four(az[:, :]), four(az[:, :]), a_max[:, :].unsqueeze(2).to_broadcast([P, 4, N]), ALU.subtract) \
                            .then_inc(S["a_shifted"], 1)

                    def norm(which):
                        pool.wait_ge(S["a_inv_ready"], at(ga, 2, which))
                        nc.gpsimd.tensor_tensor(four(az[:, :]), four(az[:, :]), a_inv[:, :].unsqueeze(2).to_broadcast([P, 4, N]), ALU.mult) \
                            .then_inc(S["a_norm"], 1)

                    def b_shift(g):
                        pool.wait_ge(S["b_z_max"], at(gb, G, g))
                        z = four(bz[:, g % 2, :])
                        nc.gpsimd.tensor_tensor(z, z, b_max[:, g % 2, :].unsqueeze(2).to_broadcast([P, 4, N]), ALU.subtract) \
                            .then_inc(S["b_shifted"], 1)

                    def b_norm(l, g):
                        k = (l - 1) * G + g
                        pool.wait_ge(S["b_inv_ready"], at(gb, 2 * G, k))
                        z = four(bz[:, k % 2, :])
                        nc.gpsimd.tensor_tensor(z, z, b_inv[:, k % 2, :].unsqueeze(2).to_broadcast([P, 4, N]), ALU.mult) \
                            .then_inc(S["b_norm"], 1)

                    def out_bias():
                        pool.wait_ge(S["bxn_ready"], at(gb, 2, 1))
                        nc.gpsimd.tensor_tensor(bx[:, :, :], bx[:, :, :], o_b[:, :].unsqueeze(1).to_broadcast([P, G, F]), ALU.add) \
                            .then_inc(S["bx_bias"], 1)

                    def rstd_c():
                        pool.wait_ge(S["c_var"], at(gc, 1, 0))
                        rstd(c_mv, c_ve, c_rs, (c_ve_link, gc, 1, 0)).then_inc(S["c_rstd"], 1)

                    def shift_c():
                        pool.wait_ge(S["c_z_max"], at(gc, 1, 0))
                        nc.gpsimd.tensor_tensor(four(cz), four(cz), c_max[:, :].unsqueeze(2).to_broadcast([P, 4, N]), ALU.subtract) \
                            .then_inc(S["c_shifted"], 1)

                    def norm_c():
                        pool.wait_ge(S["c_inv_ready"], at(gc, 1, 0))
                        nc.gpsimd.tensor_tensor(four(cz), four(cz), c_inv[:, :].unsqueeze(2).to_broadcast([P, 4, N]), ALU.mult) \
                            .then_inc(S["c_norm"], 1)

                    if with_a:
                        a_rstd()
                    if with_b:
                        b_rstd(1)
                    if with_c:
                        rstd_c()
                    if with_b:
                        b_shift(0); b_shift(1); b_norm(1, 0); b_norm(1, 1); b_shift(2); b_norm(1, 2)
                        b_shift(3); b_norm(1, 3)
                    if with_a:
                        shift(0); norm(0)
                    if with_b:
                        b_rstd(2); out_bias()
                    if with_c:
                        shift_c()
                    if with_b:
                        b_norm(2, 0); b_norm(2, 1)
                    if with_c:
                        norm_c()
                    if with_b:
                        b_norm(2, 2); b_norm(2, 3)
                    if with_a:
                        shift(1); norm(1)
                steps(pool, body)


_OUT_SHAPE = (128, 128, 256)


def kernel(**inputs):
    import numpy as np
    import concourse.bacc as bacc
    from concourse.bass_utils import run_bass_kernel_spmd as run

    heads, feats, hd = inputs["L1_gnn_W"].shape
    a = np.asarray(inputs["L1_gnn_a"])
    a_blocks = np.zeros((heads, hd, heads, 2), a.dtype)
    for h in range(heads):
        a_blocks[h, :, h, 0] = a[h, :hd]
        a_blocks[h, :, h, 1] = a[h, hd:]

    def pair(v):
        v = np.asarray(v)
        return v.reshape(2, -1).T

    def t(name):
        return np.asarray(inputs[name]).T

    l1 = np.asarray(inputs["L1_gnn_W"])
    arrays = {
        "x": inputs["x"], "adj": inputs["adj"],
        "w_mlp1": inputs["L0_gnn_mlp1_w"], "b_mlp1": inputs["L0_gnn_mlp1_b"],
        "w_mlp2": inputs["L0_gnn_mlp2_w"], "b_mlp2": inputs["L0_gnn_mlp2_b"],
        "w_fc": inputs["L0_gnn_W_fc"], "w_fcT": t("L0_gnn_W_fc"), "a_fc": pair(inputs["L0_gnn_a_fc"]),
        "w_hand": inputs["L0_gnn_W_hand"], "w_handT": t("L0_gnn_W_hand"), "a_hand": pair(inputs["L0_gnn_a_hand"]),
        "w_l1": l1.transpose(1, 0, 2).reshape(feats, heads * hd), "w_l1T": l1.transpose(0, 2, 1).reshape(heads * hd, feats),
        "a_l1": a_blocks.reshape(heads * hd, 2 * heads),
        "w_q": t("L2_gnn_wq"), "b_q": inputs["L2_gnn_bq"], "w_k": t("L2_gnn_wk"), "b_k": inputs["L2_gnn_bk"],
        "w_v": t("L2_gnn_wv"), "b_v": inputs["L2_gnn_bv"], "w_o": t("L2_gnn_wo"), "b_o": inputs["L2_gnn_bo"],
        "w_1T": t("L3_gnn_W1"), "w_2T": t("L3_gnn_W2"), "w_h3": inputs["L3_gnn_W3"],
    }
    arrays = {k: np.ascontiguousarray(v) for k, v in arrays.items()}
    nc = bacc.Bacc("TRN2", target_bir_lowering=False, num_devices=1)
    ins = {k: nc.dram_tensor("in_" + k, v.shape, mybir.dt.from_np(v.dtype), kind="ExternalInput").ap() for k, v in arrays.items()}
    out = nc.dram_tensor("out_0", _OUT_SHAPE, mybir.dt.float32, kind="ExternalOutput").ap()
    gnn_stack_kernel(nc, ins, out)
    r = run(nc, [{"in_" + k: v for k, v in arrays.items()}], core_ids=[0])
    return r.results[0]["out_0"]
```

```python
from contextlib import ExitStack

import concourse.bass as bass
from concourse import mybir


def gnn_stack_kernel(nc, ins, out):
    f32, f32r, bf16, i32 = mybir.dt.float32, mybir.dt.float32r, mybir.dt.bfloat16, mybir.dt.int32
    ALU, ACT, AX = mybir.AluOpType, mybir.ActivationFunctionType, mybir.AxisListType.X

    B, N, F = ins["x"].shape
    HID = ins["w_mlp1"].shape[1]
    HEADS = 4
    HD = F // HEADS
    G = 4
    T = G * N
    NT = B // G
    P = 128
    FC, HC = F // P, HID // P
    GP = G // 2
    EPS, SLOPE, MASKED = 1e-5, 0.2, -9.0e15
    QK_SCALE = float(HD) ** -0.5
    X_GROUPS = ins["x"].rearrange("(t g) n f -> t n g f", g=G)
    OUT_GROUPS = out.rearrange("(t g) n f -> t n g f", g=G)

    ctx = ExitStack()
    with ctx:
        def sb(name, shape, dt=f32):
            return ctx.enter_context(nc.sbuf_tensor(name, shape, dt))

        def sem(name):
            return ctx.enter_context(nc.semaphore(name))

        def split(name, chunks, cols):
            return sb(name + "_hi", [P, chunks, cols], f32r), sb(name + "_lo", [P, chunks, cols], f32r)

        mlp1_w, fc_w = split("mlp1_w", FC, HID), split("fc_w", HC, HID)
        mlp2_w, hand_w = split("mlp2_w", HC, F), split("hand_w", FC, F)
        l1_w, q_w, k_w, v_w, o_w = (split(n, FC, F) for n in ("l1_w", "q_w", "k_w", "v_w", "o_w"))
        bil_w, h3_w = split("bil_w", FC, F), split("h3_w", FC, F)
        fa1_w, fa2_w, fah_w = sb("fa1_w", [P, HC, P], f32r), sb("fa2_w", [P, FC, P], f32r), sb("fah_w", [P, FC, P], f32r)

        ident = sb("ident", [P, P])
        ident_bf = sb("ident_bf", [P, P], bf16)
        mask_gt = sb("mask_gt", [P, N], bf16)
        mask_ne = sb("mask_ne", [P, N], bf16)
        has_edge = sb("has_edge", [P, 1])
        row0, row1 = sb("row0", [P, 1]), sb("row1", [P, 1])
        head0, head1 = sb("head0", [P, HEADS]), sb("head1", [P, HEADS])
        neg_lo = sb("neg_lo", [P, 1])
        row0_s, head1_s = sb("row0_s", [P, 1]), sb("head1_s", [P, HEADS])
        mlp1_b, mlp2_b = sb("mlp1_b", [P, HC]), sb("mlp2_b", [P, FC])
        q_b, k_b = sb("q_b", [P, FC]), sb("k_b", [P, FC])
        half, k_bh = sb("half", [P, 2]), sb("k_bh", [P, FC, 2])
        v_b, o_b = sb("v_b", [P, F]), sb("o_b", [P, F])
        minus1, carrier = sb("minus1", [P, 1]), sb("carrier", [P, 1])
        eps_t, pow_t = sb("eps_t", [P, G]), sb("pow_t", [P, G])

        ax = sb("ax", [P, G, F])
        a_in = sb("a_in_hi", [P, FC, T], f32r), sb("a_in_lo", [P, FC, T], f32r)
        a_mid = sb("a_mid_hi", [P, HC, T], f32r), sb("a_mid_lo", [P, HC, T], f32r)
        o1 = sb("o1", [P, HC, T])
        o2 = o1
        ah = sb("ah", [P, G, HID])
        ay = ah[:, 0:FC, :]
        az, apt = sb("az", [P, T]), sb("apt", [P, T])
        aE, aR, aF = sb("aE", [P, 2, T]), sb("aR", [P, 2, T]), sb("aF", [P, 2, T])
        at_ = aE[:, 0, :]
        ap, aq = aR[:, 0, :], aR[:, 1, :]
        axn = ah2 = aF[:, :, :].rearrange("p a (b f) -> p (a b) f", f=F)
        a_st, a_mv = sb("a_st", [P, G, 6]), sb("a_mv", [P, G, 2])
        a_ve, a_rs = sb("a_ve", [P, G]), sb("a_rs", [P, G])
        a_max, a_sum, a_inv = sb("a_max", [P, G]), sb("a_sum", [P, G]), sb("a_inv", [P, G])
        x1 = sb("x1", [P, G, F])
        bx = sb("bx", [P, G, F])
        bq = sb("b_in_hi_lo", [P, 2 * FC, T], f32r)
        b_in = bq[:, 0:FC, :], bq[:, FC:2 * FC, :]
        bf = sb("bf", [P, T], f32r)
        bX = bq[:, :, (HEADS - 1) * N:HEADS * N]
        b1, b3 = sb("b1", [P, 2, T]), sb("b3", [P, G, F])
        bxn = b3
        bt, bz, bpt = sb("bt", [P, 2, T]), sb("bz", [P, 4, T]), sb("bpt", [P, G, T])
        b_st, b_mv = sb("b_st", [P, G, 6]), sb("b_mv", [P, G, 2])
        b_ve, b_rs = sb("b_ve", [P, G]), sb("b_rs", [P, G])
        b_max, b_sum, b_inv = sb("b_max", [P, 4, 4]), sb("b_sum", [P, 4, 4]), sb("b_inv", [P, 4, 4])
        cx = sb("cx", [P, G, F])
        c_in = sb("c_in_hi", [P, FC, T], f32r), sb("c_in_lo", [P, FC, T], f32r)
        c1, c2, c3 = sb("c1", [P, 2, T]), sb("c2", [P, 2, T]), sb("c3", [P, G, F])
        cxn = c3
        ct, cz, cpt = c2[:, 0, :], c2[:, 1, :], c1[:, 0, :]
        c_st, c_mv = sb("c_st", [P, G, 6]), sb("c_mv", [P, G, 2])
        c_ve, c_rs = sb("c_ve", [P, G]), sb("c_rs", [P, G])
        c_max, c_sum, c_inv = sb("c_max", [P, G]), sb("c_sum", [P, G]), sb("c_inv", [P, G])

        banks = [ctx.enter_context(nc.psum_tensor(f"bank{i}", [P, T], f32)) for i in range(8)]

        names = ("ax_loaded x1_loaded a_var a_rstd axn_ready a_hi_ready m1_ready out1_hi m2_ready "
                 "a_p_ready a_t_ready a_z_max a_shifted a_exp a_inv_ready a_norm a_e1 a_e2 a_u a_f out1_split "
                 "b_var b_rstd bxn_ready b_hi_ready b_t_ready b_z_max b_shifted b_exp b_inv_ready b_norm "
                 "f_hi rows_act rows_ready x1_less_1 b_e b_full bx_bias 2v_hi "
                 "c_var c_rstd cxn_ready c_hi_ready 3x_full c_t_ready c_z_max c_shifted c_exp c_inv_ready c_norm out_stored").split()
        S = {n: sem("s_" + n) for n in names}

        s_const, s_hi, s_id, s_products, s_folded = (sem(n) for n in ("s_const", "s_hi", "s_id", "s_products", "s_folded"))

        def flat(tile):
            return tile[:, :, :].rearrange("p a b -> p (a b)")

        def chunks(ap, c):
            return ap.rearrange("p (c n) -> p c n", c=c)

        half_row = FC * F
        w_plan = [("w_mlp1", mlp1_w, flat(bx)), ("w_fc", fc_w, flat(o1)), ("w_mlp2", mlp2_w, flat(cx)),
                  ("w_hand", hand_w, flat(b3)[:, 0:half_row]), ("w_l1", l1_w, flat(b3)[:, half_row:]),
                  ("w_q", q_w, flat(c1)[:, 0:half_row]), ("w_k", k_w, flat(c1)[:, half_row:]),
                  ("w_v", v_w, flat(c2)[:, 0:half_row]), ("w_o", o_w, flat(c2)[:, half_row:]), ("w_h3", h3_w, flat(x1)[:, 0:half_row])]
        w_plan = [(name, w, st, sem("s_" + name)) for name, w, st in w_plan]
        small = flat(c3)
        f_plan = [("w_fcT", flat(ah), "a_fc", small[:, 0:HC * 2], fa1_w, HC, HC, 2, banks[0:4]),
                  ("w_handT", flat(bpt)[:, 0:half_row], "a_hand", small[:, 16:16 + FC * 2], fa2_w, FC, FC, 2, banks[4:6]),
                  ("w_l1T", flat(bpt)[:, half_row:2 * half_row], "a_l1", small[:, 32:32 + FC * 2 * HEADS], fah_w, FC, FC, 2 * HEADS, banks[6:8]),
                  ("w_1T", flat(bpt)[:, 2 * half_row:3 * half_row], "w_2T", flat(bpt)[:, 3 * half_row:4 * half_row], bil_w, FC, FC, F, banks[0:2])]
        f_plan = [plan + (sem("s_" + plan[0]),) for plan in f_plan]
        adj_i = az[:, 0:N].bitcast(i32)
        with nc.Block() as block:
            @block.sync
            def _(sp):
                consts = [(adj_i, ins["adj"]),
                          (mlp1_b[:, :], ins["b_mlp1"].rearrange("(c p) -> p c", p=P)),
                          (mlp2_b[:, :], ins["b_mlp2"].rearrange("(c p) -> p c", p=P)),
                          (q_b[:, :], ins["b_q"].rearrange("(c p) -> p c", p=P)),
                          (k_b[:, :], ins["b_k"].rearrange("(c p) -> p c", p=P)),
                          (v_b[:, :], ins["b_v"].rearrange("(a f) -> a f", a=1).to_broadcast([P, F])),
                          (o_b[:, :], ins["b_o"].rearrange("(a f) -> a f", a=1).to_broadcast([P, F]))]
                with nc.allow_non_contiguous_dma("small vectors, once"):
                    for name, w, st, loaded in w_plan[0:2]:
                        sp.dma_start(chunks(st, w[0].shape[1]), ins[name].rearrange("(c p) n -> p c n", p=P)).then_inc(loaded, 16)
                    for left, left_st, right, right_st, w, kc, dc, n, bank, loaded in f_plan:
                        sp.dma_start(chunks(right_st, dc), ins[right].rearrange("(c p) n -> p c n", p=P)).then_inc(loaded, 16)
                        sp.dma_start(chunks(left_st, dc), ins[left].rearrange("(c p) n -> p c n", p=P)).then_inc(loaded, 16)
                    for dst, src in consts:
                        sp.dma_start(dst, src).then_inc(s_const, 16)
                    for name, w, st, loaded in w_plan[2:]:
                        sp.dma_start(chunks(st, w[0].shape[1]), ins[name].rearrange("(c p) n -> p c n", p=P)).then_inc(loaded, 16)
                sp.dma_start(ax[:, :, :], X_GROUPS[0]).then_inc(S["ax_loaded"], 16)

            @block.gpsimd
            def _(pool):
                nc.gpsimd.memset(ident[:, :], 0.0).then_inc(s_id, 1)
                pool.wait_ge(s_id, 1)
                nc.gpsimd.affine_select(out=ident[:, :], in_=ident[:, :], compare_op=ALU.not_equal, fill=1.0,
                                        base=0, pattern=[[-1, P]], channel_multiplier=1).then_inc(s_id, 1)
                nc.gpsimd.memset(minus1[:, :], -1.0)
                nc.gpsimd.memset(eps_t[:, :], EPS)
                nc.gpsimd.memset(pow_t[:, :], -0.5)

            @block.tensor
            def _(pe):
                for j, (left, left_st, right, right_st, w, kc, dc, n, bank, loaded) in enumerate(f_plan):
                    pe.wait_ge(loaded, 32)
                    if bank[0] is banks[0] and j:
                        pe.wait_ge(s_folded, 1)
                    for k in range(kc):
                        for d in range(dc):
                            last = nc.tensor.matmul(bank[k][:, 0:n], chunks(left_st, dc)[:, d, k * P:(k + 1) * P], chunks(right_st, dc)[:, d, :],
                                                    start=d == 0, stop=d == dc - 1)
                    last.then_inc(s_products, 1)

            @block.scalar
            def _(act):
                for name, w, st, loaded in w_plan:
                    act.wait_ge(loaded, 16)
                    nc.scalar.activation(w[0][:, :, :], chunks(st, w[0].shape[1]), ACT.Copy).then_inc(s_hi, 1)

            @block.vector
            def _(dve):
                links = sem("s_setup_links")
                done = [0]

                def link(i):
                    done[0] += 1
                    i.then_inc(links, 1)
                    dve.wait_ge(links, done[0])

                def lo_parts(first, last):
                    for i in range(first, last):
                        name, w, st, loaded = w_plan[i]
                        dve.wait_ge(s_hi, i + 1)
                        nc.vector.tensor_tensor(w[1][:, :, :], chunks(st, w[0].shape[1]), w[0][:, :, :], ALU.subtract)

                link(nc.vector.memset(at_, 0.0))
                for w in (fa1_w, fa2_w, fah_w):
                    c = w.shape[1]
                    link(nc.vector.tensor_copy(w[:, :, :], at_[:, 0:c * P].rearrange("p (c n) -> p c n", c=c)))
                lo_parts(0, 2)
                for j, (left, left_st, right, right_st, w, kc, dc, n, bank, loaded) in enumerate(f_plan):
                    dve.wait_ge(s_products, j + 1)
                    for k in range(kc):
                        if n == 2:
                            src = bank[k][:, 0:2]
                            hi, lo = w[:, k, 0:2], w[:, k, 2:4]
                        elif n == F:
                            src = bank[k][:, 0:F]
                            hi, lo = (part[:, k, :] for part in w)
                        else:
                            src = bank[k][:, 0:n].rearrange("p (h x) -> p h x", x=2)
                            rows = w[:, k, :].rearrange("p (h x) -> p h x", h=HEADS)
                            hi, lo = rows[:, :, 0:2], rows[:, :, 4:6]
                        link(nc.vector.tensor_copy(hi, src))
                        if w is fah_w:
                            link(nc.vector.tensor_copy(rows[:, :, 2:4], src))
                        last = nc.vector.tensor_tensor(lo, src, hi, ALU.subtract)
                    last.then_inc(s_folded, 1)
                dve.wait_ge(s_id, 2)
                nc.vector.tensor_copy(ident_bf[:, :], ident[:, :])
                by_head = ident[:, :].rearrange("p (h x) -> p h x", h=HEADS)
                nc.vector.tensor_reduce(head0[:, :], by_head[:, :, 0:6:2], AX, ALU.add)
                nc.vector.tensor_reduce(head1[:, :], by_head[:, :, 1:6:2], AX, ALU.add)
                nc.vector.tensor_reduce(neg_lo[:, :], by_head[:, :, 2:4], mybir.AxisListType.XY, ALU.add)
                link(nc.vector.tensor_scalar(head1_s[:, :], by_head[:, :, 3], 2.0, None, ALU.mult))
                nc.vector.tensor_reduce(row0[:, :], head0[:, :], AX, ALU.add)
                nc.vector.tensor_reduce(row1[:, :], head1[:, :], AX, ALU.add)
                nc.vector.tensor_tensor(head1_s[:, :], head1[:, :], head1_s[:, :], ALU.subtract)
                link(nc.vector.tensor_reduce(row0_s[:, :], by_head[:, :, 2], AX, ALU.add))
                nc.vector.tensor_scalar(neg_lo[:, :], neg_lo[:, :], -1.0, None, ALU.mult)
                link(nc.vector.scalar_tensor_tensor(out=row0_s[:, :], in0=row0_s[:, :], scalar=-2.0, in1=row0[:, :],
                                                    op0=ALU.mult, op1=ALU.add))
                link(nc.vector.tensor_reduce(half[:, :], ident[:, :].rearrange("p (i d) -> p i d", i=2), AX, ALU.add))
                dve.wait_ge(s_const, 16 * 7)
                link(nc.vector.tensor_scalar(q_b[:, :], q_b[:, :], QK_SCALE, None, ALU.mult))
                for m in range(FC):
                    nc.vector.tensor_scalar(k_bh[:, m, :], half[:, :], k_b[:, m:m + 1], None, ALU.mult)
                for mask, op in ((mask_gt, ALU.is_gt), (mask_ne, ALU.not_equal)):
                    link(nc.vector.tensor_scalar(at_[:, 0:N], adj_i, 0.0, None, op))
                    link(nc.vector.tensor_scalar(mask[:, :], at_[:, 0:N], 1.0, -MASKED, ALU.subtract, ALU.mult))
                link(nc.vector.tensor_reduce(has_edge[:, :], at_[:, 0:N], AX, ALU.max))
                lo_parts(2, len(w_plan))

        class Job:
            def __init__(self, name, n):
                self.n, self.full, self.taken = n, sem(name + "_full"), sem(name + "_taken")

        def at(g, n, k):
            return g * n + (k + 1)

        A_ORDER = ["m1"] * 4 + ["f1", "h1", "s1", "h1", "h1", "h1", "p1"] + ["v1"] * 4 + ["m2"] * 2 + \
                  ["f2", "h2", "s2", "h2", "p2"] + ["v2"] * 2 + ["y0"] * 2 + ["xt"] * 2
        B_ORDER = ["1x"] * 2 + ["1f"] + ["1h"] * 2 + ["1s", "1s", "1s", "1p", "1s", "1p", "1p", "1p"] + ["1v"] * 2 + \
                  ["2x"] * 2 + ["2q"] * 2 + ["2k"] * 2 + ["2s", "2s", "2h", "2s", "2h", "2p", "2s", "2p", "2p", "2p"] + ["2v"] * 2 + ["2y"] * 2
        C_ORDER = ["3x"] * 2 + ["3g"] * 2 + ["3h", "3s", "3h", "3p"] + ["3y"] * 2

        def numbered(order, prefix):
            jobs, seen, where, at = {}, {}, {}, []
            for i, name in enumerate(order):
                k = seen.get(name, 0)
                seen[name] = k + 1
                where[name, k] = i
                at.append((name, k))
            for name in seen:
                jobs[name] = Job(prefix + name, seen[name])
            return jobs, where, at

        JA, WA, SA = numbered(A_ORDER, "a_")
        JB, WB, SB_ = numbered(B_ORDER, "b_")
        JC, WC, SC_ = numbered(C_ORDER, "c_")
        A_BANKS, B_BANKS, C_BANKS = banks[0:3], banks[3:6], banks[6:8]

        def bank_a(name, k):
            return A_BANKS[WA[name, k] % len(A_BANKS)]

        def bank_b(name, k):
            return B_BANKS[WB[name, k] % len(B_BANKS)]

        def bank_c(name, k):
            return C_BANKS[WC[name, k] % len(C_BANKS)]

        def bank_free(jobs, where, order, n, name, k, g):
            i = where[name, k]
            if i >= n:
                before, j = order[i - n]
                return jobs[before].taken, at(g, jobs[before].n, j)
            before, _ = order[max(j for j in range(len(order)) if j % n == i)]
            return jobs[before].taken, (g + 1 if before == "xt" else g) * jobs[before].n

        def a_bank_free(name, k, g):
            return bank_free(JA, WA, SA, len(A_BANKS), name, k, g)

        def b_bank_free(name, k, g):
            return bank_free(JB, WB, SB_, len(B_BANKS), name, k, g)

        def c_bank_free(name, k, g):
            return bank_free(JC, WC, SC_, len(C_BANKS), name, k, g)

        def three(pe, psum, lhs, rhs, start, stop):
            nc.tensor.matmul(psum, lhs[0], rhs[0], start=start, stop=False)
            nc.tensor.matmul(psum, lhs[0], rhs[1], start=False, stop=False)
            return nc.tensor.matmul(psum, lhs[1], rhs[0], start=False, stop=stop)

        def parts(pair, *index):
            return pair[0][index], pair[1][index]

        def four(ap):
            return ap.rearrange("p (g j) -> p g j", g=4)

        ALL = slice(None)
        a_link, b_link, a_ve_link, b_ve_link = sem("a_stats_done"), sem("b_stats_done"), sem("a_var_eps"), sem("b_var_eps")
        c_link, c_ve_link, c_sum_link = sem("c_stats_done"), sem("c_var_eps"), sem("c_sum_done")
        a_sum_link, b_sum_link, max_link, b_edge_link, row_link = sem("a_sum_done"), sem("b_sum_done"), sem("b_max_done"), sem("b_inv_done"), sem("row_done")

        def steps(eng, body):
            body(-1, None, None, False, False, False, True)
            body(0, None, None, True, False, False, True)
            body(1, 0, None, True, True, False, True)
            body(2, 1, 0, True, True, True, True)
            with eng.Fori(3, NT - 1) as t:
                body(t, t - 1, t - 2, True, True, True, True)
            body(NT - 1, NT - 2, NT - 3, True, True, True, False)
            body(None, NT - 1, NT - 2, False, True, True, False)
            body(None, None, NT - 1, False, False, True, False)

        with nc.Block() as block:
            @block.sync
            def _(sp):
                def body(ga, gb, gc, with_a, with_b, with_c, another=True):
                    if with_a and another:
                        sp.wait_ge(S["axn_ready"], at(ga, 1, 0))
                        sp.dma_start(ax[:, :, :], X_GROUPS[ga + 1]).then_inc(S["ax_loaded"], 16)
                    if with_a:
                        if with_b:
                            sp.wait_ge(JB["1v"].taken, at(gb, 2, 1))
                        sp.dma_start(x1[:, :, :], X_GROUPS[ga]).then_inc(S["x1_loaded"], 16)
                    if with_c:
                        sp.wait_ge(JC["3y"].taken, at(gc, 2, 1))
                        sp.dma_start(OUT_GROUPS[gc], cx[:, :, :]).then_inc(S["out_stored"], 16)

                body(0, None, None, True, False, False)
                body(1, 0, None, True, True, False)
                body(2, 1, 0, True, True, True)
                with sp.Fori(3, NT - 1) as t:
                    body(t, t - 1, t - 2, True, True, True)
                body(NT - 1, NT - 2, NT - 3, True, True, True, another=False)
                body(None, NT - 1, NT - 2, False, True, True)
                body(None, None, NT - 1, False, False, True)
                sp.wait_ge(S["out_stored"], 16 * NT)

            @block.tensor
            def _(pe):
                def body(ga, gb, gc, with_a, with_b, with_c, with_n):
                    def transposes(bank, srcs):
                        for i, s in enumerate(srcs):
                            last = nc.tensor.transpose(bank[:, i * P:(i + 1) * P], s, ident[:, :])
                        return last

                    def project(bank, w, x, chunks, m):
                        for c in range(chunks):
                            last = three(pe, bank[:, :], parts(w, ALL, c, slice(m * P, (m + 1) * P)), parts(x, ALL, c, ALL),
                                         c == 0, c == chunks - 1)
                        return last

                    def project_terms(bank, w, x, chunks):
                        for c in range(chunks):
                            nc.tensor.matmul(bank[:, :], w[:, c, :], x[0][:, c, :], start=c == 0, stop=False)
                            last = nc.tensor.matmul(bank[:, :], w[:, c, :], x[1][:, c, :], start=False, stop=c == chunks - 1)
                        return last

                    def project_nodes(bank, off, n, w, x, chunks, g):
                        for c in range(chunks):
                            last = three(pe, bank[:, off:off + n], parts(x, ALL, c, slice(g * N, (g + 1) * N)),
                                         parts(w, ALL, c, ALL), c == 0, c == chunks - 1)
                        return last

                    def xt(c):
                        bank = bank_a("xt", c)
                        if with_a:
                            pe.wait_ge(*a_bank_free("xt", c, ga))
                        if c == 0:
                            pe.wait_ge(S["axn_ready"], at(ga + 1, 1, 0))
                        transposes(bank, [axn[:, g, c * P:(c + 1) * P] for g in range(G)]).then_inc(JA["xt"].full, 1)

                    def m1(m):
                        bank = bank_a("m1", m)
                        pe.wait_ge(*a_bank_free("m1", m, ga))
                        pe.wait_ge(JA["xt"].taken, at(ga, 2, 1))
                        project(bank, mlp1_w, a_in, FC, m).then_inc(JA["m1"].full, 1)

                    def f1():
                        bank = bank_a("f1", 0)
                        pe.wait_ge(*a_bank_free("f1", 0, ga))
                        pe.wait_ge(S["m1_ready"], at(ga, HC, HC - 1))
                        project_terms(bank, fa1_w, a_mid, HC).then_inc(JA["f1"].full, 1)

                    def h1(g):
                        bank = bank_a("h1", g)
                        pe.wait_ge(*a_bank_free("h1", g, ga))
                        project_nodes(bank, 0, HID, fc_w, a_mid, HC, g).then_inc(JA["h1"].full, 1)

                    def s1():
                        bank = bank_a("s1", 0)
                        pe.wait_ge(*a_bank_free("s1", 0, ga))
                        pe.wait_ge(S["a_p_ready"], at(ga, 2, 0))
                        pe.wait_ge(JA["f1"].taken, at(ga, 1, 0))
                        for g in range(G):
                            r = slice(g * N, (g + 1) * N)
                            last = nc.tensor.matmul(bank[:, r], ap[0:4, r], aq[0:4, r], start=True, stop=True)
                        last.then_inc(JA["s1"].full, 1)

                    def p1(which=0):
                        name = ("p1", "p2")[which]
                        bank = bank_a(name, 0)
                        pe.wait_ge(*a_bank_free(name, 0, ga))
                        pe.wait_ge(S["a_norm"], at(ga, 2, which))
                        transposes(bank, [az[:, g * N:(g + 1) * N] for g in range(G)]).then_inc(JA[name].full, 1)

                    def v1(c):
                        bank = bank_a("v1", c)
                        pe.wait_ge(*a_bank_free("v1", c, ga))
                        pe.wait_ge(JA["p1"].taken, at(ga, 1, 0))
                        pe.wait_ge(JA["h1"].taken, at(ga, G, G - 1))
                        for g in range(G):
                            r = slice(g * N, (g + 1) * N)
                            last = nc.tensor.matmul(bank[:, r], ah[:, g, c * P:(c + 1) * P], apt[:, r], start=True, stop=True)
                        last.then_inc(JA["v1"].full, 1)

                    def m2(c):
                        if c == 0:
                            for m in range(FC):
                                pe.wait_ge(*a_bank_free("m2", m, ga))
                        pe.wait_ge(S["out1_split"], at(ga, HC, c))
                        for m in range(FC):
                            last = three(pe, bank_a("m2", m)[:, :], parts(mlp2_w, ALL, c, slice(m * P, (m + 1) * P)), parts(a_mid, ALL, c, ALL),
                                         c == 0, c == HC - 1)
                            if c == HC - 1:
                                last.then_inc(JA["m2"].full, 1)

                    def f2():
                        bank = bank_a("f2", 0)
                        pe.wait_ge(*a_bank_free("f2", 0, ga))
                        pe.wait_ge(S["m2_ready"], at(ga, FC, FC - 1))
                        project_terms(bank, fa2_w, a_in, FC).then_inc(JA["f2"].full, 1)

                    def h2(b):
                        bank = bank_a("h2", b)
                        pe.wait_ge(*a_bank_free("h2", b, ga))
                        for i in range(2):
                            last = project_nodes(bank, i * F, F, hand_w, a_in, FC, 2 * b + i)
                        last.then_inc(JA["h2"].full, 1)

                    def s2():
                        bank = bank_a("s2", 0)
                        pe.wait_ge(*a_bank_free("s2", 0, ga))
                        pe.wait_ge(S["a_p_ready"], at(ga, 2, 1))
                        pe.wait_ge(JA["f2"].taken, at(ga, 1, 0))
                        nc.tensor.matmul(four(bank[:, :]), ident_bf[:, :], mask_gt[:, :].unsqueeze(1).to_broadcast([P, 4, N]), start=True, stop=False)
                        for g in range(G):
                            r = slice(g * N, (g + 1) * N)
                            last = nc.tensor.matmul(bank[:, r], ap[0:4, r], aq[0:4, r], start=False, stop=g == G - 1)
                        last.then_inc(JA["s2"].full, 1)

                    def v2(c):
                        bank = bank_a("v2", c)
                        pe.wait_ge(*a_bank_free("v2", c, ga))
                        pe.wait_ge(JA["p2"].taken, at(ga, 1, 0))
                        pe.wait_ge(JA["h2"].taken, at(ga, 2, 1))
                        for g in range(G):
                            r = slice(g * N, (g + 1) * N)
                            last = nc.tensor.matmul(bank[:, r], ah2[:, g, c * P:(c + 1) * P], apt[:, r], start=True, stop=True)
                        last.then_inc(JA["v2"].full, 1)

                    def y0(b):
                        bank = bank_a("y0", b)
                        pe.wait_ge(*a_bank_free("y0", b, ga))
                        pe.wait_ge(S["a_f"], at(ga, HC + FC, HC + FC - 1))
                        transposes(bank, [ay[:, c, (2 * b + i) * N:(2 * b + i + 1) * N] for i in range(2) for c in range(FC)]) \
                            .then_inc(JA["y0"].full, 1)

                    def x(l, c):
                        bank = bank_b(f"{l}x", c)
                        pe.wait_ge(*b_bank_free(f"{l}x", c, gb))
                        if c == 0:
                            pe.wait_ge(S["bxn_ready"], at(gb, 2, l - 1))
                        transposes(bank, [bxn[:, g, c * P:(c + 1) * P] for g in range(G)]).then_inc(JB[f"{l}x"].full, 1)

                    def proj(l, name, w, m):
                        bank = bank_b(f"{l}{name}", m)
                        pe.wait_ge(*b_bank_free(f"{l}{name}", m, gb))
                        pe.wait_ge(JB[f"{l}x"].taken, at(gb, 2, 1))
                        project(bank, w, b_in, FC, m).then_inc(JB[f"{l}{name}"].full, 1)

                    def f_l1():
                        bank = bank_b("1f", 0)
                        pe.wait_ge(*b_bank_free("1f", 0, gb))
                        pe.wait_ge(JB["1x"].taken, at(gb, 2, 1))
                        project_terms(bank, fah_w, b_in, FC).then_inc(JB["1f"].full, 1)

                    def nodes(l, w, b):
                        bank = bank_b(f"{l}h", b)
                        pe.wait_ge(*b_bank_free(f"{l}h", b, gb))
                        pe.wait_ge(JB[f"{l}x"].taken, at(gb, 2, 1))
                        for i in range(2):
                            last = project_nodes(bank, i * F, F, w, b_in, FC, 2 * b + i)
                        last.then_inc(JB[f"{l}h"].full, 1)

                    def s_l1(g):
                        bank = bank_b("1s", g)
                        pe.wait_ge(*b_bank_free("1s", g, gb))
                        if g == 0:
                            pe.wait_ge(S["rows_ready"], at(gb, 1, 0))
                        nc.tensor.matmul(four(bank[:, :]), ident_bf[:, :], mask_gt[:, :].unsqueeze(1).to_broadcast([P, 4, N]), start=True, stop=False)
                        r = slice(g * N, (g + 1) * N)
                        nc.tensor.matmul(bank[:, :], bf[:, r], bq[:, g, :], start=False, stop=True).then_inc(JB["1s"].full, 1)

                    def s_l2(g):
                        bank = bank_b("2s", g)
                        pe.wait_ge(*b_bank_free("2s", g, gb))
                        if g == 0:
                            pe.wait_ge(JB["2q"].taken, at(gb, 2, 1))
                            pe.wait_ge(JB["2k"].taken, at(gb, 2, 1))
                        nc.tensor.matmul(four(bank[:, :]), ident_bf[:, :], mask_ne[:, :].unsqueeze(1).to_broadcast([P, 4, N]), start=True, stop=False)
                        r = slice(g * N, (g + 1) * N)
                        for c in range(FC):
                            last = nc.tensor.matmul(bank[:, 2 * c * N:2 * (c + 1) * N], b1[:, c, r], bpt[:, g, 2 * c * N:2 * (c + 1) * N],
                                                    start=False, stop=c == FC - 1)
                        last.then_inc(JB["2s"].full, 1)

                    def p(l, g):
                        bank = bank_b(f"{l}p", g)
                        pe.wait_ge(*b_bank_free(f"{l}p", g, gb))
                        base = (l - 1) * G
                        pe.wait_ge(S["b_norm"], at(gb, 2 * G, base + g))
                        transposes(bank, [bz[:, g, h * N:(h + 1) * N] for h in range(4)]).then_inc(JB[f"{l}p"].full, 1)

                    def v_l1(b):
                        bank = bank_b("1v", b)
                        pe.wait_ge(*b_bank_free("1v", b, gb))
                        pe.wait_ge(JB["1h"].taken, at(gb, 2, 1))
                        pe.wait_ge(JB["1p"].taken, at(gb, G, 2 * b + 1))
                        for g in (2 * b, 2 * b + 1):
                            for h in range(HEADS):
                                off = (g % 2) * F + h * HD
                                last = nc.tensor.matmul(bank[:, off:off + HD], bpt[:, g, h * N:(h + 1) * N], b3[:, g, h * HD:(h + 1) * HD],
                                                        start=True, stop=True)
                        last.then_inc(JB["1v"].full, 1)

                    def v_l2(c):
                        bank = bank_b("2v", c)
                        pe.wait_ge(*b_bank_free("2v", c, gb))
                        pe.wait_ge(JB["2h"].taken, at(gb, 2, 1))
                        pe.wait_ge(JB["2p"].taken, at(gb, G, G - 1))
                        for g in range(G):
                            for i in range(2):
                                h = 2 * c + i
                                last = nc.tensor.matmul(bank[i * HD:(i + 1) * HD, g * N:(g + 1) * N], b3[:, g, h * HD:(h + 1) * HD],
                                                        bpt[:, g, h * N:(h + 1) * N], start=True, stop=True)
                        last.then_inc(JB["2v"].full, 1)

                    def y_l2(b):
                        bank = bank_b("2y", b)
                        pe.wait_ge(*b_bank_free("2y", b, gb))
                        pe.wait_ge(JB["2v"].taken, at(gb, 2, 1))
                        for i in range(2):
                            last = project_nodes(bank, i * F, F, o_w, b_in, FC, 2 * b + i)
                        last.then_inc(JB["2y"].full, 1)

                    def x_c(c):
                        bank = bank_c("3x", c)
                        pe.wait_ge(*c_bank_free("3x", c, gc))
                        if c == 0:
                            pe.wait_ge(S["cxn_ready"], at(gc, 1, 0))
                        transposes(bank, [cxn[:, g, c * P:(c + 1) * P] for g in range(G)]).then_inc(JC["3x"].full, 1)

                    def g_c(m):
                        bank = bank_c("3g", m)
                        pe.wait_ge(*c_bank_free("3g", m, gc))
                        pe.wait_ge(JC["3x"].taken, at(gc, 2, 1))
                        project(bank, bil_w, c_in, FC, m).then_inc(JC["3g"].full, 1)

                    def h_c(b):
                        bank = bank_c("3h", b)
                        pe.wait_ge(*c_bank_free("3h", b, gc))
                        for i in range(2):
                            last = project_nodes(bank, i * F, F, h3_w, c_in, FC, 2 * b + i)
                        last.then_inc(JC["3h"].full, 1)

                    def s_c():
                        bank = bank_c("3s", 0)
                        pe.wait_ge(*c_bank_free("3s", 0, gc))
                        pe.wait_ge(JC["3g"].taken, at(gc, 2, 1))
                        pe.wait_ge(S["3x_full"], at(gc, 2, 1))
                        nc.tensor.matmul(four(bank[:, :]), ident_bf[:, :], mask_gt[:, :].unsqueeze(1).to_broadcast([P, 4, N]), start=True, stop=False)
                        for g in range(G):
                            r = slice(g * N, (g + 1) * N)
                            for c in range(FC):
                                last = nc.tensor.matmul(bank[:, r], c1[:, c, r], c2[:, c, r], start=False, stop=(g, c) == (G - 1, FC - 1))
                        last.then_inc(JC["3s"].full, 1)

                    def p_c():
                        bank = bank_c("3p", 0)
                        pe.wait_ge(*c_bank_free("3p", 0, gc))
                        pe.wait_ge(S["c_norm"], at(gc, 1, 0))
                        transposes(bank, [cz[:, g * N:(g + 1) * N] for g in range(G)]).then_inc(JC["3p"].full, 1)

                    def y_c(b):
                        bank = bank_c("3y", b)
                        pe.wait_ge(*c_bank_free("3y", b, gc))
                        pe.wait_ge(JC["3h"].taken, at(gc, 2, 1))
                        pe.wait_ge(JC["3p"].taken, at(gc, 1, 0))
                        for i in range(2):
                            g = 2 * b + i
                            last = nc.tensor.matmul(bank[:, i * F:(i + 1) * F], cpt[:, g * N:(g + 1) * N], c3[:, g, :], start=True, stop=True)
                        last.then_inc(JC["3y"].full, 1)

                    if with_a:
                        m1(0); m1(1); m1(2); m1(3)
                    if with_b:
                        x(1, 0); x(1, 1)
                    if with_a:
                        f1()
                    if with_b:
                        f_l1(); nodes(1, l1_w, 0); nodes(1, l1_w, 1)
                    if with_a:
                        h1(0); s1(); h1(1)
                    if with_b:
                        s_l1(0); s_l1(1); s_l1(2)
                    if with_a:
                        h1(2); h1(3); p1(0)
                    if with_c:
                        x_c(0)
                    if with_b:
                        p(1, 0); s_l1(3)
                    if with_c:
                        x_c(1)
                    if with_a:
                        v1(0)
                    if with_b:
                        p(1, 1)
                    if with_a:
                        v1(1); v1(2)
                    if with_c:
                        g_c(0)
                    if with_a:
                        v1(3)
                    if with_c:
                        g_c(1)
                    if with_b:
                        p(1, 2); p(1, 3); v_l1(0); v_l1(1)
                    if with_a:
                        m2(0)
                    if with_c:
                        h_c(0); s_c(); h_c(1)
                    if with_a:
                        m2(1)
                    if with_b:
                        x(2, 0); x(2, 1)
                    if with_a:
                        m2(2); m2(3)
                    if with_b:
                        proj(2, 'q', q_w, 0); proj(2, 'q', q_w, 1); proj(2, 'k', k_w, 0); proj(2, 'k', k_w, 1)
                    if with_a:
                        f2(); h2(0)
                    if with_b:
                        s_l2(0); s_l2(1)
                    if with_a:
                        s2(); h2(1)
                    if with_b:
                        nodes(2, v_w, 0); s_l2(2); nodes(2, v_w, 1); p(2, 0)
                    if with_c:
                        p_c()
                    if with_b:
                        s_l2(3); p(2, 1)
                    if with_c:
                        y_c(0)
                    if with_a:
                        p1(1)
                    if with_c:
                        y_c(1)
                    if with_a:
                        v2(0); v2(1)
                    if with_b:
                        p(2, 2); p(2, 3); v_l2(0); v_l2(1)
                    if with_a:
                        y0(0)
                    if with_n:
                        xt(0)
                    if with_a:
                        y0(1)
                    if with_b:
                        y_l2(0)
                    if with_n:
                        xt(1)
                    if with_b:
                        y_l2(1)
                steps(pe, body)

            @block.scalar
            def _(act):
                def body(ga, gb, gc, with_a, with_b, with_c, with_n):
                    def xt(c):
                        bank = bank_a("xt", c)
                        act.wait_ge(JA["xt"].full, at(ga + 1, 2, c))
                        nc.scalar.activation(a_in[0][:, c, :], bank[:, :], ACT.Relu).then_inc(S["a_hi_ready"], 1)

                    def m1(m):
                        bank = bank_a("m1", m)
                        act.wait_ge(JA["m1"].full, at(ga, JA["m1"].n, m))
                        nc.scalar.activation(o1[:, m, :], bank[:, :], ACT.Relu, bias=mlp1_b[:, m:m + 1])
                        nc.scalar.activation(a_mid[0][:, m, :], bank[:, :], ACT.Relu, bias=mlp1_b[:, m:m + 1]).then_inc(JA["m1"].taken, 1)

                    def rows_p(which):
                        bank = bank_a(("f1", "f2")[which], 0)
                        act.wait_ge(JA[("f1", "f2")[which]].full, at(ga, JA[("f1", "f2")[which]].n, 0))
                        nc.scalar.activation(ap[0:4, :], bank[0:4, :], ACT.Identity, bias=row1[0:4, :], scale=row0[0:4, :]) \
                            .then_inc(S["a_p_ready"], 1)

                    def h1(g):
                        bank = bank_a("h1", g)
                        act.wait_ge(JA["h1"].full, at(ga, JA["h1"].n, g))
                        nc.scalar.activation(ah[:, g, :], bank[:, :], ACT.Copy).then_inc(JA["h1"].taken, 1)

                    def scaled(which):
                        bank = bank_a(("s1", "s2")[which], 0)
                        act.wait_ge(JA[("s1", "s2")[which]].full, at(ga, JA[("s1", "s2")[which]].n, 0))
                        nc.scalar.activation(at_, bank[:, :], ACT.Copy, scale=SLOPE).then_inc(S["a_t_ready"], 1)

                    def exp(which):
                        act.wait_ge(S["a_shifted"], at(ga, 2, which))
                        nc.scalar.activation(az[:, :], az[:, :], ACT.Exp).then_inc(S["a_exp"], 1)

                    def pt(which):
                        name = ("p1", "p2")[which]
                        bank = bank_a(name, 0)
                        act.wait_ge(JA[name].full, at(ga, JA[name].n, 0))
                        nc.scalar.activation(apt[:, :], bank[:, :], ACT.Copy).then_inc(JA[name].taken, 1)

                    def e1(which, c):
                        bank = bank_a(("v1", "v2")[which], c)
                        act.wait_ge(JA[("v1", "v2")[which]].full, at(ga, JA[("v1", "v2")[which]].n, c))
                        k = which * HC + c
                        if k >= 2:
                            act.wait_ge(S["a_f"], at(ga, HC + FC, k - 2))
                        nc.scalar.activation(aE[:, k % 2, :], bank[:, :], ACT.Exp).then_inc(S["a_e1"], 1)

                    def e2(which, c):
                        k = which * HC + c
                        act.wait_ge(S["a_u"], at(ga, HC + FC, k))
                        nc.scalar.activation(aE[:, k % 2, :], aE[:, k % 2, :], ACT.Exp, bias=minus1[:, :]).then_inc(S["a_e2"], 1)

                    def v1_hi(c):
                        act.wait_ge(S["a_f"], at(ga, HC + FC, c))
                        nc.scalar.activation(a_mid[0][:, c, :], aF[:, c % 2, :], ACT.Copy).then_inc(S["out1_hi"], 1)

                    def m2(m):
                        bank = bank_a("m2", m)
                        act.wait_ge(JA["m2"].full, at(ga, JA["m2"].n, m))
                        nc.scalar.activation(o2[:, m, :], bank[:, :], ACT.Relu, bias=mlp2_b[:, m:m + 1])
                        nc.scalar.activation(a_in[0][:, m, :], bank[:, :], ACT.Relu, bias=mlp2_b[:, m:m + 1]).then_inc(JA["m2"].taken, 1)

                    def h2(b):
                        bank = bank_a("h2", b)
                        act.wait_ge(JA["h2"].full, at(ga, JA["h2"].n, b))
                        nc.scalar.activation(ah2[:, 2 * b:2 * b + 2, :].rearrange("p a b -> p (a b)"), bank[:, :], ACT.Copy) \
                            .then_inc(JA["h2"].taken, 1)

                    def x(l, c):
                        bank = bank_b(f"{l}x", c)
                        act.wait_ge(JB[f"{l}x"].full, at(gb, JB[f"{l}x"].n, c))
                        nc.scalar.activation(b_in[0][:, c, :], bank[:, :], ACT.Relu).then_inc(S["b_hi_ready"], 1)

                    def f_hi():
                        bank = bank_b("1f", 0)
                        act.wait_ge(JB["1f"].full, at(gb, 1, 0))
                        nc.scalar.activation(bf[:, :], bank[:, :], ACT.Copy).then_inc(S["f_hi"], 1)

                    def rows_l1():
                        act.wait_ge(JB["1f"].taken, at(gb, 1, 0))
                        nc.scalar.activation(four(bf[:, :]), bX, ACT.Identity, bias=row1[:, :], scale=row0_s[:, :])
                        for h in (0, 1):
                            last = nc.scalar.activation(bq[:, :, h * N:(h + 1) * N], bX, ACT.Identity,
                                                        bias=head0[:, h:h + 1], scale=head1_s[:, h:h + 1])
                        last.then_inc(S["rows_act"], 1)

                    def copy_nodes(b):
                        bank = bank_b("1h", b)
                        act.wait_ge(JB["1h"].full, at(gb, 2, b))
                        nc.scalar.activation(b3[:, 2 * b:2 * b + 2, :].rearrange("p a b -> p (a b)"), bank[:, :], ACT.Copy) \
                            .then_inc(JB["1h"].taken, 1)

                    def b_scaled(g):
                        bank = bank_b("1s", g)
                        act.wait_ge(JB["1s"].full, at(gb, JB["1s"].n, g))
                        if g >= 2:
                            act.wait_ge(JB["1s"].taken, at(gb, G, g - 2))
                        nc.scalar.activation(bt[:, g % 2, :], bank[:, :], ACT.Copy, scale=SLOPE).then_inc(S["b_t_ready"], 1)

                    def b_exp(l, g):
                        k = (l - 1) * G + g
                        if l == 2:
                            act.wait_ge(JB["2s"].taken, at(gb, G, g))
                        else:
                            act.wait_ge(S["b_shifted"], at(gb, G, g))
                        nc.scalar.activation(bz[:, g, :], bz[:, g, :], ACT.Exp).then_inc(S["b_exp"], 1)

                    def b_pt(l, g):
                        bank = bank_b(f"{l}p", g)
                        act.wait_ge(JB[f"{l}p"].full, at(gb, JB[f"{l}p"].n, g))
                        nc.scalar.activation(bpt[:, g, :], bank[:, :], ACT.Copy).then_inc(JB[f"{l}p"].taken, 1)

                    def b_e(b):
                        bank = bank_b("1v", b)
                        act.wait_ge(JB["1v"].full, at(gb, 2, b))
                        nc.scalar.activation(bt[:, b, :], bank[:, :], ACT.Exp).then_inc(S["b_e"], 1)

                    def q(m):
                        bank = bank_b("2q", m)
                        act.wait_ge(JB["2q"].full, at(gb, JB["2q"].n, m))
                        nc.scalar.activation(b1[:, m, :], bank[:, :], ACT.Identity, bias=q_b[:, m:m + 1], scale=QK_SCALE).then_inc(JB["2q"].taken, 1)

                    def k(m):
                        bank = bank_b("2k", m)
                        act.wait_ge(JB["2k"].full, at(gb, JB["2k"].n, m))
                        for i in range(2):
                            h = 2 * m + i
                            last = nc.scalar.activation(bpt[:, :, h * N:(h + 1) * N], four(bank[:, :]), ACT.Identity, bias=k_bh[:, m, i:i + 1],
                                                        scale=half[:, i:i + 1])
                        last.then_inc(JB["2k"].taken, 1)

                    def heads_hi(c):
                        bank = bank_b("2v", c)
                        act.wait_ge(JB["2v"].full, at(gb, JB["2v"].n, c))
                        nc.scalar.activation(b_in[0][:, c, :], bank[:, :], ACT.Copy).then_inc(S["2v_hi"], 1)

                    def x_c(c):
                        bank = bank_c("3x", c)
                        act.wait_ge(JC["3x"].full, at(gc, 2, c))
                        nc.scalar.activation(c_in[0][:, c, :], bank[:, :], ACT.Relu).then_inc(S["c_hi_ready"], 1)
                        nc.scalar.activation(c2[:, c, :], bank[:, :], ACT.Relu).then_inc(S["3x_full"], 1)

                    def g_c(m):
                        bank = bank_c("3g", m)
                        act.wait_ge(JC["3g"].full, at(gc, 2, m))
                        nc.scalar.activation(c1[:, m, :], bank[:, :], ACT.Copy).then_inc(JC["3g"].taken, 1)

                    def h_c(b):
                        bank = bank_c("3h", b)
                        act.wait_ge(JC["3h"].full, at(gc, 2, b))
                        nc.scalar.activation(c3[:, 2 * b:2 * b + 2, :].rearrange("p a b -> p (a b)"), bank[:, :], ACT.Copy) \
                            .then_inc(JC["3h"].taken, 1)

                    def scaled_c():
                        act.wait_ge(JC["3s"].full, at(gc, 1, 0))
                        nc.scalar.activation(ct, bank_c("3s", 0)[:, :], ACT.Copy, scale=SLOPE).then_inc(S["c_t_ready"], 1)

                    def exp_c():
                        act.wait_ge(S["c_shifted"], at(gc, 1, 0))
                        nc.scalar.activation(cz, cz, ACT.Exp).then_inc(S["c_exp"], 1)

                    def pt_c():
                        act.wait_ge(JC["3p"].full, at(gc, 1, 0))
                        nc.scalar.activation(cpt, bank_c("3p", 0)[:, :], ACT.Copy).then_inc(JC["3p"].taken, 1)

                    if with_a:
                        m1(0); m1(1); m1(2); m1(3)
                    if with_b:
                        x(1, 0); x(1, 1)
                    if with_a:
                        rows_p(0)
                    if with_b:
                        f_hi(); copy_nodes(0); copy_nodes(1); rows_l1()
                    if with_a:
                        h1(0); scaled(0); h1(1)
                    if with_b:
                        b_scaled(0); b_scaled(1)
                    if with_a:
                        exp(0)
                    if with_b:
                        b_scaled(2); b_exp(1, 0)
                    if with_a:
                        h1(2)
                    if with_b:
                        b_exp(1, 1)
                    if with_a:
                        h1(3); pt(0)
                    if with_c:
                        x_c(0)
                    if with_b:
                        b_scaled(3); b_pt(1, 0)
                    if with_c:
                        x_c(1)
                    if with_a:
                        e1(0, 0)
                    if with_b:
                        b_exp(1, 2); b_pt(1, 1); b_exp(1, 3)
                    if with_a:
                        e2(0, 0); e1(0, 1)
                    if with_c:
                        g_c(0)
                    if with_a:
                        v1_hi(0); e1(0, 2)
                    if with_c:
                        g_c(1)
                    if with_a:
                        e2(0, 1)
                    if with_b:
                        b_pt(1, 2); b_pt(1, 3)
                    if with_a:
                        e1(0, 3)
                    if with_b:
                        b_e(0)
                    if with_a:
                        v1_hi(1); e2(0, 2)
                    if with_b:
                        b_e(1)
                    if with_a:
                        e2(0, 3)
                    if with_c:
                        h_c(0)
                    if with_a:
                        v1_hi(2)
                    if with_c:
                        scaled_c(); h_c(1)
                    if with_a:
                        v1_hi(3)
                    if with_b:
                        x(2, 0); x(2, 1)
                    if with_a:
                        m2(0); m2(1)
                    if with_b:
                        q(0); q(1)
                    if with_c:
                        exp_c()
                    if with_b:
                        k(0); k(1)
                    if with_a:
                        rows_p(1); h2(0)
                    if with_b:
                        b_exp(2, 0); b_exp(2, 1)
                    if with_a:
                        h2(1); scaled(1)
                    if with_b:
                        b_pt(2, 0)
                    if with_a:
                        exp(1)
                    if with_b:
                        b_exp(2, 2)
                    if with_c:
                        pt_c()
                    if with_b:
                        b_pt(2, 1); b_exp(2, 3)
                    if with_a:
                        pt(1); e1(1, 0); e1(1, 1)
                    if with_b:
                        b_pt(2, 2)
                    if with_a:
                        e2(1, 0)
                    if with_b:
                        b_pt(2, 3)
                    if with_a:
                        e2(1, 1)
                    if with_b:
                        heads_hi(0); heads_hi(1)
                    if with_n:
                        xt(0); xt(1)
                steps(act, body)

            @block.vector
            def _(dve):
                def body(ga, gb, gc, with_a, with_b, with_c, with_n):
                    def stats(x, st, mv, link):
                        for g in range(G):
                            last = nc.vector.bn_stats(st[:, g, :], x[:, g, :])
                        last.then_inc(link[0], 1)
                        dve.wait_ge(link[0], at(*link[1:]))
                        nc.vector.memset(carrier[:, :], 0.0)
                        for g in range(G):
                            last = nc.vector.bn_aggr(mv[:, g, :], st[:, g, :])
                        return last

                    def normalise(x, xn, mv, rs):
                        for g in range(G):
                            last = nc.vector.tensor_scalar(xn[:, g, :], x[:, g, :], mv[:, g, 0:1], rs[:, g:g + 1], ALU.subtract, ALU.mult)
                        return last

                    def a_stats():
                        dve.wait_ge(S["ax_loaded"], at(ga + 1, 16, 15))
                        stats(ax, a_st, a_mv, (a_link, ga + 1, 1, 0)).then_inc(S["a_var"], 1)

                    def a_normalise():
                        dve.wait_ge(S["a_rstd"], at(ga + 1, 1, 0))
                        if with_a:
                            dve.wait_ge(JA["v2"].full, at(ga, FC, FC - 1))
                        normalise(ax, axn, a_mv, a_rs).then_inc(S["axn_ready"], 1)

                    def xt(c):
                        bank = bank_a("xt", c)
                        dve.wait_ge(JA["xt"].full, at(ga + 1, 2, c))
                        dve.wait_ge(S["a_hi_ready"], at(ga + 1, 2, c))
                        nc.vector.scalar_tensor_tensor(out=a_in[1][:, c, :], in0=bank[:, :], scalar=0.0, in1=a_in[0][:, c, :],
                                                       op0=ALU.max, op1=ALU.subtract).then_inc(JA["xt"].taken, 1)

                    def m1(m):
                        dve.wait_ge(JA["m1"].taken, at(ga, HC, m))
                        nc.vector.tensor_tensor(a_mid[1][:, m, :], o1[:, m, :], a_mid[0][:, m, :], ALU.subtract).then_inc(S["m1_ready"], 1)

                    def rows_q(which):
                        name = ("f1", "f2")[which]
                        bank = bank_a(name, 0)
                        dve.wait_ge(JA[name].full, at(ga, JA[name].n, 0))
                        dve.wait_ge(S["a_p_ready"], at(ga, 2, which))
                        nc.vector.tensor_scalar(aq[0:4, :], bank[0:4, :], row1[0:4, :], row0[0:4, :], ALU.mult, ALU.add) \
                            .then_inc(JA[name].taken, 1)

                    def lrelu(which):
                        name = ("s1", "s2")[which]
                        dve.wait_ge(S["a_t_ready"], at(ga, 2, which))
                        nc.vector.tensor_tensor(az[:, :], bank_a(name, 0)[:, :], at_, ALU.max).then_inc(JA[name].taken, 1)
                        dve.wait_ge(JA[name].taken, at(ga, 1, 0))
                        nc.vector.tensor_reduce(a_max[:, :], four(az[:, :]), AX, ALU.max).then_inc(S["a_z_max"], 1)

                    def total(which):
                        dve.wait_ge(S["a_exp"], at(ga, 2, which))
                        nc.vector.tensor_reduce(a_sum[:, :], four(az[:, :]), AX, ALU.add).then_inc(a_sum_link, 1)
                        dve.wait_ge(a_sum_link, at(ga, 2, which))
                        nc.vector.reciprocal(a_inv[:, :], a_sum[:, :]).then_inc(S["a_inv_ready"], 1)

                    def u(which, c):
                        k = which * HC + c
                        name = ("v1", "v2")[which]
                        dve.wait_ge(S["a_e1"], at(ga, HC + FC, k))
                        nc.vector.tensor_scalar(aE[:, k % 2, :], aE[:, k % 2, :], 1.0, None, ALU.min).then_inc(S["a_u"], 1)
                        res = (o1, o2)[which]
                        nc.vector.scalar_tensor_tensor(out=aR[:, k % 2, :], in0=bank_a(name, c)[:, :], scalar=0.0, in1=res[:, c, :],
                                                       op0=ALU.max, op1=ALU.add).then_inc(JA[name].taken, 1)

                    def out1(c):
                        dve.wait_ge(S["a_e2"], at(ga, HC + FC, c))
                        dve.wait_ge(JA["v1"].taken, at(ga, HC, c))
                        if c >= 2:
                            dve.wait_ge(S["out1_split"], at(ga, HC, c - 2))
                        nc.vector.scalar_tensor_tensor(out=aF[:, c % 2, :], in0=aE[:, c % 2, :], scalar=-1.0, in1=aR[:, c % 2, :],
                                                       op0=ALU.add, op1=ALU.add).then_inc(S["a_f"], 1)

                    def out1_lo(c):
                        dve.wait_ge(S["out1_hi"], at(ga, HC, c))
                        nc.vector.tensor_tensor(a_mid[1][:, c, :], aF[:, c % 2, :], a_mid[0][:, c, :], ALU.subtract).then_inc(S["out1_split"], 1)

                    def m2(m):
                        dve.wait_ge(JA["m2"].taken, at(ga, FC, m))
                        nc.vector.tensor_tensor(a_in[1][:, m, :], o2[:, m, :], a_in[0][:, m, :], ALU.subtract).then_inc(S["m2_ready"], 1)

                    def out2(c):
                        k = HC + c
                        dve.wait_ge(S["a_e2"], at(ga, HC + FC, k))
                        dve.wait_ge(JA["v2"].taken, at(ga, FC, c))
                        nc.vector.scalar_tensor_tensor(out=ay[:, c, :], in0=aE[:, k % 2, :], scalar=-1.0, in1=aR[:, k % 2, :],
                                                       op0=ALU.add, op1=ALU.add).then_inc(S["a_f"], 1)

                    def y0(b):
                        bank = bank_a("y0", b)
                        dve.wait_ge(JA["y0"].full, at(ga, JA["y0"].n, b))
                        if b == 0:
                            dve.wait_ge(S["x1_loaded"], at(ga, 16, 15))
                        nc.vector.scalar_tensor_tensor(out=x1[:, 2 * b:2 * b + 2, :].rearrange("p a b -> p (a b)"), in0=bank[:, :], scalar=0.0,
                                                       in1=x1[:, 2 * b:2 * b + 2, :].rearrange("p a b -> p (a b)"),
                                                       op0=ALU.max, op1=ALU.add).then_inc(JA["y0"].taken, 1)

                    def b_stats(l):
                        x = x1 if l == 1 else bx
                        if l == 1:
                            dve.wait_ge(JA["y0"].taken, at(gb, 2, 1))
                        else:
                            dve.wait_ge(S["b_full"], at(gb, 2, 1))
                        stats(x, b_st, b_mv, (b_link, gb, 2, l - 1)).then_inc(S["b_var"], 1)

                    def b_normalise(l):
                        dve.wait_ge(S["b_rstd"], at(gb, 2, l - 1))
                        normalise(x1 if l == 1 else bx, bxn, b_mv, b_rs).then_inc(S["bxn_ready"], 1)

                    def x(l, c):
                        bank = bank_b(f"{l}x", c)
                        dve.wait_ge(JB[f"{l}x"].full, at(gb, JB[f"{l}x"].n, c))
                        dve.wait_ge(S["b_hi_ready"], at(gb, 4, 2 * (l - 1) + c))
                        nc.vector.scalar_tensor_tensor(out=b_in[1][:, c, :], in0=bank[:, :], scalar=0.0, in1=b_in[0][:, c, :],
                                                       op0=ALU.max, op1=ALU.subtract).then_inc(JB[f"{l}x"].taken, 1)

                    def f_split():
                        dve.wait_ge(S["f_hi"], at(gb, 1, 0))
                        dve.wait_ge(JB["1h"].full, at(gb, 2, 1))
                        nc.vector.scalar_tensor_tensor(out=bX, in0=four(bank_b("1f", 0)[:, :]), scalar=neg_lo[:, :], in1=four(bf[:, :]),
                                                       op0=ALU.mult, op1=ALU.add).then_inc(JB["1f"].taken, 1)

                    def rows_l1():
                        dve.wait_ge(JB["1f"].taken, at(gb, 1, 0))
                        nc.vector.tensor_scalar(bq[:, :, 2 * N:3 * N], bX, head1_s[:, 2:3], head0[:, 2:3], ALU.mult, ALU.add) \
                            .then_inc(row_link, 1)
                        dve.wait_ge(S["rows_act"], at(gb, 1, 0))
                        dve.wait_ge(row_link, at(gb, 1, 0))
                        nc.vector.tensor_scalar(bX, bX, head1_s[:, 3:4], head0[:, 3:4], ALU.mult, ALU.add).then_inc(S["rows_ready"], 1)

                    def b_lrelu(g):
                        dve.wait_ge(S["b_t_ready"], at(gb, G, g))
                        nc.vector.tensor_tensor(bz[:, g, :], bank_b("1s", g)[:, :], bt[:, g % 2, :], ALU.max).then_inc(JB["1s"].taken, 1)
                        dve.wait_ge(JB["1s"].taken, at(gb, JB["1s"].n, g))
                        nc.vector.tensor_reduce(b_max[:, g, :], four(bz[:, g, :]), AX, ALU.max).then_inc(S["b_z_max"], 1)

                    def b_max2(g):
                        bank = bank_b("2s", g)
                        dve.wait_ge(JB["2s"].full, at(gb, JB["2s"].n, g))
                        nc.vector.tensor_reduce(b_max[:, g, :], four(bank[:, :]), AX, ALU.max).then_inc(max_link, 1)
                        dve.wait_ge(max_link, at(gb, G, g))
                        nc.vector.tensor_tensor(four(bz[:, g, :]), four(bank[:, :]), b_max[:, g, :].unsqueeze(2).to_broadcast([P, 4, N]),
                                                ALU.subtract).then_inc(JB["2s"].taken, 1)

                    def b_total(l, g):
                        k = (l - 1) * G + g
                        dve.wait_ge(S["b_exp"], at(gb, 2 * G, k))
                        nc.vector.tensor_reduce(b_sum[:, g, :], four(bz[:, g, :]), AX, ALU.add).then_inc(b_sum_link, 1)
                        dve.wait_ge(b_sum_link, at(gb, 2 * G, k))
                        i = nc.vector.reciprocal(b_inv[:, g, :], b_sum[:, g, :])
                        if l == 2:
                            i.then_inc(b_edge_link, 1)
                            dve.wait_ge(b_edge_link, at(gb, G, g))
                            i = nc.vector.tensor_scalar(b_inv[:, g, :], b_inv[:, g, :], has_edge[:, :], None, ALU.mult)
                        i.then_inc(S["b_inv_ready"], 1)

                    def elu(b):
                        bank = bank_b("1v", b)
                        rows = bx[:, 2 * b:2 * b + 2, :].rearrange("p a b -> p (a b)")
                        dve.wait_ge(S["b_e"], at(gb, 2, b))
                        if b == 0:
                            dve.wait_ge(S["x1_less_1"], at(gb, 1, 0))
                        nc.vector.scalar_tensor_tensor(out=rows, in0=bank[:, :], scalar=0.0, in1=x1[:, 2 * b:2 * b + 2, :].rearrange("p a b -> p (a b)"),
                                                       op0=ALU.max, op1=ALU.add).then_inc(JB["1v"].taken, 1)
                        dve.wait_ge(JB["1v"].taken, at(gb, 2, b))
                        nc.vector.scalar_tensor_tensor(out=rows, in0=bt[:, b, :], scalar=1.0, in1=rows,
                                                       op0=ALU.min, op1=ALU.add).then_inc(S["b_full"], 1)

                    def v_bias(b):
                        bank = bank_b("2h", b)
                        dve.wait_ge(JB["2h"].full, at(gb, JB["2h"].n, b))
                        nc.vector.tensor_tensor(b3[:, 2 * b:2 * b + 2, :], bank[:, :].rearrange("p (a b) -> p a b", a=2),
                                                v_b[:, :].unsqueeze(1).to_broadcast([P, 2, F]), ALU.add).then_inc(JB["2h"].taken, 1)

                    def heads_lo(c):
                        bank = bank_b("2v", c)
                        dve.wait_ge(S["2v_hi"], at(gb, 2, c))
                        nc.vector.tensor_tensor(b_in[1][:, c, :], bank[:, :], b_in[0][:, c, :], ALU.subtract).then_inc(JB["2v"].taken, 1)

                    def y_l2(b):
                        bank = bank_b("2y", b)
                        dve.wait_ge(JB["2y"].full, at(gb, JB["2y"].n, b))
                        r = slice(2 * b, 2 * b + 2)
                        if b == 0:
                            dve.wait_ge(S["bx_bias"], at(gb, 1, 0))
                            dve.wait_ge(S["out_stored"], 16 * gb)
                        nc.vector.tensor_tensor(cx[:, r, :].rearrange("p a b -> p (a b)"), bank[:, :],
                                                bx[:, r, :].rearrange("p a b -> p (a b)"), ALU.add).then_inc(JB["2y"].taken, 1)

                    def stats_c():
                        dve.wait_ge(JB["2y"].taken, at(gc, 2, 1))
                        stats(cx, c_st, c_mv, (c_link, gc, 1, 0)).then_inc(S["c_var"], 1)

                    def normalise_c():
                        dve.wait_ge(S["c_rstd"], at(gc, 1, 0))
                        normalise(cx, cxn, c_mv, c_rs).then_inc(S["cxn_ready"], 1)

                    def x_c(c):
                        bank = bank_c("3x", c)
                        dve.wait_ge(S["3x_full"], at(gc, 2, c))
                        nc.vector.scalar_tensor_tensor(out=c_in[1][:, c, :], in0=bank[:, :], scalar=0.0, in1=c_in[0][:, c, :],
                                                       op0=ALU.max, op1=ALU.subtract).then_inc(JC["3x"].taken, 1)

                    def lrelu_c():
                        dve.wait_ge(S["c_t_ready"], at(gc, 1, 0))
                        nc.vector.tensor_tensor(cz, bank_c("3s", 0)[:, :], ct, ALU.max).then_inc(JC["3s"].taken, 1)
                        dve.wait_ge(JC["3s"].taken, at(gc, 1, 0))
                        nc.vector.tensor_reduce(c_max[:, :], four(cz), AX, ALU.max).then_inc(S["c_z_max"], 1)

                    def total_c():
                        dve.wait_ge(S["c_exp"], at(gc, 1, 0))
                        nc.vector.tensor_reduce(c_sum[:, :], four(cz), AX, ALU.add).then_inc(c_sum_link, 1)
                        dve.wait_ge(c_sum_link, at(gc, 1, 0))
                        nc.vector.reciprocal(c_inv[:, :], c_sum[:, :]).then_inc(S["c_inv_ready"], 1)

                    def y_c(b):
                        bank = bank_c("3y", b)
                        dve.wait_ge(JC["3y"].full, at(gc, JC["3y"].n, b))
                        r = slice(2 * b, 2 * b + 2)
                        nc.vector.scalar_tensor_tensor(out=cx[:, r, :].rearrange("p a b -> p (a b)"), in0=bank[:, :], scalar=0.0,
                                                       in1=cx[:, r, :].rearrange("p a b -> p (a b)"), op0=ALU.max, op1=ALU.add) \
                            .then_inc(JC["3y"].taken, 1)

                    if with_b:
                        b_stats(1)
                    if with_c:
                        stats_c()
                    if with_b:
                        b_normalise(1)
                    if with_a:
                        m1(0); m1(1); m1(2); m1(3)
                    if with_b:
                        x(1, 0); x(1, 1)
                    if with_c:
                        normalise_c()
                    if with_n:
                        a_stats()
                    if with_a:
                        rows_q(0)
                    if with_b:
                        f_split(); rows_l1()
                    if with_a:
                        lrelu(0)
                    if with_b:
                        b_lrelu(0); b_lrelu(1)
                    if with_a:
                        total(0)
                    if with_b:
                        b_total(1, 0); b_lrelu(2); b_total(1, 1)
                    if with_c:
                        x_c(0)
                    if with_b:
                        b_lrelu(3)
                    if with_c:
                        x_c(1)
                    if with_a:
                        u(0, 0)
                    if with_b:
                        b_total(1, 2); b_total(1, 3)
                    if with_a:
                        out1(0); u(0, 1); out1_lo(0); u(0, 2); out1(1); u(0, 3)
                    if with_b:
                        elu(0); elu(1); b_stats(2)
                    if with_a:
                        out1(2); out1_lo(1)
                    if with_b:
                        b_normalise(2)
                    if with_a:
                        out1(3); out1_lo(2); out1_lo(3)
                    if with_b:
                        x(2, 0); x(2, 1)
                    if with_c:
                        lrelu_c()
                    if with_a:
                        m2(0); m2(1)
                    if with_c:
                        total_c()
                    if with_a:
                        rows_q(1)
                    if with_b:
                        b_max2(0); b_max2(1); b_total(2, 0); b_total(2, 1); v_bias(0)
                    if with_a:
                        lrelu(1)
                    if with_b:
                        b_max2(2); v_bias(1)
                    if with_a:
                        total(1)
                    if with_b:
                        b_max2(3); b_total(2, 2); b_total(2, 3)
                    if with_c:
                        y_c(0); y_c(1)
                    if with_a:
                        u(1, 0); u(1, 1); out2(0)
                    if with_n:
                        a_normalise()
                    if with_a:
                        out2(1)
                    if with_b:
                        heads_lo(0); heads_lo(1)
                    if with_a:
                        y0(0); y0(1)
                    if with_n:
                        xt(0)
                    if with_b:
                        y_l2(0)
                    if with_n:
                        xt(1)
                    if with_b:
                        y_l2(1)
                steps(dve, body)

            @block.gpsimd
            def _(pool):
                def body(ga, gb, gc, with_a, with_b, with_c, with_n):
                    def rstd(mv, ve, rs, link):
                        nc.gpsimd.tensor_tensor(ve[:, :], mv[:, :, 1], eps_t[:, :], ALU.add).then_inc(link[0], 1)
                        pool.wait_ge(link[0], at(*link[1:]))
                        return nc.gpsimd.tensor_tensor(rs[:, :], ve[:, :], pow_t[:, :], ALU.pow)

                    def a_rstd():
                        pool.wait_ge(S["a_var"], at(ga + 1, 1, 0))
                        rstd(a_mv, a_ve, a_rs, (a_ve_link, ga + 1, 1, 0)).then_inc(S["a_rstd"], 1)

                    def b_rstd(l):
                        pool.wait_ge(S["b_var"], at(gb, 2, l - 1))
                        rstd(b_mv, b_ve, b_rs, (b_ve_link, gb, 2, l - 1)).then_inc(S["b_rstd"], 1)

                    def shift(which):
                        pool.wait_ge(S["a_z_max"], at(ga, 2, which))
                        nc.gpsimd.tensor_tensor(four(az[:, :]), four(az[:, :]), a_max[:, :].unsqueeze(2).to_broadcast([P, 4, N]), ALU.subtract) \
                            .then_inc(S["a_shifted"], 1)

                    def norm(which):
                        pool.wait_ge(S["a_inv_ready"], at(ga, 2, which))
                        nc.gpsimd.tensor_tensor(four(az[:, :]), four(az[:, :]), a_inv[:, :].unsqueeze(2).to_broadcast([P, 4, N]), ALU.mult) \
                            .then_inc(S["a_norm"], 1)

                    def b_shift(g):
                        pool.wait_ge(S["b_z_max"], at(gb, G, g))
                        z = four(bz[:, g, :])
                        nc.gpsimd.tensor_tensor(z, z, b_max[:, g, :].unsqueeze(2).to_broadcast([P, 4, N]), ALU.subtract) \
                            .then_inc(S["b_shifted"], 1)

                    def b_norm(l, g):
                        k = (l - 1) * G + g
                        pool.wait_ge(S["b_inv_ready"], at(gb, 2 * G, k))
                        z = four(bz[:, g, :])
                        nc.gpsimd.tensor_tensor(z, z, b_inv[:, g, :].unsqueeze(2).to_broadcast([P, 4, N]), ALU.mult) \
                            .then_inc(S["b_norm"], 1)

                    def x1_less_1():
                        pool.wait_ge(S["bxn_ready"], at(gb, 2, 0))
                        nc.gpsimd.tensor_tensor(x1[:, :, :], x1[:, :, :], minus1[:, :].unsqueeze(1).to_broadcast([P, G, F]), ALU.add) \
                            .then_inc(S["x1_less_1"], 1)

                    def out_bias():
                        pool.wait_ge(S["bxn_ready"], at(gb, 2, 1))
                        nc.gpsimd.tensor_tensor(bx[:, :, :], bx[:, :, :], o_b[:, :].unsqueeze(1).to_broadcast([P, G, F]), ALU.add) \
                            .then_inc(S["bx_bias"], 1)

                    def rstd_c():
                        pool.wait_ge(S["c_var"], at(gc, 1, 0))
                        rstd(c_mv, c_ve, c_rs, (c_ve_link, gc, 1, 0)).then_inc(S["c_rstd"], 1)

                    def shift_c():
                        pool.wait_ge(S["c_z_max"], at(gc, 1, 0))
                        nc.gpsimd.tensor_tensor(four(cz), four(cz), c_max[:, :].unsqueeze(2).to_broadcast([P, 4, N]), ALU.subtract) \
                            .then_inc(S["c_shifted"], 1)

                    def norm_c():
                        pool.wait_ge(S["c_inv_ready"], at(gc, 1, 0))
                        nc.gpsimd.tensor_tensor(four(cz), four(cz), c_inv[:, :].unsqueeze(2).to_broadcast([P, 4, N]), ALU.mult) \
                            .then_inc(S["c_norm"], 1)

                    if with_b:
                        b_rstd(1)
                    if with_c:
                        rstd_c()
                    if with_b:
                        x1_less_1()
                    if with_n:
                        a_rstd()
                    if with_a:
                        shift(0)
                    if with_b:
                        b_shift(0); b_shift(1)
                    if with_a:
                        norm(0)
                    if with_b:
                        b_norm(1, 0); b_shift(2); b_norm(1, 1); b_shift(3); b_norm(1, 2); b_norm(1, 3)
                        b_rstd(2); out_bias()
                    if with_c:
                        shift_c(); norm_c()
                    if with_b:
                        b_norm(2, 0); b_norm(2, 1)
                    if with_a:
                        shift(1); norm(1)
                    if with_b:
                        b_norm(2, 2); b_norm(2, 3)
                steps(pool, body)


_OUT_SHAPE = (128, 128, 256)


def kernel(**inputs):
    import numpy as np
    import concourse.bacc as bacc
    from concourse.bass_utils import run_bass_kernel_spmd as run

    heads, feats, hd = inputs["L1_gnn_W"].shape
    a = np.asarray(inputs["L1_gnn_a"])
    a_blocks = np.zeros((heads, hd, heads, 2), a.dtype)
    for h in range(heads):
        a_blocks[h, :, h, 0] = a[h, :hd]
        a_blocks[h, :, h, 1] = a[h, hd:]

    def pair(v):
        v = np.asarray(v)
        return v.reshape(2, -1).T

    def t(name):
        return np.asarray(inputs[name]).T

    l1 = np.asarray(inputs["L1_gnn_W"])
    arrays = {
        "x": inputs["x"], "adj": inputs["adj"],
        "w_mlp1": inputs["L0_gnn_mlp1_w"], "b_mlp1": inputs["L0_gnn_mlp1_b"],
        "w_mlp2": inputs["L0_gnn_mlp2_w"], "b_mlp2": inputs["L0_gnn_mlp2_b"],
        "w_fc": inputs["L0_gnn_W_fc"], "w_fcT": t("L0_gnn_W_fc"), "a_fc": pair(inputs["L0_gnn_a_fc"]),
        "w_hand": inputs["L0_gnn_W_hand"], "w_handT": t("L0_gnn_W_hand"), "a_hand": pair(inputs["L0_gnn_a_hand"]),
        "w_l1": l1.transpose(1, 0, 2).reshape(feats, heads * hd), "w_l1T": l1.transpose(0, 2, 1).reshape(heads * hd, feats),
        "a_l1": a_blocks.reshape(heads * hd, 2 * heads),
        "w_q": t("L2_gnn_wq"), "b_q": inputs["L2_gnn_bq"], "w_k": t("L2_gnn_wk"), "b_k": inputs["L2_gnn_bk"],
        "w_v": t("L2_gnn_wv"), "b_v": inputs["L2_gnn_bv"], "w_o": t("L2_gnn_wo"), "b_o": inputs["L2_gnn_bo"],
        "w_1T": t("L3_gnn_W1"), "w_2T": t("L3_gnn_W2"), "w_h3": inputs["L3_gnn_W3"],
    }
    arrays = {k: np.ascontiguousarray(v) for k, v in arrays.items()}
    nc = bacc.Bacc("TRN2", target_bir_lowering=False, num_devices=1)
    ins = {k: nc.dram_tensor("in_" + k, v.shape, mybir.dt.from_np(v.dtype), kind="ExternalInput").ap() for k, v in arrays.items()}
    out = nc.dram_tensor("out_0", _OUT_SHAPE, mybir.dt.float32, kind="ExternalOutput").ap()
    gnn_stack_kernel(nc, ins, out)
    r = run(nc, [{"in_" + k: v for k, v in arrays.items()}], core_ids=[0])
    return r.results[0]["out_0"]
```
